# Optimizing a Trainium2 kernel written in Bass

```python
import numpy as np
import jax
import jax.numpy as jnp

def _softmax(x, axis=-1):
    return jax.nn.softmax(x, axis=axis)

def _gelu(x):
    return jax.nn.gelu(x, approximate=True)

def _silu(x):
    return jax.nn.silu(x)

def _sigmoid(x):
    return jax.nn.sigmoid(x)

def _layernorm(x, axis=-1, eps=1e-05):
    m = jnp.mean(x, axis=axis, keepdims=True)
    v = jnp.var(x, axis=axis, keepdims=True)
    return (x - m) / jnp.sqrt(v + eps)

def _scatter_add(tgt, idx, src, axis=0):
    return tgt.at[idx].add(src)

def _segment_sum(src, seg, n):
    return jax.ops.segment_sum(src, seg, n)
kernel_name = 'mk_flamingo_gated_d2_seqx_r4_5ebe53'

def setup_inputs(seed: int=0):
    np.random.seed(seed)
    _w = jnp.asarray

    def _rec_inputs():
        import jax
        import jax.numpy as jnp
        _rk = jax.random.key(seed)
        x = -0.000125 + 0.9999 * jax.random.normal(jax.random.fold_in(_rk, 1), (4, 512, 512), jnp.float32)
        _lenS = 512 - jax.random.randint(jax.random.fold_in(_rk, 7), (4,), 0, max(1, 512 // 4) + 1, jnp.int32)
        _lenS2 = 512 - jax.random.randint(jax.random.fold_in(_rk, 8), (4,), 0, max(1, 512 // 4) + 1, jnp.int32)
        itok_BxS_13_99985 = jax.random.randint(jax.random.fold_in(_rk, 11), (4, 512), 13, 99986, jnp.int32)
        _ctx_2048P = jax.random.normal(jax.random.fold_in(_rk, 12), (4, 16, 512), jnp.float32)
        _ctx_2048c = jax.random.dirichlet(jax.random.fold_in(_rk, 512), 0.3 * jnp.ones((16,), jnp.float32), (4, 512))
        _ctx_2048t = jnp.einsum('bsk,bkd->bsd', _ctx_2048c, _ctx_2048P)
        _ctx_2048t = _ctx_2048t * jax.lax.rsqrt(jnp.mean(jnp.square(_ctx_2048t)) + 1e-12) * 0.953939
        ctx_2048 = 6.82029e-06 + 0.0200006 * (_ctx_2048t + 0.3 * jax.random.normal(jax.random.fold_in(_rk, 612), (4, 512, 512), jnp.float32))
        _g = jax.random.normal(jax.random.fold_in(_rk, 9001), (2, 2), jnp.float32)
        _g = jnp.sign(_g) * jnp.maximum(jnp.abs(_g), 1.0) + (_g == 0) * 1.0
        g_xattn = _g[0]
        g_ffn = _g[1]
        return (x, itok_BxS_13_99985, ctx_2048, g_xattn, g_ffn)
    x, itok_BxS_13_99985, ctx_2048, g_xattn, g_ffn = _rec_inputs()

    def _L0_xattn_setup():
        import jax, jax.numpy as jnp
        import numpy as np
        B, S, D = (4, 1024, 512)
        E = 4
        F = 2048 // E
        VOCAB = 25000
        key = jax.random.key(seed)
        k1, k2, k3, k4, k5 = jax.random.split(key, 5)
        hidden_states = jax.random.normal(k1, (B, S, D), dtype=jnp.float32)
        token_ids = jax.random.randint(k2, (B, S), 0, VOCAB, dtype=jnp.int64)
        Wg = jax.random.normal(k3, (E, F, D), dtype=jnp.float32) * 0.02
        Wu = jax.random.normal(k4, (E, F, D), dtype=jnp.float32) * 0.02
        Wd = jax.random.normal(k5, (E, D, F), dtype=jnp.float32) * 0.02
        return {'hidden_states': hidden_states, 'token_ids': token_ids, 'Wg': Wg, 'Wu': Wu, 'Wd': Wd}
    _L0_xattn_all = _L0_xattn_setup()
    _L0_xattn_in = {k: v for k, v in _L0_xattn_all.items() if k in ()}
    del _L0_xattn_all

    def _L0_ffn_setup():
        import jax, jax.numpy as jnp
        import numpy as np
        HIDDEN = 512
        INTER = 2048
        SCALE = 64.0

        def fwht(x):
            orig_shape = x.shape
            n = orig_shape[-1]
            x = x.reshape(-1, n)
            h = 1
            while h < n:
                x = x.reshape(-1, n // (2 * h), 2, h)
                a, b = (x[:, :, 0, :], x[:, :, 1, :])
                x = jnp.stack([a + b, a - b], axis=2).reshape(-1, n)
                h *= 2
            return (x / jnp.sqrt(jnp.asarray(n, x.dtype))).reshape(orig_shape)
        key = jax.random.key(seed)
        ks = jax.random.split(key, 8)
        inp = jax.random.normal(ks[0], (4, 512, HIDDEN), dtype=jnp.float32)
        SU_ug = jnp.where(jax.random.bernoulli(ks[1], 0.5, (HIDDEN,)), 1.0, -1.0).astype(jnp.float32)
        SU_dp = jnp.where(jax.random.bernoulli(ks[2], 0.5, (INTER,)), 1.0, -1.0).astype(jnp.float32)
        Wscale_ug = jax.random.uniform(ks[3], (2 * INTER,), jnp.float32, 0.5, 1.5)
        Wscale_dp = jax.random.uniform(ks[4], (HIDDEN,), jnp.float32, 0.5, 1.5)
        W_up = jax.random.normal(ks[5], (INTER, HIDDEN), dtype=jnp.float32) * 0.02
        W_gate = jax.random.normal(ks[6], (INTER, HIDDEN), dtype=jnp.float32) * 0.02
        W_down = jax.random.normal(ks[7], (HIDDEN, INTER), dtype=jnp.float32) * 0.02
        return {'input': inp, 'SU_ug': SU_ug, 'SU_dp': SU_dp, 'Wscale_ug': Wscale_ug, 'Wscale_dp': Wscale_dp, 'W_up': W_up, 'W_gate': W_gate, 'W_down': W_down}
    _L0_ffn_all = _L0_ffn_setup()
    _L0_ffn_in = {k: v for k, v in _L0_ffn_all.items() if k in ('SU_ug', 'SU_dp', 'Wscale_ug', 'Wscale_dp', 'W_up', 'W_gate', 'W_down')}
    del _L0_ffn_all

    def _L1_xattn_setup():
        import jax, jax.numpy as jnp
        import numpy as np
        B_DIM, T_DIM, C_DIM = (16, 256, 512)

        def _wkv(w, u, k, v):
            Bn, Tn, Cn = k.shape
            NEG_INF = jnp.float32(-1e+38)

            def step(carry, kv_t):
                p, q, o = carry
                kt, vt = kv_t
                no = jnp.maximum(o, u + kt)
                A = jnp.exp(o - no)
                E = jnp.exp(u + kt - no)
                y = (A * p + E * vt) / (A * q + E)
                no2 = jnp.maximum(w + o, kt)
                A2 = jnp.exp(w + o - no2)
                E2 = jnp.exp(kt - no2)
                return ((A2 * p + E2 * vt, A2 * q + E2, no2), y)
            init = (jnp.zeros((Bn, Cn), k.dtype), jnp.zeros((Bn, Cn), k.dtype), jnp.full((Bn, Cn), NEG_INF, k.dtype))
            kT = jnp.moveaxis(k, 1, 0)
            vT = jnp.moveaxis(v, 1, 0)
            _, yT = jax.lax.scan(step, init, (kT, vT))
            return jnp.moveaxis(yT, 0, 1)
        key = jax.random.key(seed)
        k1, k2, k3, k4 = jax.random.split(key, 4)
        w = -jnp.exp(jax.random.normal(k1, (C_DIM,), jnp.float32))
        u = jax.random.normal(k2, (C_DIM,), jnp.float32)
        k = jax.random.normal(k3, (B_DIM, T_DIM, C_DIM), jnp.float32)
        v = jax.random.normal(k4, (B_DIM, T_DIM, C_DIM), jnp.float32)
        return {'B': B_DIM, 'T': T_DIM, 'C': C_DIM, 'w': w, 'u': u, 'k': k, 'v': v}
    _L1_xattn_all = _L1_xattn_setup()
    _L1_xattn_in = {k: v for k, v in _L1_xattn_all.items() if k in ('w', 'u')}
    del _L1_xattn_all

    def _L1_ffn_setup():
        import jax, jax.numpy as jnp
        import numpy as np
        BS, SLEN, DIM, HID, E, TOPK = (4, 512, 512, 448, 8, 2)
        key = jax.random.key(seed)
        ks = jax.random.split(key, 9)
        s = 0.02
        return {'x': jax.random.normal(ks[0], (BS, SLEN, DIM), jnp.float32), 'gate_w': jax.random.normal(ks[1], (DIM, E), jnp.float32) * s, 'w1': jax.random.normal(ks[2], (E, DIM, HID), jnp.float32) * s, 'w2': jax.random.normal(ks[3], (E, HID, DIM), jnp.float32) * s, 'w3': jax.random.normal(ks[4], (E, DIM, HID), jnp.float32) * s, 'sw1': jax.random.normal(ks[5], (DIM, HID), jnp.float32) * s, 'sw2': jax.random.normal(ks[6], (HID, DIM), jnp.float32) * s, 'sw3': jax.random.normal(ks[7], (DIM, HID), jnp.float32) * s, 'expert_bias': jnp.zeros((E,), jnp.float32)}
    _L1_ffn_all = _L1_ffn_setup()
    _L1_ffn_in = {k: v for k, v in _L1_ffn_all.items() if k in ('gate_w', 'w1', 'w2', 'w3', 'sw1', 'sw2', 'sw3', 'expert_bias')}
    del _L1_ffn_all
    return {'x': x, 'itok_BxS_13_99985': itok_BxS_13_99985, 'ctx_2048': ctx_2048, 'g_xattn': g_xattn, 'g_ffn': g_ffn, 'L0_ffn_SU_ug': _L0_ffn_in['SU_ug'], 'L0_ffn_SU_dp': _L0_ffn_in['SU_dp'], 'L0_ffn_Wscale_ug': _L0_ffn_in['Wscale_ug'], 'L0_ffn_Wscale_dp': _L0_ffn_in['Wscale_dp'], 'L0_ffn_W_up': _L0_ffn_in['W_up'], 'L0_ffn_W_gate': _L0_ffn_in['W_gate'], 'L0_ffn_W_down': _L0_ffn_in['W_down'], 'L1_xattn_w': _L1_xattn_in['w'], 'L1_xattn_u': _L1_xattn_in['u'], 'L1_ffn_gate_w': _L1_ffn_in['gate_w'], 'L1_ffn_w1': _L1_ffn_in['w1'], 'L1_ffn_w2': _L1_ffn_in['w2'], 'L1_ffn_w3': _L1_ffn_in['w3'], 'L1_ffn_sw1': _L1_ffn_in['sw1'], 'L1_ffn_sw2': _L1_ffn_in['sw2'], 'L1_ffn_sw3': _L1_ffn_in['sw3'], 'L1_ffn_expert_bias': _L1_ffn_in['expert_bias']}

def reference(x, itok_BxS_13_99985, ctx_2048, g_xattn, g_ffn, L0_ffn_SU_ug, L0_ffn_SU_dp, L0_ffn_Wscale_ug, L0_ffn_Wscale_dp, L0_ffn_W_up, L0_ffn_W_gate, L0_ffn_W_down, L1_xattn_w, L1_xattn_u, L1_ffn_gate_w, L1_ffn_w1, L1_ffn_w2, L1_ffn_w3, L1_ffn_sw1, L1_ffn_sw2, L1_ffn_sw3, L1_ffn_expert_bias):
    import jax
    import jax.numpy as jnp

    def _L0_xattn_ref(hidden_states, token_ids, Wg, Wu, Wd):
        import jax, jax.numpy as jnp
        import numpy as np
        B, S, D = (4, 1024, 512)
        E = 4
        F = 2048 // E
        VOCAB = 25000
        tokens_per_expert = VOCAB // E
        tid = jnp.clip(token_ids, 0, VOCAB - 1)
        expert_ids = jnp.minimum(tid // tokens_per_expert, E - 1)
        out = jnp.zeros_like(hidden_states)
        for e in range(E):
            g = jax.nn.silu(jnp.einsum('bsd,fd->bsf', hidden_states, Wg[e]))
            u = jnp.einsum('bsd,fd->bsf', hidden_states, Wu[e])
            y = jnp.einsum('bsf,df->bsd', g * u, Wd[e])
            out = jnp.where((expert_ids == e)[..., None], y, out)
        return out

    def _L0_ffn_ref(input, SU_ug, SU_dp, Wscale_ug, Wscale_dp, W_up, W_gate, W_down):
        import jax, jax.numpy as jnp
        import numpy as np
        HIDDEN = 512
        INTER = 2048
        SCALE = 64.0

        def fwht(x):
            orig_shape = x.shape
            n = orig_shape[-1]
            x = x.reshape(-1, n)
            h = 1
            while h < n:
                x = x.reshape(-1, n // (2 * h), 2, h)
                a, b = (x[:, :, 0, :], x[:, :, 1, :])
                x = jnp.stack([a + b, a - b], axis=2).reshape(-1, n)
                h *= 2
            return (x / jnp.sqrt(jnp.asarray(n, x.dtype))).reshape(orig_shape)
        n = SU_ug.shape[0]
        x = input.reshape(-1, n)
        x = fwht(x * SU_ug) / SCALE
        x_up = x @ W_up.T * (Wscale_ug[:INTER] * SCALE)
        x_gate = x @ W_gate.T * (Wscale_ug[INTER:] * SCALE)
        x = jax.nn.silu(x_gate) * x_up
        x = fwht(x * SU_dp) / SCALE
        x = x @ W_down.T * (Wscale_dp * SCALE)
        return x.reshape(input.shape)

    def _L1_xattn_ref(B, T, C, w, u, k, v):
        import jax, jax.numpy as jnp
        import numpy as np
        B_DIM, T_DIM, C_DIM = (16, 256, 512)

        def _wkv(w, u, k, v):
            Bn, Tn, Cn = k.shape
            NEG_INF = jnp.float32(-1e+38)

            def step(carry, kv_t):
                p, q, o = carry
                kt, vt = kv_t
                no = jnp.maximum(o, u + kt)
                A = jnp.exp(o - no)
                E = jnp.exp(u + kt - no)
                y = (A * p + E * vt) / (A * q + E)
                no2 = jnp.maximum(w + o, kt)
                A2 = jnp.exp(w + o - no2)
                E2 = jnp.exp(kt - no2)
                return ((A2 * p + E2 * vt, A2 * q + E2, no2), y)
            init = (jnp.zeros((Bn, Cn), k.dtype), jnp.zeros((Bn, Cn), k.dtype), jnp.full((Bn, Cn), NEG_INF, k.dtype))
            kT = jnp.moveaxis(k, 1, 0)
            vT = jnp.moveaxis(v, 1, 0)
            _, yT = jax.lax.scan(step, init, (kT, vT))
            return jnp.moveaxis(yT, 0, 1)
        return _wkv(w, u, k, v)

    def _L1_ffn_ref(x, gate_w, w1, w2, w3, sw1, sw2, sw3, expert_bias):
        import jax, jax.numpy as jnp
        import numpy as np
        BS, SLEN, DIM, HID, E, TOPK = (4, 512, 512, 448, 8, 2)
        bs, slen, dim = x.shape
        T = bs * slen
        xf = x.reshape(T, dim)
        scores = jax.nn.softmax((xf @ gate_w).astype(jnp.float32), axis=-1)
        _, sel = jax.lax.top_k(scores + expert_bias[None, :], TOPK)
        top_scores = jnp.take_along_axis(scores, sel, axis=1)
        flat_sel = sel.reshape(-1)
        counts = jnp.bincount(flat_sel, length=E).astype(jnp.int32)
        order = jnp.argsort(flat_sel, stable=True)
        top_scores_sorted = top_scores.reshape(-1)[order]
        token_idx = order // TOPK
        routed_in = xf[token_idx] * top_scores_sorted[:, None]
        h = jax.nn.silu(jax.lax.ragged_dot(routed_in, w1, counts)) * jax.lax.ragged_dot(routed_in, w3, counts)
        routed_out = jax.lax.ragged_dot(h, w2, counts)
        out = jax.nn.silu(xf @ sw1) * (xf @ sw3) @ sw2
        out = out.at[token_idx].add(routed_out)
        return out.reshape(bs, slen, dim)
    x = x + jnp.tanh(g_xattn[0]) * _L0_xattn_ref(_layernorm(x, axis=-1), itok_BxS_13_99985, ctx_2048, ctx_2048, ctx_2048)
    x = x + jnp.tanh(g_ffn[0]) * _L0_ffn_ref(_layernorm(x, axis=-1), L0_ffn_SU_ug, L0_ffn_SU_dp, L0_ffn_Wscale_ug, L0_ffn_Wscale_dp, L0_ffn_W_up, L0_ffn_W_gate, L0_ffn_W_down)
    x = x + jnp.tanh(g_xattn[1]) * _L1_xattn_ref(4, 512, 512, L1_xattn_w, L1_xattn_u, _layernorm(x, axis=-1), ctx_2048)
    x = x + jnp.tanh(g_ffn[1]) * _L1_ffn_ref(_layernorm(x, axis=-1), L1_ffn_gate_w, L1_ffn_w1, L1_ffn_w2, L1_ffn_w3, L1_ffn_sw1, L1_ffn_sw2, L1_ffn_sw3, L1_ffn_expert_bias)
    return x

_drawn_inputs = setup_inputs


def setup_inputs(seed=0):
    import zlib

    import numpy as np

    out = dict(_drawn_inputs(seed))
    spreads = {'g_ffn': (-1.0, 0.6), 'L1_ffn_expert_bias': (0.0, 0.8)}
    factors = {'L1_xattn_w': 8.0,
     'L1_xattn_u': 8.0,
     'L1_ffn_gate_w': 8.0,
     'L1_ffn_w1': 8.0,
     'L1_ffn_w2': 8.0,
     'L1_ffn_w3': 8.0,
     'L1_ffn_sw1': 8.0,
     'L1_ffn_sw2': 8.0,
     'L1_ffn_sw3': 8.0}
    for name, (base, spread) in spreads.items():
        noise = np.random.default_rng([zlib.crc32(name.encode()), seed]).standard_normal(out[name].shape)
        drawn = base * np.exp(spread * noise) if base else spread * noise
        out[name] = jnp.asarray(drawn.astype(out[name].dtype))
    for name, factor in factors.items():
        out[name] = (out[name] * factor).astype(out[name].dtype)
    return out
```

```python
import concourse.bass as bass
from concourse import mybir
from contextlib import ExitStack

ALU = mybir.AluOpType
ACT = mybir.ActivationFunctionType
AX = mybir.AxisListType
F32 = mybir.dt.float32
F32R = mybir.dt.float32r
I32 = mybir.dt.int32

P = 128
D = 512
DC = D // P
TOK = 2048
TT = TOK // P
EPS = 1e-5

E0 = 4
VOCAB = 25000
NT0 = TT + E0 - 1

F0 = 2048
FC = F0 // P
FB = 256
NJ = F0 // FB
NB = 4
T_SUG, T_SDP, T_WUP, T_WGT, T_DEC, T_BON, T_ROWS = 0, 4, 20, 36, 52, 56, 60

NU = NB * DC
BIG = 34.0
LOWEST = -1.0e38

E1 = 8
HID = 448
HC = 4
HP = HID // HC
NT1 = 2 * TT + E1 - 1
G_W = HID + E1
W_1, W_3, W_2, W_W = 0, HC * G_W, HC * (G_W + HID), HC * (G_W + HID + D)

C_ID, C_TRI, C_ONES, C_H, C_H4, C_H16, C_THR, C_IOTA = 0, 128, 256, 384, 512, 640, 768, 784
C_HALF = C_IOTA + 48
C_W = C_HALF + 4


def program(nc, x, tok, ctx, g_xattn, g_ffn, su_ug, su_dp, wscale_ug, wscale_dp, w_up, w_gate, w_down,
            wkv_w, wkv_u, gate_w, w1, w2, w3, sw1, sw2, sw3, expert_bias, consts, out):
    es = ExitStack()
    with es:
        def sb(name, shape, dt=F32, stack=es):
            return stack.enter_context(nc.sbuf_tensor(name, shape, dt))

        def sem(name):
            return es.enter_context(nc.semaphore(name))

        bank = [es.enter_context(nc.psum_tensor(f"bank{i}", [P, 512], F32)) for i in range(8)]
        xs_dram = nc.dram_tensor("xs_sorted", (NT0 * P, D), F32).ap()
        xs1_dram = nc.dram_tensor("xs1_sorted", (NT1 * P, D), F32).ap()
        y1_dram = nc.dram_tensor("y1_all", ((TT + NT1) * P, D), F32).ap()
        y_dram = nc.dram_tensor("y_sorted", (NT0 * P, D), F32).ap()

        cst = sb("cst", [P, C_W])
        gates = sb("gates", [P, 4])
        gates_raw = sb("gates_raw", [P, 4])
        tab_in = sb("tab_in", [T_ROWS, P])
        tab = sb("tab", [P, T_ROWS])
        wrow = sb("wrow", [P, D])
        stats = sb("stats", [P, TT, 6])
        mv = sb("mv", [P, TT, 2])
        vare = sb("vare", [P, TT])
        rstd = sb("rstd", [P, TT])
        xres = sb("xres", [P, TT, D])
        sd = ExitStack()
        xsd = [sb(f"xsd{i}", [P, D], F32, sd) for i in range(2)]
        dxh = [sb(f"dxh{i}", [P, DC, P], F32R, sd) for i in range(2)]
        dxl = [sb(f"dxl{i}", [P, DC, P], F32R, sd) for i in range(2)]
        dsg = sb("dsg", [P, HID], F32, sd)
        dmid = [sb(f"dmid{i}", [P, HID], F32, sd) for i in range(2)]
        dhh = [sb(f"dhh{i}", [HP, HC, P], F32R, sd) for i in range(2)]
        dhl = [sb(f"dhl{i}", [HP, HC, P], F32R, sd) for i in range(2)]
        dys = [sb(f"dys{i}", [P, D], F32, sd) for i in range(2)]
        wst = [sb(f"wst{i}", [P, 2048], F32, sd) for i in range(3)]
        row = sb("row", [P, 4, D], F32, sd)
        lg = sb("lg", [P, TT, E1], F32, sd)
        prob = sb("prob", [P, TT, E1], F32, sd)
        pb = sb("pb", [P, TT, E1], F32, sd)
        bias8 = sb("bias8", [P, E1], F32, sd)
        best = sb("best", [P, TT, 8], F32, sd)
        bix = sb("bix", [P, TT, 8], mybir.dt.uint32, sd)
        bixf = sb("bixf", [P, TT, 8], F32, sd)
        red = sb("red", [P, TT], F32, sd)
        sel = [sb(f"sel{i}", [P, TT, E1], F32, sd) for i in range(2)]
        tmp8 = sb("tmp8", [P, TT, E1], F32, sd)
        mask1 = sb("mask1", [P, TT + 1, E1], F32, sd)
        base1 = sb("base1", [P, TT + 1, E1], F32, sd)
        cmp1 = sb("cmp1", [P, E1, TT], F32, sd)
        nt1 = sb("nt1", [P, E1], F32, sd)
        tend1 = sb("tend1", [P, E1], F32, sd)
        tst1 = sb("tst1", [P, E1], F32, sd)
        tcmp1 = sb("tcmp1", [P, 48, E1 - 1], F32, sd)
        tex1 = sb("tex1", [P, 48], F32, sd)
        tex1_i = sb("tex1_i", [P, 48], I32, sd)
        tend1_i = sb("tend1_i", [P, E1], I32, sd)
        slf = sb("slf", [P, 2, TT], F32, sd)
        slw = sb("slw", [P, 2, TT], I32, sd)
        slr = sb("slr", [P, 2, TT], I32, sd)
        rsc = sb("rsc", [P, 2, TT], F32, sd)
        pace = sb("pace", [P, 32], F32, sd)
        wlim = sb("wlim", [P, DC], F32, sd)
        wub = sb("wub", [P, DC], F32, sd)
        s1 = ExitStack()
        sb("fill_h", [P, W_W], F32, s1)
        co = sb("co", [P, 513], F32, s1)
        cd = sb("cd", [P, 512], F32, s1)
        ce = [sb(f"ce{i}", [P, 3, 512], F32, s1) for i in range(2)]
        cev = sb("cev", [P, 512], F32, s1)
        cp = sb("cp", [P, 513], F32, s1)
        cq = sb("cq", [P, 513], F32, s1)
        s1.close()
        s1 = ExitStack()
        fin = sb("fin", [P, 12, D], F32, s1)
        s1.close()
        Wh = sb("Wh", [P, 2, W_W], F32R, sd)
        s1 = ExitStack()
        sb("fill_l", [P, W_W], F32, s1)
        vnat = sb("vnat", [P, 4, D], F32, s1)
        xnc = sb("xnc", [P, 4, D], F32, s1)
        cy = [sb(f"cy{i}", [P, 512], F32, s1) for i in range(2)]
        cnum = sb("cnum", [P, 512], F32, s1)
        s1.close()
        Wl = sb("Wl", [P, 2, W_W], F32R, sd)
        sd.close()

        wd16 = sb("wd16", [P, FC, D])

        sa = ExitStack()
        wh = sb("wh", [P, E0 * DC, D], F32R, sa)
        wl = sb("wl", [P, E0 * DC, D], F32R, sa)
        nat = sb("nat", [P, 2, DC, D], F32, sa)
        wdn = sb("wdn", [P, 2, 8, P], F32, sa)
        xn = sb("xn", [P, 4, D], F32, sa)
        tok_sb = sb("tok_sb", [P, TT], I32, sa)
        zero = sb("zero", [P, D], F32, sa)
        ge = sb("ge", [P, TT + 1, E0 + 1], F32, sa)
        mask = sb("mask", [P, TT + 1, E0], F32, sa)
        base = sb("base", [P, TT + 1, E0], F32, sa)
        cmp = sb("cmp", [P, E0, TT], F32, sa)
        ntile = sb("ntile", [P, E0], F32, sa)
        tend = sb("tend", [P, E0], F32, sa)
        tstart = sb("tstart", [P, E0], F32, sa)
        tcmp = sb("tcmp", [P, 48, E0 - 1], F32, sa)
        tex = sb("tex", [P, 48], F32, sa)
        tex_i = sb("tex_i", [P, 48], I32, sa)
        slot_f = sb("slot_f", [P, TT], F32, sa)
        slot = sb("slot", [P, TT], I32, sa)
        xs = [sb(f"xs{i}", [P, D], F32, sa) for i in range(2)]
        xh = [sb(f"xh{i}", [P, DC, P], F32R, sa) for i in range(2)]
        xl = [sb(f"xl{i}", [P, DC, P], F32R, sa) for i in range(2)]
        sg = [sb(f"sg{i}", [P, D], F32, sa) for i in range(2)]
        mid = [sb(f"mid{i}", [P, D], F32, sa) for i in range(2)]
        hh = [sb(f"hh{i}", [P, DC, P], F32R, sa) for i in range(2)]
        hl = [sb(f"hl{i}", [P, DC, P], F32R, sa) for i in range(2)]
        ysb = [sb(f"ysb{i}", [P, D], F32, sa) for i in range(2)]
        sa.close()

        sbk = ExitStack()
        xTh = sb("xTh", [P, NB, DC, 512], F32R, sbk)
        xTl = sb("xTl", [P, NB, DC, 512], F32R, sbk)
        sx = ExitStack()
        xnb = sb("xnb", [P, 4, D], F32, sx)
        sx.close()
        bhh = [sb(f"bhh{i}", [P, 2, 512], F32R, sbk) for i in range(2)]
        bhl = [sb(f"bhl{i}", [P, 2, 512], F32R, sbk) for i in range(2)]
        bs = sb("bs", [P, 2, 512], F32, sbk)
        wn = sb("wn", [P, 8, P], F32, sbk)
        wt1 = sb("wt1", [P, DC, FB], F32, sbk)
        gwh = [sb(f"gwh{i}", [P, 2, DC, FB], F32R, sbk) for i in range(2)]
        gwl = [sb(f"gwl{i}", [P, 2, DC, FB], F32R, sbk) for i in range(2)]
        gsc = [sb(f"gsc{i}", [P, 2], F32, sbk) for i in range(2)]
        wdt = sb("wdt", [P, 2, D], F32, sbk)
        wdh = sb("wdh", [P, 2, D], F32R, sbk)
        wdl = sb("wdl", [P, 2, D], F32R, sbk)
        sbk.close()

        ident = cst[:, C_ID:C_ID + P]
        tri = cst[:, C_TRI:C_TRI + P]
        ones = cst[:, C_ONES:C_ONES + P]

        s_cst = sem("s_cst")
        s_gl = sem("s_gl")
        s_x = [sem(f"s_xin{i}") for i in range(4)]
        s_ctx = [sem(f"s_ctx{i}") for i in range(E0)]
        s_zero = sem("s_zero")
        s_zeroed = sem("s_zeroed")
        s_gate = sem("s_gate")
        s_rt = sem("s_rt")
        s_rank = sem("s_rank")
        s_slot = sem("s_slot")
        s_var = sem("s_var")
        s_rstd = sem("s_rstd")
        s_xn = sem("s_xn")
        s_scat = [sem(f"s_scat{i}") for i in range(4)]
        s_wT = sem("s_wT")
        s_wh = sem("s_wh")
        s_wl = sem("s_wl")
        s_xs = [sem(f"s_xs{i}") for i in range(2)]
        s_xT = sem("s_xT")
        s_xh = sem("s_xh")
        s_xl = sem("s_xl")
        s_up = sem("s_up")
        s_sg = sem("s_sg")
        s_mid = sem("s_mid")
        s_mT = sem("s_mT")
        s_hh = sem("s_hh")
        s_hl = sem("s_hl")
        s_down = sem("s_down")
        s_y = sem("s_y")
        s_yst = [sem(f"s_yst{i}") for i in range(2)]
        s_yg = [sem(f"s_yg{i}") for i in range(4)]
        s_x1 = sem("s_x1")
        s_out = sem("s_out")
        s_tab = sem("s_tab")
        s_tabT = sem("s_tabT")
        s_tabc = sem("s_tabc")
        s_wrow = sem("s_wrow")
        s_wdn = [sem(f"s_wdn{i}") for i in range(2)]
        s_w16 = sem("s_w16")
        s_w16c = sem("s_w16c")
        s_xnb = sem("s_xnb")
        s_bT = sem("s_bT")
        s_bTh = sem("s_bTh")
        s_bTl = sem("s_bTl")
        s_wn = sem("s_wn")
        s_pa = sem("s_pa")
        s_pb = sem("s_pb")
        s_pw = sem("s_pw")
        s_t1 = sem("s_t1")
        s_gwh = sem("s_gwh")
        s_gwl = sem("s_gwl")
        s_gsc = sem("s_gsc")
        s_wdt = sem("s_wdt")
        s_wdh = sem("s_wdh")
        s_wdl = sem("s_wdl")
        s_gu = sem("s_gu")
        s_bs = sem("s_bs")
        s_bh = sem("s_bh")
        s_bhh = sem("s_bhh")
        s_bhl = sem("s_bhl")
        s_bd = sem("s_bd")
        s_acc = sem("s_acc")
        s_vn = sem("s_vn")
        s_cxn = sem("s_cxn")
        s_ck = sem("s_ck")
        s_cv = sem("s_cv")
        s_cf = sem("s_cf")
        s_cl = sem("s_cl")
        s_ce = sem("s_ce")
        s_cn = sem("s_cn")
        s_cna = sem("s_cna")
        s_cd = sem("s_cd")
        s_cy = sem("s_cy")
        s_co = sem("s_co")
        s_cr = sem("s_cr")
        s_wst = [sem(f"s_wst{i}") for i in range(3)]
        s_whi = [sem(f"s_whi{i}") for i in range(3)]
        s_w13 = sem("s_w13")
        s_w2 = sem("s_w2")
        s_dxn = sem("s_dxn")
        s_dxs = [sem(f"s_dxs{i}") for i in range(2)]
        s_dxT = sem("s_dxT")
        s_dxh = sem("s_dxh")
        s_dxl = sem("s_dxl")
        s_dup = sem("s_dup")
        s_dsg = sem("s_dsg")
        s_dmid = sem("s_dmid")
        s_dmT = sem("s_dmT")
        s_dhh = sem("s_dhh")
        s_dhl = sem("s_dhl")
        s_dd = sem("s_dd")
        s_dy = sem("s_dy")
        s_dst = [sem(f"s_dst{i}") for i in range(2)]
        s_b8 = sem("s_b8")
        s_lg = sem("s_lg")
        s_gw = sem("s_gw")
        s_gwlow = sem("s_gwlow")
        s_ex8 = sem("s_ex8")
        s_mask1 = sem("s_mask1")
        s_rank1 = sem("s_rank1")
        s_slot1 = sem("s_slot1")
        s_row = sem("s_row")
        s_rsc = [sem(f"s_rsc{i}") for i in range(4)]
        s_zero1 = sem("s_zero1")
        s_fin = [[sem(f"s_fin{i}_{k}") for k in range(3)] for i in range(4)]
        s_x4 = sem("s_x4")

        x_v = x.rearrange("b (i p) d -> p (b i) d", p=P)
        out_v = out.rearrange("b (i p) d -> p (b i) d", p=P)
        tok_v = tok.rearrange("b (i p) -> p (b i)", p=P)
        ctx_v = ctx.rearrange("e (f p) d -> p e f d", p=P)
        yg = [nat[:, 0, i, :] for i in range(4)]
        wd_v = w_down.rearrange("(h a) (c p) -> (a c) h p", a=8, p=P)
        wug_v = [w.rearrange("(h a) (c p) -> (a c) h p", a=32, p=P) for w in (w_gate, w_up)]

        def wait(eng, s, v):
            if not isinstance(v, int) or v > 0:
                eng.wait_ge(s, v)

        def f32(ap):
            return ap.bitcast(F32)

        def inside(t, lo, hi):
            return not isinstance(t, int) or lo <= t < hi

        block = es.enter_context(nc.Block())

        @block.sync
        def _(sp):
            sp.dma_start(cst[:, :], consts).then_inc(s_cst, 16)
            sp.dma_start(tok_sb[:, :], tok_v, allow_slow_non_contiguous=True).then_inc(s_cst, 16)
            sp.dma_start(tab_in[T_SUG:T_SDP, :], su_ug.rearrange("(c p) -> c p", p=P)).then_inc(s_tab, 16)
            sp.dma_start(tab_in[T_SDP:T_WUP, :], su_dp.rearrange("(c p) -> c p", p=P)).then_inc(s_tab, 16)
            sp.dma_start(tab_in[T_DEC:T_BON, :], wkv_w.rearrange("(c p) -> c p", p=P)).then_inc(s_tab, 16)
            sp.dma_start(tab_in[T_BON:T_ROWS, :], wkv_u.rearrange("(c p) -> c p", p=P)).then_inc(s_tab, 16)
            sp.dma_start(tab_in[T_WUP:T_DEC, :], wscale_ug.rearrange("(c p) -> c p", p=P)).then_inc(s_tab, 16)
            for e in range(2):
                sp.dma_start(nat[:, e, :, :], ctx_v[:, e, :, :]).then_inc(s_ctx[e], 16)
            for q in range(4):
                sp.dma_start(xres[:, 4 * q:4 * q + 4, :], x_v[:, 4 * q:4 * q + 4, :]).then_inc(s_x[q], 16)
            for n in range(2):
                sp.dma_start(wdn[:, n, :, :], wd_v[:, 8 * n:8 * n + 8, :]).then_inc(s_wdn[n], 16)
            for e in range(2, E0):
                sp.wait_ge(s_wT, (e - 1) * DC)
                sp.dma_start(nat[:, e % 2, :, :], ctx_v[:, e, :, :]).then_inc(s_ctx[e], 16)
            for n in range(2, 8):
                sp.wait_ge(s_w16, 2 * (n - 1))
                sp.dma_start(wdn[:, n % 2, :, :], wd_v[:, 8 * n:8 * n + 8, :]).then_inc(s_wdn[n % 2], 16)
            for q in range(4):
                sp.wait_ge(s_scat[q], 16 * TT // 4)

            def load(t, par):
                sp.dma_start(xs[par][:, :], xs_dram[bass.ds(t * P, P), :]).then_inc(s_xs[par], 16)

            load(0, 0)
            load(1, 1)

            def step(t, par):
                if inside(t + 2, 0, NT0):
                    sp.wait_ge(s_xT, t + 1)
                    load(t + 2, par)
                if inside(t - 2, 0, NT0):
                    sp.wait_ge(s_y, t - 1)
                    sp.dma_start(y_dram[bass.ds((t - 2) * P, P), :], ysb[par][:, :]).then_inc(s_yst[par], 16)

            step(0, 0)
            step(1, 1)
            with sp.Fori(2, 2 + 2 * ((NT0 - 4) // 2), 2) as t:
                step(t, 0)
                step(t + 1, 1)
            for t in range(2 + 2 * ((NT0 - 4) // 2), NT0 + 2):
                step(t, t % 2)

            sp.wait_ge(s_x1, TT)

            def load_wn(j, m):
                wait(sp, s_pa, 4 * j + 2 * m)
                sp.dma_start(wn[:, :, :], wug_v[m][:, bass.ds(j * 8, 8), :]).then_inc(s_wn, 16)

            load_wn(0, 0)
            load_wn(0, 1)
            load_wn(1, 0)
            load_wn(1, 1)
            with sp.Fori(2, NJ) as j:
                load_wn(j, 0)
                load_wn(j, 1)

            sp.wait_ge(s_acc, 16 * NJ)
            sp.dma_start(bias8[:, :], expert_bias.rearrange("(a n) -> a n", a=1).broadcast_to([P, E1])).then_inc(s_b8, 16)

            def load(t, par):
                sp.dma_start(xsd[par][:, :], xs1_dram[bass.ds((t - TT) * P, P), :]).then_inc(s_dxs[par], 16)

            def store(t, par):
                sp.wait_ge(s_dy, t + 1)
                sp.dma_start(y1_dram[bass.ds(t * P, P), :], dys[par][:, :]).then_inc(s_dst[par], 16)

            for n in range(TT + 7):
                if n % 4 == 0 and n < NU:
                    wait(sp, s_cv, n)
                    sp.dma_start(vnat[:, :, :], ctx_v[:, n // 4, :, :]).then_inc(s_vn, 16)
                if n >= 7:
                    store(n - 7, (n - 7) % 2)
            for i in range(4):
                sp.wait_ge(s_rsc[i], 16 * 2 * TT // 4)
            load(TT, 0)
            load(TT + 1, 1)
            for t in range(2):
                sp.wait_ge(s_dxT, TT + t + 1)
                load(TT + 2 + t, t)
            with sp.Fori(TT + 2, TT + NT1 - 4, 2) as t:
                for i in range(2):
                    sp.wait_ge(s_dxT, t + i + 1)
                    load(t + i + 2, i)
                    store(t + i - 2, i)
            sp.wait_ge(s_dxT, TT + NT1 - 2)
            load(TT + NT1 - 1, 0)
            for t in range(TT + NT1 - 5, TT + NT1):
                store(t, t % 2)

            for t in range(TT):
                if t >= 4:
                    sp.wait_ge(s_x4, t - 3)
                else:
                    for i in range(2):
                        sp.wait_ge(s_dst[i], 16 * ((TT + NT1 + 1 - i) // 2))
                sp.dma_start(fin[:, 3 * (t % 4), :], y1_dram[t * P:(t + 1) * P, :]).then_inc(s_fin[t % 4][0], 16)
                if t % 4 == 3 and t >= 7:
                    q = t // 4 - 1
                    sp.wait_ge(s_x4, 4 * q + 4)
                    sp.dma_start(out_v[:, 4 * q:4 * q + 4, :], xres[:, 4 * q:4 * q + 4, :]).then_inc(s_out, 16)
            sp.wait_ge(s_x4, TT)
            sp.dma_start(out_v[:, TT - 4:TT, :], xres[:, TT - 4:TT, :]).then_inc(s_out, 16)
            sp.wait_ge(s_out, 64)

        @block.gpsimd
        def _(pool):
            pool.wait_ge(s_cst, 32)
            pool.memset(zero[:, :], 0.0).then_inc(s_zero, 1)
            pool.wait_ge(s_zero, 1)
            for dram, rows, s in ((xs_dram, NT0, s_zeroed), (xs1_dram, NT1, s_zero1)):
                pool.dma_start(dram.rearrange("(p r) d -> p r d", p=P), zero[:, :].unsqueeze(1).broadcast_to([P, rows, D]))\
                    .then_inc(s, 16)

            def inv_std(n, q=None):
                q = n % 4 if q is None else q
                pool.wait_ge(s_var, n + 1)
                pool.tensor_tensor(rstd[:, 4 * q:4 * q + 4], vare[:, 4 * q:4 * q + 4],
                                   cst[:, C_HALF:C_HALF + 4], ALU.pow).then_inc(s_rstd, 1)

            for q in range(4):
                inv_std(q)
            pool.wait_ge(s_zeroed, 16)
            pool.wait_ge(s_slot, 1)
            for i in range(TT):
                pool.wait_ge(s_xn, i + 1)
                pool.indirect_dma_start(xs_dram, bass.IndirectOffsetOnAxis(ap=slot[:, i:i + 1], axis=0),
                                        xn[:, i % 4, :], None).then_inc(s_scat[i % 4], 16)
            pool.wait_ge(s_yst[0], 16 * ((NT0 + 1) // 2))
            pool.wait_ge(s_yst[1], 16 * (NT0 // 2))
            for q in range(NB):
                for i in range(4 * q, 4 * q + 4):
                    if i >= 4:
                        pool.wait_ge(s_x1, i - 3)
                    pool.indirect_dma_start(yg[i % 4], None, y_dram,
                                            bass.IndirectOffsetOnAxis(ap=slot[:, i:i + 1], axis=0))\
                        .then_inc(s_yg[i % 4], 16)
                if q >= 1:
                    inv_std(4 + q - 1)
            inv_std(4 + NB - 1)

            def w_part(idx, p):
                if isinstance(idx, int) and idx == 0:
                    return (sw1.rearrange("(k p) n -> p k n", p=P), sw3.rearrange("(k p) n -> p k n", p=P),
                            sw2.rearrange("(k p) n -> p k n", p=HP))[p]
                w, q = ((w1, P), (w3, P), (w2, HP))[p]
                return w[bass.ds(idx - 1, 1), :, :].rearrange("e (k p) n -> p (e k) n", p=q)

            places = [0]

            def alone(idx):
                if not isinstance(idx, int) or idx > 2:
                    n = places[0] = places[0] + 1
                    pool.tensor_tensor(pace[:, n:n + 1], pace[:, 0:1], pace[:, 0:1], ALU.add)

            def w_raw(idx, p):
                q, n = (P, HID) if p < 2 else (HP, D)
                rows = wst[p][0:q, 0:HC * (G_W if p == 0 else n)].rearrange("p (k n) -> p k n", k=HC)
                pool.dma_start(rows[:, :, 0:n], w_part(idx, p)).then_inc(s_wst[p], 16)

            def w_place(whole, slot, p, width):
                q, at, step = ((P, W_1, G_W), (P, W_3, HID), (HP, W_2, D))[p]
                return whole[0:q, slot, at:at + HC * step].rearrange("p (k n) -> p k n", k=HC)[:, :, 0:width]

            def w_high(idx, p, slot):
                pool.dma_start(w_place(Wh, slot, p, (HID, HID, D)[p]), w_part(idx, p)).then_inc(s_whi[p], 16)

            def w_low(idx, p, slot, first=False):
                width = (HID, HID, D)[p]
                q, step = ((P, G_W), (P, HID), (HP, D))[p]
                pool.wait_ge(s_wst[p], 16 * (idx + 1))
                pool.wait_ge(s_whi[p], 16 * (idx + 1))
                src = wst[p][0:q, 0:HC * step].rearrange("p (k n) -> p k n", k=HC)[:, :, 0:width]
                pool.tensor_tensor(w_place(Wl, slot, p, width), src, f32(w_place(Wh, slot, p, width)), ALU.subtract)\
                    .then_inc((s_w13, s_w13, s_w2)[p], 1)
                if p < 2:
                    pool.wait_ge(s_w13, 2 * idx + p + 1)
                else:
                    pool.wait_ge(s_w2, idx + 1)

            pool.wait_ge(s_acc, 16 * NJ)
            inv_std(8)
            pool.memset(pace[:, :], 0.0).then_inc(s_zero, 1)
            pool.wait_ge(s_zero, 2)

            def w_shared():
                rows = wst[0][:, 0:HC * G_W].rearrange("p (k n) -> p k n", k=HC)
                router = gate_w.rearrange("(k p) n -> p k n", p=P)
                pool.dma_start(rows[:, :, HID:G_W], router).then_inc(s_gw, 16)
                pool.dma_start(w_place(Wh, 0, 0, G_W)[:, :, HID:G_W], router).then_inc(s_gw, 16)
                for p in range(3):
                    w_raw(0, p)
                    w_high(0, p, 0)
                pool.wait_ge(s_gw, 32)
                pool.tensor_tensor(w_place(Wl, 0, 0, G_W)[:, :, HID:G_W], rows[:, :, HID:G_W],
                                   f32(w_place(Wh, 0, 0, G_W))[:, :, HID:G_W], ALU.subtract).then_inc(s_gwlow, 1)

            def w_all(idx, slot, ups=None, downs=None, more=True):
                if ups is not None:
                    pool.wait_ge(s_dup, ups)
                    alone(idx)
                for p in range(2):
                    w_high(idx, p, slot)
                for p in range(2):
                    w_low(idx, p, slot)
                    if more:
                        alone(idx)
                        w_raw(idx + 1, p)
                if downs is not None:
                    pool.wait_ge(s_dd, downs)
                    alone(idx)
                w_high(idx, 2, slot)
                w_low(idx, 2, slot)
                if more:
                    alone(idx)
                    w_raw(idx + 1, 2)

            def clamp(n):
                pool.wait_ge(s_cf, n + 1)
                wait(pool, s_ce, 3 * n)
                pool.tensor_scalar(row[:, 0, :], cd[:, :], 0.0, None, ALU.max).then_inc(s_cl, 1)
                pool.tensor_scalar(row[:, 1, :], cd[:, :], 0.0, None, ALU.min).then_inc(s_cl, 1)
                pool.tensor_scalar(row[:, 2, :], cd[:, :], wlim[:, n % DC:n % DC + 1], None, ALU.min).then_inc(s_cl, 1)

            def finish(n):
                pool.wait_ge(s_cn, n + 1)
                pool.tensor_tensor(cnum[:, :], cnum[:, :], cp[:, 0:512], ALU.add).then_inc(s_cna, 1)
                pool.wait_ge(s_cna, n + 1)
                pool.wait_ge(s_cd, n + 1)
                wait(pool, s_cr, n - 1)
                pool.tensor_tensor(cy[n % 2][:, :], cnum[:, :], ce[n % 2][:, 2, :], ALU.mult).then_inc(s_cy, 1)

            w_shared()
            clamp(0)
            power = 9
            for n in range(NU + 1):
                if n + 1 < NU:
                    clamp(n + 1)
                if n == 0:
                    for p in range(3):
                        w_low(0, p, 0)
                if n < NU:
                    finish(n)
                if n % 4 == 2 and n + 2 < NU:
                    inv_std(power, n // 4 + 1)
                    power += 1
                if n % 4 == 0 and n >= 4:
                    inv_std(power, n // 4 - 1)
                    power += 1
            pool.wait_ge(s_co, NU)
            for p in range(3):
                w_raw(1, p)
            w_all(1, 1)
            pool.wait_ge(s_zero1, 16)
            pool.wait_ge(s_slot1, 1)
            for t in range(TT):
                for k in range(2):
                    n = 2 * t + k
                    pool.wait_ge(s_row, n + 1)
                    pool.indirect_dma_start(xs1_dram, bass.IndirectOffsetOnAxis(ap=slw[:, k, t:t + 1], axis=0),
                                            row[:, n % 4, :], None).then_inc(s_rsc[n % 4], 16)
            w_all(2, 0, TT, TT)

            def w_next(idx, slot, more=True):
                last = pool.value_load(tend1_i[0:1, bass.ds(idx - 3, 1)], min_val=1, max_val=NT1)
                w_all(idx, slot, last + TT, last + TT, more)

            with pool.Fori(3, E1 - 2, 2) as idx:
                w_next(idx, 1)
                w_next(idx + 1, 0)
            w_next(E1 - 1, 1)
            w_next(E1, 0, False)
            for i in range(2):
                pool.wait_ge(s_dst[i], 16 * ((TT + NT1 + 1 - i) // 2))
            for t in range(TT):
                if t >= 4:
                    pool.wait_ge(s_x4, t - 3)
                for k in range(2):
                    pool.indirect_dma_start(fin[:, 3 * (t % 4) + 1 + k, :], None, y1_dram,
                                            bass.IndirectOffsetOnAxis(ap=slr[:, k, t:t + 1], axis=0))\
                        .then_inc(s_fin[t % 4][1 + k], 16)

        @block.scalar
        def _(act):
            act.dma_start(gates_raw[:, 0:2], g_xattn.rearrange("(a n) -> a n", a=1).broadcast_to([P, 2])).then_inc(s_gl, 16)
            act.dma_start(gates_raw[:, 2:4], g_ffn.rearrange("(a n) -> a n", a=1).broadcast_to([P, 2])).then_inc(s_gl, 16)
            act.dma_start(wrow[:, :], wscale_dp.rearrange("(a n) -> a n", a=1).broadcast_to([P, D])).then_inc(s_wrow, 16)
            act.wait_ge(s_gl, 32)
            act.activation(gates[:, :], gates_raw[:, :], ACT.Tanh).then_inc(s_gate, 1)
            act.wait_ge(s_tabT, 1)
            act.activation(tab[:, :], bank[4][:, 0:T_ROWS], ACT.Copy).then_inc(s_tabc, 1)
            act.wait_ge(s_tabc, 1)
            act.mul(tab[:, T_SUG:T_SDP], tab[:, T_SUG:T_SDP], float(D) ** -0.5).then_inc(s_tabc, 1)
            act.mul(tab[:, T_SDP:T_WUP], tab[:, T_SDP:T_WUP], float(F0) ** -0.5).then_inc(s_tabc, 1)
            act.wait_ge(s_wrow, 16)
            act.wait_ge(s_gate, 1)
            act.mul(wrow[:, :], wrow[:, :], gates[:, 2:3]).then_inc(s_tabc, 1)
            for j in range(E0 * DC):
                act.wait_ge(s_wT, j + 1)
                act.activation(wh[:, j, :], bank[6 + j % 2][:, :], ACT.Copy).then_inc(s_wh, 1)

            for n in range(16):
                act.wait_ge(s_w16, n + 1)
                act.activation(wd16[:, :, 32 * n:32 * n + 32],
                               bank[6 + n % 2][:, :].rearrange("p (n c) -> p c n", c=FC), ACT.Copy).then_inc(s_w16c, 1)

            def x_high(t, par):
                act.wait_ge(s_xT, t + 1)
                if inside(t - 2, 0, NT0):
                    act.wait_ge(s_up, t - 1)
                act.activation(xh[par][:, :, :].rearrange("p k n -> p (k n)"), bank[0][:, :], ACT.Copy).then_inc(s_xh, 1)

            def step(t, par):
                if inside(t + 1, 0, NT0):
                    x_high(t + 1, 1 - par)
                if inside(t, 0, NT0):
                    act.wait_ge(s_up, t + 1)
                    if inside(t - 2, 0, NT0):
                        act.wait_ge(s_mid, t - 1)
                    act.activation(sg[par][:, :], bank[2 + par][:, :], ACT.Silu).then_inc(s_sg, 1)
                if inside(t - 1, 0, NT0):
                    act.wait_ge(s_mT, t)
                    if inside(t - 3, 0, NT0):
                        act.wait_ge(s_down, t - 2)
                    act.activation(hh[1 - par][:, :, :].rearrange("p k n -> p (k n)"), bank[1][:, :], ACT.Copy).then_inc(s_hh, 1)
                if inside(t - 2, 0, NT0):
                    act.wait_ge(s_down, t - 1)
                    if inside(t - 4, 0, NT0):
                        act.wait_ge(s_yst[par], 16 * (t // 2 - 1) if isinstance(t, int) else ((t - par) * 8 - 16))
                    act.activation(ysb[par][:, :], bank[4 + par][:, :], ACT.Copy).then_inc(s_y, 1)

            x_high(0, 0)
            for t in range(0, 4):
                step(t, t % 2)
            with act.Fori(4, 4 + 2 * ((NT0 - 1 - 4) // 2), 2) as t:
                step(t, 0)
                step(t + 1, 1)
            for t in range(4 + 2 * ((NT0 - 1 - 4) // 2), NT0 + 2):
                step(t, t % 2)

            for n in range(NB * DC):
                act.wait_ge(s_bT, n + 1)
                b, c = divmod(n, DC)
                act.mul(xTh[:, b, c, :], bank[n % 4][:, :], tab[:, T_SUG + c:T_SUG + c + 1]).then_inc(s_bTh, 1)

            def prep_gu(j, m, slot):
                for i in range(2):
                    act.wait_ge(s_pb, 4 * j + 2 * m + i + 1)
                    wait(act, s_gu, 8 * (j - 1))
                    act.activation(gwh[slot][:, m, 2 * i:2 * i + 2, :].rearrange("p c f -> p (c f)"),
                                   bank[6 + i][:, :], ACT.Copy).then_inc(s_gwh, 1)

            def chunk(j, slot, more):
                for b in range(NB):
                    for f in range(2):
                        k = 8 * j + 2 * b + f
                        act.wait_ge(s_gu, k + 1)
                        wait(act, s_bhl, k - 1)
                        if b == 0 and f == 0:
                            act.wait_ge(s_gsc, j + 1)
                        act.activation(bs[:, f, :], bank[2 * f][:, :], ACT.Silu,
                                       scale=gsc[slot][:, f:f + 1]).then_inc(s_bs, 1)
                        act.wait_ge(s_bh, k + 1)
                        wait(act, s_bd, 4 * (4 * j + b - 1))
                        act.activation(bhh[b % 2][:, f, :], bs[:, f, :], ACT.Copy).then_inc(s_bhh, 1)
                    if b == 0:
                        wait(act, s_bd, 16 * j)
                        for f in range(2):
                            act.wait_ge(s_wdt, 2 * j + f + 1)
                            act.activation(wdh[:, f, :], wdt[:, f, :], ACT.Copy).then_inc(s_wdh, 1)
                    if more and b in (1, 2):
                        prep_gu(j + 1, b - 1, 1 - slot)

            prep_gu(0, 0, 0)
            prep_gu(0, 1, 0)
            chunk(0, 0, True)
            with act.Fori(1, NJ - 2, 2) as j:
                chunk(j, 1, True)
                chunk(j + 1, 0, True)
            chunk(NJ - 1, 1, False)

            def exps(n):
                act.wait_ge(s_cl, 3 * n + 3)
                wait(act, s_cy, n - 1)
                e = ce[n % 2]
                act.activation(e[:, 0, :], row[:, 0, :], ACT.Exp, scale=-1.0).then_inc(s_ce, 1)
                act.activation(e[:, 1, :], row[:, 1, :], ACT.Exp).then_inc(s_ce, 1)
                act.activation(e[:, 2, :], row[:, 2, :], ACT.Exp, bias=wub[:, n % DC:n % DC + 1]).then_inc(s_ce, 1)

            def d_x(t, par):
                act.wait_ge(s_dxT, t + 1)
                wait(act, s_dup, t - 1)
                act.activation(dxh[par][:, :, :].rearrange("p k n -> p (k n)"), bank[0][:, :], ACT.Copy).then_inc(s_dxh, 1)

            def d_gate(t, par):
                act.wait_ge(s_dup, t + 1)
                wait(act, s_dmid, t)
                act.activation(dsg[:, :], bank[2][:, 0:HID], ACT.Silu).then_inc(s_dsg, 1)

            def d_hid(t, par):
                act.wait_ge(s_dmT, t + 1)
                wait(act, s_dd, t - 1)
                act.activation(dhh[par][:, :, :].rearrange("p k n -> p (k n)"), bank[1][0:HP, :], ACT.Copy).then_inc(s_dhh, 1)

            def d_y(t, par):
                act.wait_ge(s_dd, t + 1)
                if not isinstance(t, int) or t >= 2:
                    act.wait_ge(s_dst[par], 16 * (t // 2) if isinstance(t, int) else (t - par) * 8)
                act.activation(dys[par][:, :], bank[4][:, :], ACT.Copy).then_inc(s_dy, 1)

            act.wait_ge(s_acc, 16 * NJ)
            exps(0)
            for n in range(NU + 5):
                t = n - 5
                if t >= 0 and t % 4 != 3:
                    d_x(t + 1, (t + 1) % 2)
                if t >= 1:
                    d_hid(t - 1, (t - 1) % 2)
                if n + 1 < NU:
                    exps(n + 1)
                if t >= 0:
                    d_gate(t, t % 2)
                if t >= 2:
                    d_y(t - 2, t % 2)
                if t >= -1 and t % 4 == 3 and t + 1 < TT:
                    d_x(t + 1, (t + 1) % 2)
            d_hid(TT - 1, 1)
            d_y(TT - 2, 0)
            d_y(TT - 1, 1)
            act.wait_ge(s_lg, TT + 1)
            act.activation(prob[:, :, :], lg[:, :, :], ACT.Exp).then_inc(s_ex8, 1)
            d_x(TT, 0)
            d_x(TT + 1, 1)
            d_gate(TT, 0)
            d_x(TT + 2, 0)
            d_gate(TT + 1, 1)
            d_hid(TT, 0)
            with act.Fori(TT + 2, TT + NT1 - 2, 2) as t:
                for i in range(2):
                    d_x(t + i + 1, 1 - i)
                    d_gate(t + i, i)
                    d_hid(t + i - 1, 1 - i)
                    d_y(t + i - 2, i)
            T = TT + NT1 - 1
            d_gate(T, T % 2)
            d_hid(T - 1, (T - 1) % 2)
            d_y(T - 2, T % 2)
            d_hid(T, T % 2)
            d_y(T - 1, (T - 1) % 2)
            d_y(T, T % 2)

        @block.tensor
        def _(pe):
            pe.wait_ge(s_cst, 32)

            def weights(e):
                pe.wait_ge(s_ctx[e], 16)
                for k in range(DC):
                    j = e * DC + k
                    if j >= 2:
                        pe.wait_ge(s_wl, j - 1)
                    for f in range(DC):
                        mm = pe.transpose(bank[6 + j % 2][:, f * P:(f + 1) * P], nat[:, e % 2, f, k * P:(k + 1) * P], ident)
                    mm.then_inc(s_wT, 1)

            pe.wait_ge(s_tab, 80)
            pe.transpose(bank[4][:, 0:T_ROWS], tab_in[:, :], ident[0:T_ROWS, 0:T_ROWS]).then_inc(s_tabT, 1)
            pe.wait_ge(s_rt, 1)
            n = (TT + 1) * E0
            pe.matmul(bank[5][:, 0:n], tri, mask[:, :, :].rearrange("p i e -> p (i e)"), start=True, stop=False)
            for j in range(TT):
                pe.matmul(bank[5][:, (j + 1) * E0:n].rearrange("p (i e) -> p i e", e=E0), ones,
                               mask[:, j:j + 1, :].broadcast_to([P, TT - j, E0]), start=False, stop=False,
                               skip_group_check=True)
            pe.matmul(bank[5][:, 0:n].rearrange("p (i e) -> p i e", e=E0), ones,
                      mask[:, TT:TT + 1, :].broadcast_to([P, TT + 1, E0]), start=False, stop=True).then_inc(s_rank, 1)
            for e in range(E0):
                weights(e)
            for n in range(16):
                if n % 2 == 0:
                    pe.wait_ge(s_wdn[n // 2 % 2], 16 * (n // 4 + 1))
                wait(pe, s_wl, E0 * DC - 1 + n if n < 2 else 0)
                wait(pe, s_w16c, n - 1)
                for i in range(4):
                    mm = pe.matmul(bank[6 + n % 2][:, i * P:(i + 1) * P], wdn[:, n // 2 % 2, 4 * (n % 2) + i, :],
                                   cst[:, C_H16:C_H16 + P], start=True, stop=True)
                mm.then_inc(s_w16, 1)
            pe.wait_ge(s_wl, E0 * DC)
            pe.wait_ge(s_slot, 1)

            def x_turn(t, par):
                pe.wait_ge(s_xs[par], (t // 2 + 1) * 16 if isinstance(t, int) else (t - par) * 8 + 16)
                if inside(t - 1, 0, NT0):
                    pe.wait_ge(s_xl, t)
                for k in range(DC):
                    mm = pe.transpose(bank[0][:, k * P:(k + 1) * P], xs[par][:, k * P:(k + 1) * P], ident)
                mm.then_inc(s_xT, 1)

            def step(t, par, ex=[None, None]):
                if inside(t + 1, 0, NT0):
                    x_turn(t + 1, 1 - par)
                if inside(t, 0, NT0):
                    ex[par] = pe.value_load(tex_i[0:1, bass.ds(t, 1)], min_val=0, max_val=E0 - 1)
                    pe.wait_ge(s_xl, t + 1)
                    if inside(t - 2, 0, NT0):
                        pe.wait_ge(s_mid, t - 1)
                    n = 0
                    for a, w in ((xl, wh), (xh, wl), (xh, wh)):
                        for k in range(DC):
                            mm = pe.matmul(bank[2 + par][:, :], a[par][:, k, :], w[:, bass.ds(ex[par] * DC + k, 1), :],
                                           start=(n == 0), stop=(n == 3 * DC - 1))
                            n += 1
                    mm.then_inc(s_up, 1)
                if inside(t - 1, 0, NT0):
                    pe.wait_ge(s_mid, t)
                    if inside(t - 2, 0, NT0):
                        pe.wait_ge(s_hl, t - 1)
                    for k in range(DC):
                        mm = pe.transpose(bank[1][:, k * P:(k + 1) * P], mid[1 - par][:, k * P:(k + 1) * P], ident)
                    mm.then_inc(s_mT, 1)
                if inside(t - 2, 0, NT0):
                    ey = pe.value_load(tex_i[0:1, bass.ds(t - 2, 1)], min_val=0, max_val=E0 - 1)
                    pe.wait_ge(s_hl, t - 1)
                    if inside(t - 4, 0, NT0):
                        pe.wait_ge(s_y, t - 3)
                    n = 0
                    for a, w in ((hl, wh), (hh, wl), (hh, wh)):
                        for k in range(DC):
                            mm = pe.matmul(bank[4 + par][:, :], a[par][:, k, :], w[:, bass.ds(ey * DC + k, 1), :],
                                           start=(n == 0), stop=(n == 3 * DC - 1))
                            n += 1
                    mm.then_inc(s_down, 1)

            x_turn(0, 0)
            for t in range(0, 4):
                step(t, t % 2)
            with pe.Fori(4, 4 + 2 * ((NT0 - 1 - 4) // 2), 2) as t:
                step(t, 0)
                step(t + 1, 1)
            for t in range(4 + 2 * ((NT0 - 1 - 4) // 2), NT0 + 2):
                step(t, t % 2)

            for b in range(NB):
                pe.wait_ge(s_xnb, 4 * b + 4)
                for c in range(DC):
                    n = b * DC + c
                    wait(pe, s_bTl, n - 3)
                    for i in range(4):
                        mm = pe.transpose(bank[n % 4][:, i * P:(i + 1) * P], xnb[:, i, c * P:(c + 1) * P], ident)
                    mm.then_inc(s_bT, 1)

            def prep_a(j, m):
                pe.wait_ge(s_wn, 16 * (2 * j + m + 1))
                for i in range(2):
                    if m == 0:
                        wait(pe, s_wdt, 2 * j - 1 + i)
                    else:
                        pe.wait_ge(s_gwl, 4 * j + 1 + i)
                    for h in range(4):
                        mm = pe.matmul(bank[6 + i][:, h * P:(h + 1) * P], wn[:, 4 * i + h, :], cst[:, C_H4:C_H4 + P],
                                       start=True, stop=True)
                    mm.then_inc(s_pa, 1)

            def prep_b(j, m):
                pe.wait_ge(s_t1, 4 * j + 2 * m + 2)
                for i in range(2):
                    pe.matmul(bank[6 + i][:, :], cst[:, C_H:C_H + P],
                              wt1[:, 2 * i:2 * i + 2, :].rearrange("p c f -> p (c f)"), start=True, stop=True)\
                        .then_inc(s_pb, 1)

            def prep_w(j):
                for f in range(2):
                    pe.wait_ge(s_gwl, 4 * j + 3 + f)
                    pe.matmul(bank[6 + f][:, :], cst[:, C_H:C_H + P],
                              wd16[:, bass.ds(2 * j + f, 1), :].rearrange("p a d -> p (a d)"), start=True, stop=True)\
                        .then_inc(s_pw, 1)

            def gate_up(j, b, slot):
                pe.wait_ge(s_gwl, 4 * j + 4)
                for f in range(2):
                    wait(pe, s_bh, 8 * j + 2 * b + f - 1)
                    for m in range(2):
                        n = 0
                        for w, a in ((gwl, xTh), (gwh, xTl), (gwh, xTh)):
                            for c in range(DC):
                                mm = pe.matmul(bank[2 * f + m][:, :], w[slot][:, m, c, f * P:(f + 1) * P], a[:, b, c, :],
                                               start=(n == 0), stop=(n == 3 * DC - 1))
                                n += 1
                    mm.then_inc(s_gu, 1)

            def down(j, b):
                pe.wait_ge(s_bhl, 8 * j + 2 * b + 2)
                pe.wait_ge(s_wdl, 2 * j + 2)
                for i in range(4):
                    wait(pe, s_acc, 16 * j + 4 * b + i - 1)
                    n = 0
                    for a, w in ((bhl, wdh), (bhh, wdl), (bhh, wdh)):
                        for f in range(2):
                            mm = pe.matmul(bank[4 + i % 2][:, :], a[b % 2][:, f, i * P:(i + 1) * P], w[:, f, :],
                                           start=(n == 0), stop=(n == 5))
                            n += 1
                    mm.then_inc(s_bd, 1)

            def chunk(j, slot, first, more):
                gate_up(j, 0, slot)
                if not first:
                    down(j - 1, 3)
                if more:
                    prep_a(j + 1, 0)
                gate_up(j, 1, slot)
                down(j, 0)
                if more:
                    prep_b(j + 1, 0)
                    prep_a(j + 1, 1)
                gate_up(j, 2, slot)
                down(j, 1)
                if more:
                    prep_b(j + 1, 1)
                gate_up(j, 3, slot)
                down(j, 2)
                if more:
                    prep_w(j + 1)

            prep_a(0, 0)
            prep_b(0, 0)
            prep_a(0, 1)
            prep_b(0, 1)
            prep_w(0)
            chunk(0, 0, True, True)
            with pe.Fori(1, NJ - 2, 2) as j:
                chunk(j, 1, False, True)
                chunk(j + 1, 0, False, True)
            chunk(NJ - 1, 1, False, False)
            down(NJ - 1, 3)

            def c_keys(n):
                pe.wait_ge(s_cxn, n // DC * 4 + 4)
                wait(pe, s_cf, n)
                for i in range(4):
                    mm = pe.transpose(bank[5][:, i * P:(i + 1) * P], xnc[:, i, n % DC * P:(n % DC + 1) * P], ident)
                mm.then_inc(s_ck, 1)

            def c_values(n):
                pe.wait_ge(s_vn, 16 * (n // DC + 1))
                wait(pe, s_cn, n)
                for i in range(4):
                    mm = pe.transpose(bank[6][:, i * P:(i + 1) * P], vnat[:, i, n % DC * P:(n % DC + 1) * P], ident)
                mm.then_inc(s_cv, 1)

            def c_back(n):
                pe.wait_ge(s_cy, n + 1)
                wait(pe, s_co, n)
                for i in range(4):
                    mm = pe.transpose(bank[7][:, i * P:(i + 1) * P], cy[n % 2][:, i * P:(i + 1) * P], ident)
                mm.then_inc(s_cr, 1)

            def d_x(t, par, shared):
                if shared:
                    pe.wait_ge(s_dxn, t + 1)
                else:
                    pe.wait_ge(s_dxs[par], ((t - TT) // 2 + 1) * 16 if isinstance(t, int) else (t - TT - par) * 8 + 16)
                wait(pe, s_dxl, t)
                for k in range(DC):
                    mm = pe.transpose(bank[0][:, k * P:(k + 1) * P], xsd[par][:, k * P:(k + 1) * P], ident)
                mm.then_inc(s_dxT, 1)

            def d_up(t, par, shared):
                slot = 0
                if not shared:
                    e = pe.value_load(tex1_i[0:1, bass.ds(t - TT, 1)], min_val=0, max_val=E1 - 1)
                    pe.wait_ge(s_w13, e * 2 + 4)
                    slot = (e + 1) % 2
                else:
                    pe.wait_ge(s_w13, 2)
                    pe.wait_ge(s_gwlow, 1)
                pe.wait_ge(s_dxl, t + 1)
                wait(pe, s_dmid, t)
                for o, at, step, width in ((2, W_1, G_W, G_W if shared else HID), (3, W_3, HID, HID)):
                    n = 0
                    for a, w in ((dxl, Wh), (dxh, Wl), (dxh, Wh)):
                        for k in range(DC):
                            mm = pe.matmul(bank[o][:, 0:width], a[par][:, k, :],
                                           w[:, bass.ds(slot, 1), at + k * step:at + k * step + width].rearrange("p a n -> p (a n)"),
                                           start=(n == 0), stop=(n == 3 * DC - 1))
                            n += 1
                mm.then_inc(s_dup, 1)

            def d_mid(t, par):
                pe.wait_ge(s_dmid, t + 1)
                wait(pe, s_dhl, t)
                for k in range(HC):
                    mm = pe.transpose(bank[1][0:HP, k * P:(k + 1) * P], dmid[par][:, k * HP:(k + 1) * HP], ident)
                mm.then_inc(s_dmT, 1)

            def d_down(t, par, shared):
                slot = 0
                if not shared:
                    e = pe.value_load(tex1_i[0:1, bass.ds(t - TT, 1)], min_val=0, max_val=E1 - 1)
                    pe.wait_ge(s_w2, e + 2)
                    slot = (e + 1) % 2
                else:
                    pe.wait_ge(s_w2, 1)
                pe.wait_ge(s_dhl, t + 1)
                wait(pe, s_dy, t)
                n = 0
                for a, w in ((dhl, Wh), (dhh, Wl), (dhh, Wh)):
                    for k in range(HC):
                        mm = pe.matmul(bank[4][:, :], a[par][:, k, :],
                                       w[0:HP, bass.ds(slot, 1), W_2 + k * D:W_2 + (k + 1) * D].rearrange("p a n -> p (a n)"),
                                       start=(n == 0), stop=(n == 3 * HC - 1))
                        n += 1
                mm.then_inc(s_dd, 1)

            pe.wait_ge(s_acc, 16 * NJ)
            c_keys(0)
            for n in range(NU + 5):
                if n + 1 < NU:
                    c_keys(n + 1)
                t = n - 5
                if t >= 0 and t % 4 != 3:
                    d_x(t + 1, (t + 1) % 2, True)
                if 1 <= n <= NU:
                    c_back(n - 1)
                if n < NU:
                    c_values(n)
                if t >= 0:
                    if t >= 1:
                        d_mid(t - 1, (t - 1) % 2)
                    d_up(t, t % 2, True)
                    if t >= 2:
                        d_down(t - 2, t % 2, True)
                if t >= -1 and t % 4 == 3 and t + 1 < TT:
                    d_x(t + 1, (t + 1) % 2, True)
            d_mid(TT - 1, 1)
            d_down(TT - 2, 0, True)
            d_down(TT - 1, 1, True)
            pe.wait_ge(s_mask1, 1)
            w = (TT + 1) * E1
            pe.matmul(bank[5][:, 0:w], tri, mask1[:, :, :].rearrange("p i e -> p (i e)"), start=True, stop=False)
            for j in range(TT):
                pe.matmul(bank[5][:, (j + 1) * E1:w].rearrange("p (i e) -> p i e", e=E1), ones,
                          mask1[:, j:j + 1, :].broadcast_to([P, TT - j, E1]), start=False, stop=False, skip_group_check=True)
            pe.matmul(bank[5][:, 0:w].rearrange("p (i e) -> p i e", e=E1), ones,
                      mask1[:, TT:TT + 1, :].broadcast_to([P, TT + 1, E1]), start=False, stop=True).then_inc(s_rank1, 1)
            pe.wait_ge(s_slot1, 1)
            d_x(TT, 0, False)
            d_x(TT + 1, 1, False)
            d_up(TT, 0, False)
            d_x(TT + 2, 0, False)
            d_up(TT + 1, 1, False)
            d_mid(TT, 0)
            with pe.Fori(TT + 2, TT + NT1 - 2, 2) as t:
                for i in range(2):
                    d_x(t + i + 1, 1 - i, False)
                    d_up(t + i, i, False)
                    d_mid(t + i - 1, 1 - i)
                    d_down(t + i - 2, i, False)
            T = TT + NT1 - 1
            d_up(T, T % 2, False)
            d_mid(T - 1, (T - 1) % 2)
            d_down(T - 2, T % 2, False)
            d_mid(T, T % 2)
            d_down(T - 1, (T - 1) % 2, False)
            d_down(T, T % 2, False)

        @block.vector
        def _(dve):
            rt = [0]

            def chain(ins):
                rt[0] += 1
                ins.then_inc(s_rt, 1)
                dve.wait_ge(s_rt, rt[0])

            dve.memset(mask[:, :, :], 0.0)
            dve.wait_ge(s_cst, 32)
            for e in range(E0 + 1):
                last = dve.tensor_scalar(ge[:, 0:TT, e], tok_sb[:, :], float(e * (VOCAB // E0)) if 0 < e < E0 else (-3.0e9 if e == 0 else 3.0e9),
                                         None, ALU.is_ge)
            last.then_inc(s_gate, 1)
            dve.wait_ge(s_gate, 2)
            chain(dve.tensor_tensor(mask[:, 0:TT, :], ge[:, 0:TT, 0:E0], ge[:, 0:TT, 1:E0 + 1], ALU.subtract))
            for q in range(4):
                dve.wait_ge(s_x[q], 16)
                for i in range(4 * q, 4 * q + 4):
                    last = dve.bn_stats(stats[:, i, :], xres[:, i, :])
                chain(last)
                for i in range(4 * q, 4 * q + 4):
                    last = dve.bn_aggr(mv[:, i, :], stats[:, i, :])
                chain(last)
                dve.tensor_scalar(vare[:, 4 * q:4 * q + 4], mv[:, 4 * q:4 * q + 4, 1], EPS, None, ALU.add).then_inc(s_var, 1)
            dve.wait_ge(s_rank, 1)
            chain(dve.tensor_copy(base[:, :, :].rearrange("p i e -> p (i e)"), bank[5][:, 0:(TT + 1) * E0]))
            chain(dve.tensor_tensor(cmp[:, :, :], base[:, TT, :].unsqueeze(2).broadcast_to([P, E0, TT]),
                                    cst[:, C_THR:C_THR + TT].unsqueeze(1).broadcast_to([P, E0, TT]), ALU.is_gt))
            chain(dve.tensor_reduce(ntile[:, :], cmp[:, :, :], AX.X, ALU.add))
            chain(dve.tensor_tensor_scan(tend[:, :], ones[:, 0:E0], ntile[:, :], 0.0, ALU.mult, ALU.add))
            chain(dve.tensor_tensor(tstart[:, :], tend[:, :], ntile[:, :], ALU.subtract))
            chain(dve.tensor_scalar(tstart[:, :], tstart[:, :], float(P), None, ALU.mult))
            chain(dve.tensor_tensor(base[:, 0:TT, :], base[:, 0:TT, :], tstart[:, :].unsqueeze(1).broadcast_to([P, TT, E0]), ALU.add))
            chain(dve.tensor_tensor(base[:, 0:TT, :], base[:, 0:TT, :], mask[:, 0:TT, :], ALU.mult))
            chain(dve.tensor_reduce(slot_f[:, :], base[:, 0:TT, :], AX.X, ALU.add))
            chain(dve.tensor_copy(slot[:, :], slot_f[:, :]))
            chain(dve.tensor_tensor(tcmp[:, :, :], cst[:, C_IOTA:C_IOTA + 48].unsqueeze(2).broadcast_to([P, 48, E0 - 1]),
                                    tend[:, 0:E0 - 1].unsqueeze(1).broadcast_to([P, 48, E0 - 1]), ALU.is_ge))
            chain(dve.tensor_reduce(tex[:, :], tcmp[:, :, :], AX.X, ALU.add))
            dve.tensor_copy(tex_i[:, :], tex[:, :]).then_inc(s_slot, 1)
            for i in range(TT):
                if i % 4 == 0:
                    dve.wait_ge(s_rstd, i // 4 + 1)
                wait(dve, s_scat[i % 4], 16 * (i // 4))
                dve.tensor_scalar(xn[:, i % 4, :], xres[:, i, :], mv[:, i, 0:1], rstd[:, i:i + 1],
                                  ALU.subtract, ALU.mult).then_inc(s_xn, 1)
            for j in range(E0 * DC):
                dve.wait_ge(s_wh, j + 1)
                dve.tensor_tensor(wl[:, j, :], bank[6 + j % 2][:, :], f32(wh[:, j, :]), ALU.subtract).then_inc(s_wl, 1)

            def x_low(t, par):
                dve.wait_ge(s_xh, t + 1)
                dve.tensor_tensor(xl[par][:, :, :].rearrange("p k n -> p (k n)"), bank[0][:, :],
                                  f32(xh[par][:, :, :]).rearrange("p k n -> p (k n)"), ALU.subtract).then_inc(s_xl, 1)

            def step(t, par):
                if inside(t + 1, 0, NT0):
                    x_low(t + 1, 1 - par)
                if inside(t, 0, NT0):
                    dve.wait_ge(s_sg, t + 1)
                    if inside(t - 2, 0, NT0):
                        dve.wait_ge(s_mT, t - 1)
                    dve.tensor_tensor(mid[par][:, :], bank[2 + par][:, :], sg[par][:, :], ALU.mult).then_inc(s_mid, 1)
                if inside(t - 1, 0, NT0):
                    dve.wait_ge(s_hh, t)
                    dve.tensor_tensor(hl[1 - par][:, :, :].rearrange("p k n -> p (k n)"), bank[1][:, :],
                                      f32(hh[1 - par][:, :, :]).rearrange("p k n -> p (k n)"), ALU.subtract).then_inc(s_hl, 1)

            x_low(0, 0)
            for t in range(0, 4):
                step(t, t % 2)
            with dve.Fori(4, 4 + 2 * ((NT0 - 1 - 4) // 2), 2) as t:
                step(t, 0)
                step(t + 1, 1)
            for t in range(4 + 2 * ((NT0 - 1 - 4) // 2), NT0 + 2):
                step(t, t % 2)
            for q in range(NB):
                for i in range(4 * q, 4 * q + 4):
                    dve.wait_ge(s_yg[i % 4], 16 * (i // 4 + 1))
                    dve.scalar_tensor_tensor(out=xres[:, i, :], in0=yg[i % 4], scalar=gates[:, 0:1], in1=xres[:, i, :],
                                             op0=ALU.mult, op1=ALU.add).then_inc(s_x1, 1)
                    dve.wait_ge(s_x1, i + 1)
                    last = dve.bn_stats(stats[:, i, :], xres[:, i, :])
                chain(last)
                for i in range(4 * q, 4 * q + 4):
                    last = dve.bn_aggr(mv[:, i, :], stats[:, i, :])
                chain(last)
                dve.tensor_scalar(vare[:, 4 * q:4 * q + 4], mv[:, 4 * q:4 * q + 4, 1], EPS, None, ALU.add).then_inc(s_var, 1)

            for b in range(NB):
                dve.wait_ge(s_rstd, 4 + b + 1)
                wait(dve, s_bT, 4 * b)
                for i in range(4):
                    t = 4 * b + i
                    dve.tensor_scalar(xnb[:, i, :], xres[:, t, :], mv[:, t, 0:1], rstd[:, t:t + 1],
                                      ALU.subtract, ALU.mult).then_inc(s_xnb, 1)
                for c in range(DC):
                    n = b * DC + c
                    dve.wait_ge(s_bTh, n + 1)
                    dve.scalar_tensor_tensor(out=xTl[:, b, c, :], in0=bank[n % 4][:, :], scalar=tab[:, T_SUG + c:T_SUG + c + 1],
                                             in1=f32(xTh[:, b, c, :]), op0=ALU.mult, op1=ALU.subtract).then_inc(s_bTl, 1)

            def prep_a(j, m):
                wait(dve, s_pb, 4 * j + 2 * m)
                for i in range(2):
                    dve.wait_ge(s_pa, 4 * j + 2 * m + i + 1)
                    dve.tensor_copy(wt1[:, :, i * P:(i + 1) * P], bank[6 + i][:, :].rearrange("p (n c) -> p c n", c=DC))\
                       .then_inc(s_t1, 1)

            def prep_b(j, m, slot):
                for i in range(2):
                    dve.wait_ge(s_gwh, 4 * j + 2 * m + i + 1)
                    dve.tensor_tensor(gwl[slot][:, m, 2 * i:2 * i + 2, :].rearrange("p c f -> p (c f)"), bank[6 + i][:, :],
                                      f32(gwh[slot][:, m, 2 * i:2 * i + 2, :]).rearrange("p c f -> p (c f)"), ALU.subtract)\
                       .then_inc(s_gwl, 1)

            def prep_w(j, slot):
                dve.tensor_scalar(gsc[slot][:, :], tab[:, bass.ds(T_WGT + 2 * j, 2)], 1.0, None, ALU.mult).then_inc(s_gsc, 1)
                wait(dve, s_wdh, 2 * j)
                wait(dve, s_wdl, 2 * j)
                for f in range(2):
                    dve.wait_ge(s_pw, 2 * j + f + 1)
                    dve.scalar_tensor_tensor(out=wdt[:, f, :], in0=bank[6 + f][:, :], scalar=tab[:, bass.ds(T_SDP + 2 * j + f, 1)],
                                             in1=wrow[:, :], op0=ALU.mult, op1=ALU.mult).then_inc(s_wdt, 1)

            def add_down(j, b):
                for i in range(4):
                    dve.wait_ge(s_bd, 16 * j + 4 * b + i + 1)
                    wait(dve, s_acc, 16 * j + 4 * b + i - 8)
                    dve.tensor_tensor(xres[:, 4 * b + i, :], bank[4 + i % 2][:, :], xres[:, 4 * b + i, :], ALU.add)\
                       .then_inc(s_acc, 1)

            def hidden(j, b):
                for f in range(2):
                    k = 8 * j + 2 * b + f
                    dve.wait_ge(s_bs, k + 1)
                    dve.scalar_tensor_tensor(out=bs[:, f, :], in0=bank[2 * f + 1][:, :], scalar=tab[:, bass.ds(T_WUP + 2 * j + f, 1)],
                                             in1=bs[:, f, :], op0=ALU.mult, op1=ALU.mult).then_inc(s_bh, 1)
                    dve.wait_ge(s_bhh, k + 1)
                    dve.tensor_tensor(bhl[b % 2][:, f, :], bs[:, f, :], f32(bhh[b % 2][:, f, :]), ALU.subtract)\
                       .then_inc(s_bhl, 1)

            def low_down(j):
                for f in range(2):
                    dve.wait_ge(s_wdh, 2 * j + f + 1)
                    dve.tensor_tensor(wdl[:, f, :], wdt[:, f, :], f32(wdh[:, f, :]), ALU.subtract).then_inc(s_wdl, 1)

            def chunk(j, slot, first, more):
                hidden(j, 0)
                if not first:
                    add_down(j - 1, 3)
                low_down(j)
                if more:
                    prep_a(j + 1, 0)
                hidden(j, 1)
                add_down(j, 0)
                if more:
                    prep_b(j + 1, 0, 1 - slot)
                    prep_a(j + 1, 1)
                hidden(j, 2)
                add_down(j, 1)
                if more:
                    prep_b(j + 1, 1, 1 - slot)
                hidden(j, 3)
                add_down(j, 2)
                if more:
                    prep_w(j + 1, 1 - slot)

            dve.wait_ge(s_tabc, 4)
            prep_a(0, 0)
            prep_b(0, 0, 0)
            prep_a(0, 1)
            prep_b(0, 1, 0)
            prep_w(0, 0)
            chunk(0, 0, True, True)
            with dve.Fori(1, NJ - 2, 2) as j:
                chunk(j, 1, False, True)
                chunk(j + 1, 0, False, True)
            chunk(NJ - 1, 1, False, False)
            add_down(NJ - 1, 3)

            def norm_stats(b, done):
                for i in range(4 * b, 4 * b + 4):
                    last = dve.bn_stats(stats[:, i, :], xres[:, i, :])
                chain(last)
                for i in range(4 * b, 4 * b + 4):
                    last = dve.bn_aggr(mv[:, i, :], stats[:, i, :])
                chain(last)
                dve.tensor_scalar(vare[:, 4 * b:4 * b + 4], mv[:, 4 * b:4 * b + 4, 1], EPS, None, ALU.add).then_inc(s_var, 1)
                dve.wait_ge(s_rstd, done)

            def norm(out_ap, t, scale):
                return dve.tensor_scalar(out_ap, xres[:, t, :], mv[:, t, 0:1], scale, ALU.subtract, ALU.mult)

            def c_norm(b):
                norm_stats(b, 9 + (0, 1, 3, 5)[b])
                wait(dve, s_ck, 4 * b)
                for i in range(4):
                    norm(xnc[:, i, :], 4 * b + i, rstd[:, 4 * b + i:4 * b + i + 1]).then_inc(s_cxn, 1)

            def front(n):
                decay = tab[:, T_DEC + n % DC:T_DEC + n % DC + 1]
                dve.wait_ge(s_ck, n + 1)
                chain(dve.tensor_tensor_scan(co[:, 1:513], decay.broadcast_to([P, 512]), bank[5][:, :], LOWEST, ALU.add, ALU.max))
                wait(dve, s_cl, 3 * n)
                dve.scalar_tensor_tensor(out=cd[:, :], in0=bank[5][:, :], scalar=decay, in1=co[:, 0:512],
                                         op0=ALU.subtract, op1=ALU.subtract).then_inc(s_cf, 1)

            def back(n):
                e = ce[n % 2]
                dve.wait_ge(s_ce, 3 * n + 3)
                dve.wait_ge(s_cv, n + 1)
                chain(dve.tensor_tensor(cev[:, :], bank[6][:, :], e[:, 1, :], ALU.mult))
                wait(dve, s_cna, n)
                dve.tensor_tensor_scan(cp[:, 1:513], e[:, 0, :], cev[:, :], 0.0, ALU.mult, ALU.add)
                chain(dve.tensor_tensor_scan(cq[:, 1:513], e[:, 0, :], e[:, 1, :], 0.0, ALU.mult, ALU.add))
                wait(dve, s_cy, n)
                dve.tensor_tensor(cnum[:, :], bank[6][:, :], e[:, 2, :], ALU.mult).then_inc(s_cn, 1)
                chain(dve.tensor_tensor(e[:, 2, :], e[:, 2, :], cq[:, 0:512], ALU.add))
                dve.reciprocal(e[:, 2, :], e[:, 2, :]).then_inc(s_cd, 1)

            def add_out(n):
                b, c = divmod(n, DC)
                dve.wait_ge(s_cr, n + 1)
                x_part = xres[:, 4 * b:4 * b + 4, c * P:(c + 1) * P]
                dve.scalar_tensor_tensor(out=x_part, in0=bank[7][:, :].rearrange("p (i c) -> p i c", i=4), scalar=gates[:, 1:2],
                                         in1=x_part, op0=ALU.mult, op1=ALU.add).then_inc(s_co, 1)

            def d_norm(b):
                dve.wait_ge(s_co, 4 * b + 4)
                norm_stats(b, 9 + (2, 4, 6, 7)[b])

            def d_xn(t, par):
                wait(dve, s_dxT, t - 1)
                norm(xsd[par][:, :], t, rstd[:, t:t + 1]).then_inc(s_dxn, 1)

            def d_x(t, par):
                dve.wait_ge(s_dxh, t + 1)
                dve.tensor_tensor(dxl[par][:, :, :].rearrange("p k n -> p (k n)"), bank[0][:, :],
                                  f32(dxh[par][:, :, :]).rearrange("p k n -> p (k n)"), ALU.subtract).then_inc(s_dxl, 1)

            def d_mul(t, par, shared):
                dve.wait_ge(s_dsg, t + 1)
                wait(dve, s_dmT, t - 1)
                if shared:
                    dve.tensor_copy(lg[:, t, :], bank[2][:, HID:G_W]).then_inc(s_lg, 1)
                dve.tensor_tensor(dmid[par][:, :], bank[3][:, 0:HID], dsg[:, :], ALU.mult).then_inc(s_dmid, 1)

            def d_hid(t, par):
                dve.wait_ge(s_dhh, t + 1)
                dve.tensor_tensor(dhl[par][:, :, :].rearrange("p k n -> p (k n)"), bank[1][0:HP, :],
                                  f32(dhh[par][:, :, :]).rearrange("p k n -> p (k n)"), ALU.subtract).then_inc(s_dhl, 1)

            dve.wait_ge(s_acc, 16 * NJ)
            dve.memset(co[:, 0:1], LOWEST)
            dve.memset(cp[:, 0:1], 0.0)
            dve.memset(cq[:, 0:1], 0.0)
            dve.memset(mask1[:, :, :], 0.0)
            chain(dve.tensor_tensor(wub[:, :], tab[:, T_DEC:T_BON], tab[:, T_BON:T_ROWS], ALU.add))
            chain(dve.tensor_scalar(wlim[:, :], wub[:, :], -1.0, BIG, ALU.mult, ALU.add))
            c_norm(0)
            front(0)
            for n in range(NU + 5):
                t = n - 5
                if t >= 0 and t % 4 != 3:
                    d_xn(t + 1, (t + 1) % 2)
                if n + 1 < NU:
                    front(n + 1)
                if t >= 0 and t % 4 != 3:
                    d_x(t + 1, (t + 1) % 2)
                if t >= 1:
                    d_hid(t - 1, (t - 1) % 2)
                if 1 <= n <= NU:
                    add_out(n - 1)
                if n < NU:
                    back(n)
                if t >= 0:
                    d_mul(t, t % 2, True)
                if n % 4 == 2 and n + 2 < NU:
                    c_norm(n // 4 + 1)
                if n % 4 == 0 and 4 <= n <= NU:
                    d_norm(n // 4 - 1)
                    d_xn(t + 1, (t + 1) % 2)
                    d_x(t + 1, (t + 1) % 2)
            d_hid(TT - 1, 1)

            def per_token(ap):
                return ap.unsqueeze(2).broadcast_to([P, TT, E1])

            dve.wait_ge(s_lg, TT)
            dve.wait_ge(s_b8, 16)
            chain(dve.tensor_reduce(red[:, :], lg[:, :, :], AX.X, ALU.max))
            dve.tensor_tensor(lg[:, :, :], lg[:, :, :], per_token(red[:, :]), ALU.subtract).then_inc(s_lg, 1)
            dve.wait_ge(s_ex8, 1)
            chain(dve.tensor_reduce(red[:, :], prob[:, :, :], AX.X, ALU.add))
            chain(dve.reciprocal(red[:, :], red[:, :]))
            chain(dve.tensor_tensor(prob[:, :, :], prob[:, :, :], per_token(red[:, :]), ALU.mult))
            chain(dve.tensor_tensor(pb[:, :, :], prob[:, :, :], bias8[:, :].unsqueeze(1).broadcast_to([P, TT, E1]), ALU.add))
            for t in range(TT):
                last = dve.max(best[:, t, :], pb[:, t, :])
            chain(last)
            for t in range(TT):
                last = dve.max_index(bix[:, t, :], best[:, t, :], pb[:, t, :])
            chain(last)
            chain(dve.tensor_copy(bixf[:, :, :], bix[:, :, :]))
            count = cst[:, C_IOTA:C_IOTA + E1].unsqueeze(1).broadcast_to([P, TT, E1])
            for k in range(2):
                last = dve.tensor_tensor(sel[k][:, :, :], per_token(bixf[:, :, k]), count, ALU.is_equal)
            chain(last)
            dve.tensor_tensor(mask1[:, 0:TT, :], sel[0][:, :, :], sel[1][:, :, :], ALU.add).then_inc(s_mask1, 1)
            for k in range(2):
                chain(dve.tensor_tensor(tmp8[:, :, :], sel[k][:, :, :], prob[:, :, :], ALU.mult))
                chain(dve.tensor_reduce(rsc[:, k, :], tmp8[:, :, :], AX.X, ALU.add))
                chain(dve.tensor_tensor(rsc[:, k, :], rsc[:, k, :], rstd[:, :], ALU.mult))
            dve.wait_ge(s_rank1, 1)
            chain(dve.tensor_copy(base1[:, :, :].rearrange("p i e -> p (i e)"), bank[5][:, 0:(TT + 1) * E1]))
            chain(dve.tensor_tensor(cmp1[:, :, :], base1[:, TT, :].unsqueeze(2).broadcast_to([P, E1, TT]),
                                    cst[:, C_THR:C_THR + TT].unsqueeze(1).broadcast_to([P, E1, TT]), ALU.is_gt))
            chain(dve.tensor_reduce(nt1[:, :], cmp1[:, :, :], AX.X, ALU.add))
            chain(dve.tensor_scalar(nt1[:, :], nt1[:, :], 1.0, None, ALU.max))
            chain(dve.tensor_tensor_scan(tend1[:, :], ones[:, 0:E1], nt1[:, :], 0.0, ALU.mult, ALU.add))
            chain(dve.tensor_tensor(tst1[:, :], tend1[:, :], nt1[:, :], ALU.subtract))
            chain(dve.tensor_scalar(tst1[:, :], tst1[:, :], float(P), None, ALU.mult))
            chain(dve.tensor_tensor(base1[:, 0:TT, :], base1[:, 0:TT, :], tst1[:, :].unsqueeze(1).broadcast_to([P, TT, E1]), ALU.add))
            for k in range(2):
                chain(dve.tensor_tensor(tmp8[:, :, :], base1[:, 0:TT, :], sel[k][:, :, :], ALU.mult))
                chain(dve.tensor_reduce(slf[:, k, :], tmp8[:, :, :], AX.X, ALU.add))
            chain(dve.tensor_copy(slw[:, :, :], slf[:, :, :]))
            chain(dve.tensor_scalar(slf[:, :, :], slf[:, :, :], float(TOK), None, ALU.add))
            chain(dve.tensor_copy(slr[:, :, :], slf[:, :, :]))
            chain(dve.tensor_copy(tend1_i[:, :], tend1[:, :]))
            chain(dve.tensor_tensor(tcmp1[:, :, :], cst[:, C_IOTA:C_IOTA + 48].unsqueeze(2).broadcast_to([P, 48, E1 - 1]),
                                    tend1[:, 0:E1 - 1].unsqueeze(1).broadcast_to([P, 48, E1 - 1]), ALU.is_ge))
            chain(dve.tensor_reduce(tex1[:, :], tcmp1[:, :, :], AX.X, ALU.add))
            dve.tensor_copy(tex1_i[:, :], tex1[:, :]).then_inc(s_slot1, 1)
            for t in range(TT):
                for k in range(2):
                    n = 2 * t + k
                    wait(dve, s_rsc[n % 4], 16 * (n // 4))
                    norm(row[:, n % 4, :], t, rsc[:, k, t:t + 1]).then_inc(s_row, 1)
            d_x(TT, 0)
            d_x(TT + 1, 1)
            d_mul(TT, 0, False)
            d_x(TT + 2, 0)
            d_mul(TT + 1, 1, False)
            d_hid(TT, 0)
            with dve.Fori(TT + 2, TT + NT1 - 2, 2) as t:
                for i in range(2):
                    d_x(t + i + 1, 1 - i)
                    d_mul(t + i, i, False)
                    d_hid(t + i - 1, 1 - i)
            T = TT + NT1 - 1
            d_mul(T, T % 2, False)
            d_hid(T - 1, (T - 1) % 2)
            d_hid(T, T % 2)
            for t in range(TT):
                for k in range(3):
                    dve.wait_ge(s_fin[t % 4][k], 16 * (t // 4 + 1))
                    last = dve.scalar_tensor_tensor(out=xres[:, t, :], in0=fin[:, 3 * (t % 4) + k, :], scalar=gates[:, 3:4],
                                                    in1=xres[:, t, :], op0=ALU.mult, op1=ALU.add)
                    if k < 2:
                        chain(last)
                last.then_inc(s_x4, 1)


def shape_constants():
    import numpy as np
    def had(n):
        h = np.ones((1, 1), np.float32)
        while h.shape[0] < n:
            h = np.block([[h, h], [h, -h]])
        return h
    c = np.zeros((P, C_W), np.float32)
    c[:, C_ID:C_ID + P] = np.eye(P)
    c[:, C_TRI:C_TRI + P] = np.triu(np.ones((P, P)), 1)
    c[:, C_ONES:C_ONES + P] = 1.0
    c[:, C_H:C_H + P] = had(P)
    c[:, C_H4:C_H4 + P] = np.kron(np.eye(32), had(4))
    c[:, C_H16:C_H16 + P] = np.kron(np.eye(8), had(16))
    c[:, C_THR:C_THR + 16] = P * np.arange(16)
    c[:, C_IOTA:C_IOTA + 48] = np.arange(48)
    c[:, C_HALF:C_HALF + 4] = -0.5
    return c


_INS = ['x', 'itok_BxS_13_99985', 'ctx_2048', 'g_xattn', 'g_ffn',
        'L0_ffn_SU_ug', 'L0_ffn_SU_dp', 'L0_ffn_Wscale_ug', 'L0_ffn_Wscale_dp', 'L0_ffn_W_up', 'L0_ffn_W_gate', 'L0_ffn_W_down',
        'L1_xattn_w', 'L1_xattn_u', 'L1_ffn_gate_w', 'L1_ffn_w1', 'L1_ffn_w2', 'L1_ffn_w3',
        'L1_ffn_sw1', 'L1_ffn_sw2', 'L1_ffn_sw3', 'L1_ffn_expert_bias']


def kernel(**inputs):
    import numpy as _np
    import concourse.bacc as _bacc
    from concourse import mybir as _mybir
    from concourse.bass_utils import run_bass_kernel_spmd as _run

    nc = _bacc.Bacc("TRN2", target_bir_lowering=False, num_devices=1)
    arrays, args = {}, []
    for name in _INS:
        a = _np.ascontiguousarray(inputs[name])
        arrays[f"in_{name}"] = a
        args.append(nc.dram_tensor(f"in_{name}", a.shape, _mybir.dt.from_np(a.dtype), kind="ExternalInput").ap())
    arrays["shape_constants"] = shape_constants()
    args.append(nc.dram_tensor("shape_constants", (P, C_W), F32, kind="ExternalInput").ap())
    args.append(nc.dram_tensor("out_0", (4, 512, D), F32, kind="ExternalOutput").ap())
    program(nc, *args)
    r = _run(nc, [arrays], core_ids=[0])
    return r.results[0]["out_0"]
```

```python
import concourse.bass as bass
from concourse import mybir
from contextlib import ExitStack

ALU = mybir.AluOpType
ACT = mybir.ActivationFunctionType
AX = mybir.AxisListType
F32 = mybir.dt.float32
F32R = mybir.dt.float32r
I32 = mybir.dt.int32

P = 128
D = 512
DC = D // P
TOK = 2048
TT = TOK // P
EPS = 1e-5

E0 = 4
VOCAB = 25000
NT0 = TT + E0 - 1

F0 = 2048
FC = F0 // P
FB = 256
NJ = F0 // FB
NB = 4
T_SUG, T_SDP, T_WUP, T_WGT, T_DEC, T_BON, T_ROWS = 0, 4, 20, 36, 52, 56, 60

NU = NB * DC
BIG = 34.0
LOWEST = -1.0e38

E1 = 8
HID = 448
HC = 4
HP = HID // HC
HELD = TT - 4
NT1 = 2 * TT + E1 - 1
G_W = HID + E1
W_1, W_3, W_2, W_W = 0, HC * G_W, HC * (G_W + HID), HC * (G_W + HID + D)

C_ID, C_TRI, C_ONES, C_H, C_H4, C_H16, C_THR, C_IOTA = 0, 128, 256, 384, 512, 640, 768, 784
C_HALF = C_IOTA + 48
C_W = C_HALF + 4


def program(nc, x, tok, ctx, g_xattn, g_ffn, su_ug, su_dp, wscale_ug, wscale_dp, w_up, w_gate, w_down,
            wkv_w, wkv_u, gate_w, w1, w2, w3, sw1, sw2, sw3, expert_bias, consts, out):
    es = ExitStack()
    with es:
        def sb(name, shape, dt=F32, stack=es):
            return stack.enter_context(nc.sbuf_tensor(name, shape, dt))

        def sem(name):
            return es.enter_context(nc.semaphore(name))

        bank = [es.enter_context(nc.psum_tensor(f"bank{i}", [P, 512], F32)) for i in range(8)]
        xs_dram = nc.dram_tensor("xs_sorted", (NT0 * P, D), F32).ap()
        xs1_dram = nc.dram_tensor("xs1_sorted", (NT1 * P, D), F32).ap()
        y1_dram = nc.dram_tensor("y1_all", ((TT + NT1) * P, D), F32).ap()
        y_dram = nc.dram_tensor("y_sorted", (NT0 * P, D), F32).ap()

        cst = sb("cst", [P, C_W])
        gates = sb("gates", [P, 4])
        zero = sb("zero", [P, P])
        gates_raw = sb("gates_raw", [P, 4])
        tab_in = sb("tab_in", [T_ROWS, P])
        tab = sb("tab", [P, T_ROWS])
        wrow = sb("wrow", [P, D])
        stats = sb("stats", [P, TT, 6])
        mv = sb("mv", [P, TT, 2])
        vare = sb("vare", [P, TT])
        rstd = sb("rstd", [P, TT])
        xres = sb("xres", [P, TT, D])
        sd = ExitStack()
        xsd = [sb(f"xsd{i}", [P, D], F32, sd) for i in range(2)]
        dxh = [sb(f"dxh{i}", [P, DC, P], F32R, sd) for i in range(4)]
        dxl = [sb(f"dxl{i}", [P, DC, P], F32R, sd) for i in range(4)]
        dsg = sb("dsg", [P, HID], F32, sd)
        dmid = [sb(f"dmid{i}", [P, HID], F32, sd) for i in range(2)]
        dhh = [sb(f"dhh{i}", [HP, HC, P], F32R, sd) for i in range(2)]
        dhl = [sb(f"dhl{i}", [HP, HC, P], F32R, sd) for i in range(2)]
        dys = [sb(f"dys{i}", [P, D], F32, sd) for i in range(2)]
        wst = [sb(f"wst{i}", [P, 2048], F32, sd) for i in range(3)]
        row = sb("row", [P, 4, D], F32, sd)
        lg = sb("lg", [P, TT, E1], F32, sd)
        prob = sb("prob", [P, TT, E1], F32, sd)
        pb = sb("pb", [P, TT, E1], F32, sd)
        bias8 = sb("bias8", [P, E1], F32, sd)
        best = sb("best", [P, TT, 8], F32, sd)
        bix = sb("bix", [P, TT, 8], mybir.dt.uint32, sd)
        bixf = sb("bixf", [P, TT, 8], F32, sd)
        red = sb("red", [P, TT], F32, sd)
        sel = [sb(f"sel{i}", [P, TT, E1], F32, sd) for i in range(2)]
        tmp8 = sb("tmp8", [P, TT, E1], F32, sd)
        mask1 = sb("mask1", [P, TT + 1, E1], F32, sd)
        base1 = sb("base1", [P, TT + 1, E1], F32, sd)
        cmp1 = sb("cmp1", [P, E1, TT], F32, sd)
        nt1 = sb("nt1", [P, E1], F32, sd)
        tend1 = sb("tend1", [P, E1], F32, sd)
        tst1 = sb("tst1", [P, E1], F32, sd)
        tcmp1 = sb("tcmp1", [P, 48, E1 - 1], F32, sd)
        tex1 = sb("tex1", [P, 48], F32, sd)
        tex1_i = sb("tex1_i", [P, 48], I32, sd)
        tend1_i = sb("tend1_i", [P, E1], I32, sd)
        slf = sb("slf", [P, 2, TT], F32, sd)
        slw = sb("slw", [P, 2, TT], I32, sd)
        slr = sb("slr", [P, 2, TT], I32, sd)
        rsc = sb("rsc", [P, 2, TT], F32, sd)
        pace = sb("pace", [P, 32], F32, sd)
        wlim = sb("wlim", [P, DC], F32, sd)
        wub = sb("wub", [P, DC], F32, sd)
        s1 = ExitStack()
        sb("fill_h", [P, W_W], F32, s1)
        co = sb("co", [P, 513], F32, s1)
        cd = sb("cd", [P, 512], F32, s1)
        ce = [sb(f"ce{i}", [P, 3, 512], F32, s1) for i in range(2)]
        cev = sb("cev", [P, 512], F32, s1)
        cp = sb("cp", [P, 513], F32, s1)
        cq = sb("cq", [P, 513], F32, s1)
        s1.close()
        s1 = ExitStack()
        fin = sb("fin", [P, 12, D], F32, s1)
        s1.close()
        Wh = sb("Wh", [P, 2, W_W], F32R, sd)
        s1 = ExitStack()
        sb("fill_l", [P, W_W], F32, s1)
        vnat = sb("vnat", [P, 4, D], F32, s1)
        xnc = sb("xnc", [P, 4, D], F32, s1)
        cy = [sb(f"cy{i}", [P, 512], F32, s1) for i in range(2)]
        cnum = sb("cnum", [P, 512], F32, s1)
        s1.close()
        Wl = sb("Wl", [P, 2, W_W], F32R, sd)
        sd.close()

        wd16 = sb("wd16", [P, FC, D])

        sa = ExitStack()
        wh = sb("wh", [P, E0 * DC, D], F32R, sa)
        wl = sb("wl", [P, E0 * DC, D], F32R, sa)
        nat = sb("nat", [P, 2, DC, D], F32, sa)
        wdn = sb("wdn", [P, 2, 8, P], F32, sa)
        xn = sb("xn", [P, 4, D], F32, sa)
        tok_sb = sb("tok_sb", [P, TT], I32, sa)
        ge = sb("ge", [P, TT + 1, E0 + 1], F32, sa)
        mask = sb("mask", [P, TT + 1, E0], F32, sa)
        base = sb("base", [P, TT + 1, E0], F32, sa)
        cmp = sb("cmp", [P, E0, TT], F32, sa)
        ntile = sb("ntile", [P, E0], F32, sa)
        tend = sb("tend", [P, E0], F32, sa)
        tstart = sb("tstart", [P, E0], F32, sa)
        tlast = sb("tlast", [P, E0], F32, sa)
        tlast_i = sb("tlast_i", [P, E0], I32, sa)
        tcmp = sb("tcmp", [P, 48, E0 - 1], F32, sa)
        tex = sb("tex", [P, 48], F32, sa)
        tex_i = sb("tex_i", [P, 48], I32, sa)
        slot_f = sb("slot_f", [P, TT], F32, sa)
        slot = sb("slot", [P, TT], I32, sa)
        xs = [sb(f"xs{i}", [P, D], F32, sa) for i in range(2)]
        xh = [sb(f"xh{i}", [P, DC, P], F32R, sa) for i in range(2)]
        xl = [sb(f"xl{i}", [P, DC, P], F32R, sa) for i in range(2)]
        sg = [sb(f"sg{i}", [P, D], F32, sa) for i in range(2)]
        mid = [sb(f"mid{i}", [P, D], F32, sa) for i in range(2)]
        hh = [sb(f"hh{i}", [P, DC, P], F32R, sa) for i in range(2)]
        hl = [sb(f"hl{i}", [P, DC, P], F32R, sa) for i in range(2)]
        ysb = [sb(f"ysb{i}", [P, D], F32, sa) for i in range(2)]
        sa.close()

        sbk = ExitStack()
        xTh = sb("xTh", [P, NB, DC, 512], F32R, sbk)
        xTl = sb("xTl", [P, NB, DC, 512], F32R, sbk)
        sx = ExitStack()
        xnb = sb("xnb", [P, 4, D], F32, sx)
        sx.close()
        bhh = [sb(f"bhh{i}", [P, 2, 512], F32R, sbk) for i in range(2)]
        bhl = [sb(f"bhl{i}", [P, 2, 512], F32R, sbk) for i in range(2)]
        bs = sb("bs", [P, 2, 512], F32, sbk)
        wn = sb("wn", [P, 8, P], F32, sbk)
        wt1h = sb("wt1h", [P, DC, FB], F32R, sbk)
        gwh = [sb(f"gwh{i}", [P, 2, DC, FB], F32R, sbk) for i in range(2)]
        gwl = [sb(f"gwl{i}", [P, 2, DC, FB], F32R, sbk) for i in range(2)]
        gsc = [sb(f"gsc{i}", [P, 2], F32, sbk) for i in range(2)]
        sx = ExitStack()
        wt1l = sb("wt1l", [P, DC, FB], F32R, sx)
        sx.close()
        wdt = sb("wdt", [P, 2, D], F32, sbk)
        Hr = sb("Hr", [P, P], F32R, sbk)
        wdh = sb("wdh", [P, 2, D], F32R, sbk)
        wdl = sb("wdl", [P, 2, D], F32R, sbk)
        sbk.close()

        ident = cst[:, C_ID:C_ID + P]
        tri = cst[:, C_TRI:C_TRI + P]
        ones = cst[:, C_ONES:C_ONES + P]

        s_cst = sem("s_cst")
        s_gl = sem("s_gl")
        s_x = [sem(f"s_xin{i}") for i in range(4)]
        s_ctx = [sem(f"s_ctx{i}") for i in range(E0)]
        s_zero = sem("s_zero")
        s_zeroed = sem("s_zeroed")
        s_zlast = sem("s_zlast")
        s_gate = sem("s_gate")
        s_rt = sem("s_rt")
        s_rank = sem("s_rank")
        s_slot = sem("s_slot")
        s_var = sem("s_var")
        s_rstd = sem("s_rstd")
        s_xn = sem("s_xn")
        s_scat = [sem(f"s_scat{i}") for i in range(4)]
        s_wT = sem("s_wT")
        s_wh = sem("s_wh")
        s_wl = sem("s_wl")
        s_xs = [sem(f"s_xs{i}") for i in range(2)]
        s_xT = sem("s_xT")
        s_xh = sem("s_xh")
        s_xl = sem("s_xl")
        s_up = sem("s_up")
        s_sg = sem("s_sg")
        s_mid = sem("s_mid")
        s_mT = sem("s_mT")
        s_hh = sem("s_hh")
        s_hl = sem("s_hl")
        s_down = sem("s_down")
        s_y = sem("s_y")
        s_yst = [sem(f"s_yst{i}") for i in range(2)]
        s_yg = [sem(f"s_yg{i}") for i in range(4)]
        s_x1 = sem("s_x1")
        s_out = sem("s_out")
        s_tab = sem("s_tab")
        s_tabT = sem("s_tabT")
        s_tabc = sem("s_tabc")
        s_wrow = sem("s_wrow")
        s_wdn = [sem(f"s_wdn{i}") for i in range(4)]
        s_w16 = sem("s_w16")
        s_w16c = sem("s_w16c")
        s_xnb = sem("s_xnb")
        s_bT = sem("s_bT")
        s_bTh = sem("s_bTh")
        s_bTl = sem("s_bTl")
        s_wn = sem("s_wn")
        s_pa = sem("s_pa")
        s_pb = sem("s_pb")
        s_pw = sem("s_pw")
        s_t1h = sem("s_t1h")
        s_t1 = sem("s_t1")
        s_hr = sem("s_hr")
        s_gwh = sem("s_gwh")
        s_gwl = sem("s_gwl")
        s_gsc = sem("s_gsc")
        s_wdt = sem("s_wdt")
        s_wdh = sem("s_wdh")
        s_wdl = sem("s_wdl")
        s_gu = sem("s_gu")
        s_bs = sem("s_bs")
        s_bh = sem("s_bh")
        s_bhh = sem("s_bhh")
        s_bhl = sem("s_bhl")
        s_bd = sem("s_bd")
        s_acc = sem("s_acc")
        s_vn = sem("s_vn")
        s_cxn = sem("s_cxn")
        s_ck = sem("s_ck")
        s_cv = sem("s_cv")
        s_cf = sem("s_cf")
        s_cl = sem("s_cl")
        s_ce = sem("s_ce")
        s_cn = sem("s_cn")
        s_cna = sem("s_cna")
        s_cd = sem("s_cd")
        s_cy = sem("s_cy")
        s_co = sem("s_co")
        s_cr = sem("s_cr")
        s_wst = [sem(f"s_wst{i}") for i in range(3)]
        s_whi = [sem(f"s_whi{i}") for i in range(3)]
        s_w13 = sem("s_w13")
        s_w2 = sem("s_w2")
        s_dxn = sem("s_dxn")
        s_dxs = [sem(f"s_dxs{i}") for i in range(2)]
        s_dxT = sem("s_dxT")
        s_dxh = sem("s_dxh")
        s_dxl = sem("s_dxl")
        s_dup = sem("s_dup")
        s_dsg = sem("s_dsg")
        s_dmid = sem("s_dmid")
        s_dmT = sem("s_dmT")
        s_dhh = sem("s_dhh")
        s_dhl = sem("s_dhl")
        s_dd = sem("s_dd")
        s_dy = sem("s_dy")
        s_dst = [sem(f"s_dst{i}") for i in range(2)]
        s_b8 = sem("s_b8")
        s_lp = sem("s_lp")
        s_lg = sem("s_lg")
        s_gw = sem("s_gw")
        s_gwhi = sem("s_gwhigh")
        s_wsh = [sem(f"s_wsh{i}") for i in range(3)]
        s_gwlow = sem("s_gwlow")
        s_ex8 = sem("s_ex8")
        s_mask1 = sem("s_mask1")
        s_rank1 = sem("s_rank1")
        s_slot1 = sem("s_slot1")
        s_row = sem("s_row")
        s_rsc = [sem(f"s_rsc{i}") for i in range(4)]
        s_zero1 = sem("s_zero1")
        s_shl = sem("s_shl")
        s_sha = sem("s_sha")
        s_fin = [[sem(f"s_fin{i}_{k}") for k in range(2)] for i in range(6)]
        s_x4 = sem("s_x4")

        x_v = x.rearrange("b (i p) d -> p (b i) d", p=P)
        out_v = out.rearrange("b (i p) d -> p (b i) d", p=P)
        tok_v = tok.rearrange("b (i p) -> p (b i)", p=P)
        ctx_v = ctx.rearrange("e (f p) d -> p e f d", p=P)
        yg = [nat[:, 0, i, :] for i in range(4)]
        wdn_at = [wdn[:, n, :, :] for n in range(2)] + [
            nat[:, 1, 2 * n:2 * n + 2, :].rearrange("p a (h c) -> p (a h) c", c=P) for n in range(2)]
        wd_v = w_down.rearrange("(h a) (c p) -> (a c) h p", a=8, p=P)
        wug_v = [w.rearrange("(h a) (c p) -> (a c) h p", a=32, p=P) for w in (w_gate, w_up)]

        def wait(eng, s, v):
            if not isinstance(v, int) or v > 0:
                eng.wait_ge(s, v)

        def f32(ap):
            return ap.bitcast(F32)

        def inside(t, lo, hi):
            return not isinstance(t, int) or lo <= t < hi

        shared_part = (sw1.rearrange("(k p) n -> p k n", p=P), sw3.rearrange("(k p) n -> p k n", p=P),
                       sw2.rearrange("(k p) n -> p k n", p=HP))
        router = gate_w.rearrange("(k p) n -> p k n", p=P)

        def w_rows(p, width):
            q, step = ((P, G_W), (P, HID), (HP, D))[p]
            return wst[p][0:q, 0:HC * step].rearrange("p (k n) -> p k n", k=HC)[:, :, 0:width]

        def x_buf(t, par):
            return par + 2 if isinstance(t, int) and HELD + 2 <= t < TT else par

        block = es.enter_context(nc.Block())

        @block.sync
        def _(sp):
            sp.dma_start(cst[:, :], consts).then_inc(s_cst, 16)
            sp.dma_start(tok_sb[:, :], tok_v, allow_slow_non_contiguous=True).then_inc(s_cst, 16)
            sp.dma_start(tab_in[T_SUG:T_SDP, :], su_ug.rearrange("(c p) -> c p", p=P)).then_inc(s_tab, 16)
            sp.dma_start(tab_in[T_SDP:T_WUP, :], su_dp.rearrange("(c p) -> c p", p=P)).then_inc(s_tab, 16)
            sp.dma_start(tab_in[T_DEC:T_BON, :], wkv_w.rearrange("(c p) -> c p", p=P)).then_inc(s_tab, 16)
            sp.dma_start(tab_in[T_BON:T_ROWS, :], wkv_u.rearrange("(c p) -> c p", p=P)).then_inc(s_tab, 16)
            sp.dma_start(tab_in[T_WUP:T_DEC, :], wscale_ug.rearrange("(c p) -> c p", p=P)).then_inc(s_tab, 16)
            for e in range(2):
                sp.dma_start(nat[:, e, :, :], ctx_v[:, e, :, :]).then_inc(s_ctx[e], 16)
            for q in range(4):
                sp.dma_start(xres[:, 4 * q:4 * q + 4, :], x_v[:, 4 * q:4 * q + 4, :]).then_inc(s_x[q], 16)
            for n in range(2):
                sp.dma_start(wdn_at[n], wd_v[:, 8 * n:8 * n + 8, :]).then_inc(s_wdn[n], 16)
            for e in range(2, E0):
                sp.wait_ge(s_wT, (e - 1) * DC)
                sp.dma_start(nat[:, e % 2, :, :], ctx_v[:, e, :, :]).then_inc(s_ctx[e], 16)
            sp.wait_ge(s_wT, E0 * DC)
            for n in range(2, 4):
                sp.dma_start(wdn_at[n], wd_v[:, 8 * n:8 * n + 8, :]).then_inc(s_wdn[n], 16)
            for q in range(4):
                sp.wait_ge(s_scat[q], 16 * TT // 4)

            def load(t, par):
                sp.dma_start(xs[par][:, :], xs_dram[bass.ds(t * P, P), :]).then_inc(s_xs[par], 16)

            load(0, 0)
            load(1, 1)

            def step(t, par):
                if inside(t + 2, 0, NT0):
                    sp.wait_ge(s_xT, t + 1)
                    load(t + 2, par)
                if inside(t - 2, 0, NT0):
                    sp.wait_ge(s_y, t - 1)
                    sp.dma_start(y_dram[bass.ds((t - 2) * P, P), :], ysb[par][:, :]).then_inc(s_yst[par], 16)

            step(0, 0)
            step(1, 1)
            with sp.Fori(2, 2 + 2 * ((NT0 - 4) // 2), 2) as t:
                step(t, 0)
                step(t + 1, 1)
            for t in range(2 + 2 * ((NT0 - 4) // 2), NT0 + 2):
                step(t, t % 2)

            for n in range(4, 8):
                sp.wait_ge(s_w16, 2 * (n - 3))
                sp.dma_start(wdn_at[n % 4], wd_v[:, 8 * n:8 * n + 8, :]).then_inc(s_wdn[n % 4], 16)
            sp.wait_ge(s_w16, 16)
            sp.wait_ge(s_x1, TT)

            def load_wn(j, m):
                wait(sp, s_pa, 4 * j + 2 * m)
                sp.dma_start(wn[:, :, :], wug_v[m][:, bass.ds(j * 8, 8), :]).then_inc(s_wn, 16)

            load_wn(0, 0)
            load_wn(0, 1)
            load_wn(1, 0)
            load_wn(1, 1)
            with sp.Fori(2, NJ) as j:
                load_wn(j, 0)
                load_wn(j, 1)

            sp.wait_ge(s_acc, 16 * NJ)
            sp.dma_start(vnat[:, :, :], ctx_v[:, 0, :, :]).then_inc(s_vn, 16)
            sp.dma_start(w_rows(0, G_W)[:, :, HID:G_W], router).then_inc(s_gw, 16)
            for p in range(3):
                sp.dma_start(w_rows(p, (HID, HID, D)[p]), shared_part[p]).then_inc(s_wsh[p], 16)
            sp.dma_start(bias8[:, :], expert_bias.rearrange("(a n) -> a n", a=1).broadcast_to([P, E1])).then_inc(s_b8, 16)

            def load(t, par):
                sp.dma_start(xsd[par][:, :], xs1_dram[bass.ds((t - TT) * P, P), :]).then_inc(s_dxs[par], 16)

            def store(t, par):
                sp.wait_ge(s_dy, t + 1)
                sp.dma_start(y1_dram[bass.ds(t * P, P), :], dys[par][:, :]).then_inc(s_dst[par], 16)

            for n in range(TT + 7):
                if n % 4 == 0 and 0 < n < NU:
                    wait(sp, s_cv, n)
                    sp.dma_start(vnat[:, :, :], ctx_v[:, n // 4, :, :]).then_inc(s_vn, 16)
                if n >= 7:
                    store(n - 7, (n - 7) % 2)
            for i in range(4):
                sp.wait_ge(s_rsc[i], 16 * 2 * TT // 4)
            load(TT, 0)
            load(TT + 1, 1)
            for t in range(2):
                sp.wait_ge(s_dxT, TT + t + 1)
                load(TT + 2 + t, t)
            for i in range(2):
                sp.wait_ge(s_dst[i], 16 * TT // 2)

            def pair(t):
                for i in range(2):
                    sp.wait_ge(s_dxT, t + i + 1)
                    load(t + i + 2, i)
                    store(t + i - 2, i)

            with sp.Fori(TT + 2, TT + 1 + 2 * TT, 2) as t:
                sp.wait_ge(s_sha, t - TT)
                sp.dma_start(row[:, 0, :], y1_dram[bass.ds((t - TT - 2) * (P // 2), P), :]).then_inc(s_shl, 16)
                pair(t)
            for t in range(TT + 2 + 2 * TT, TT + NT1 - 4, 2):
                pair(t)
            sp.wait_ge(s_dxT, TT + NT1 - 2)
            load(TT + NT1 - 1, 0)
            for t in range(TT + NT1 - 5, TT + NT1):
                store(t, t % 2)

            for t in range(TT):
                if t % 4 == 3 and t >= 7:
                    q = t // 4 - 1
                    sp.wait_ge(s_x4, 4 * q + 4)
                    sp.dma_start(out_v[:, 4 * q:4 * q + 4, :], xres[:, 4 * q:4 * q + 4, :]).then_inc(s_out, 16)
            sp.wait_ge(s_x4, TT)
            sp.dma_start(out_v[:, TT - 4:TT, :], xres[:, TT - 4:TT, :]).then_inc(s_out, 16)
            sp.wait_ge(s_out, 64)

        @block.gpsimd
        def _(pool):
            pool.wait_ge(s_cst, 32)
            pool.memset(zero[:, :], 0.0).then_inc(s_zero, 1)
            pool.wait_ge(s_zero, 1)
            pool.dma_start(xs_dram[TOK:NT0 * P, :].rearrange("(p r) (a d) -> p (r a) d", p=P, d=P),
                           zero[:, :].unsqueeze(1).broadcast_to([P, (NT0 - TT) * DC, P])).then_inc(s_zeroed, 16)

            def inv_std(n, q=None):
                q = n % 4 if q is None else q
                pool.wait_ge(s_var, n + 1)
                pool.tensor_tensor(rstd[:, 4 * q:4 * q + 4], vare[:, 4 * q:4 * q + 4],
                                   cst[:, C_HALF:C_HALF + 4], ALU.pow).then_inc(s_rstd, 1)

            for q in range(4):
                inv_std(q)
            pool.wait_ge(s_zeroed, 16)
            pool.wait_ge(s_slot, 1)
            for e in range(E0):
                last = pool.value_load(tlast_i[0:1, e:e + 1], min_val=0, max_val=NT0 - 1)
                if e >= 1:
                    pool.wait_ge(s_zlast, 16 * e)
                pool.dma_start(xs_dram[bass.ds(last * P, P), :].rearrange("p (a d) -> p a d", d=P),
                               zero[:, :].unsqueeze(1).broadcast_to([P, DC, P])).then_inc(s_zlast, 16)
            pool.wait_ge(s_zlast, 16 * E0)
            for i in range(TT):
                pool.wait_ge(s_xn, i + 1)
                pool.indirect_dma_start(xs_dram, bass.IndirectOffsetOnAxis(ap=slot[:, i:i + 1], axis=0),
                                        xn[:, i % 4, :], None).then_inc(s_scat[i % 4], 16)
            pool.wait_ge(s_yst[0], 16 * ((NT0 + 1) // 2))
            pool.wait_ge(s_yst[1], 16 * (NT0 // 2))
            for q in range(NB):
                for i in range(4 * q, 4 * q + 4):
                    if i >= 4:
                        pool.wait_ge(s_x1, i - 3)
                    pool.indirect_dma_start(yg[i % 4], None, y_dram,
                                            bass.IndirectOffsetOnAxis(ap=slot[:, i:i + 1], axis=0))\
                        .then_inc(s_yg[i % 4], 16)
                if q >= 1:
                    inv_std(4 + q - 1)
            inv_std(4 + NB - 1)

            def w_part(idx, p):
                if isinstance(idx, int) and idx == 0:
                    return shared_part[p]
                w, q = ((w1, P), (w3, P), (w2, HP))[p]
                return w[bass.ds(idx - 1, 1), :, :].rearrange("e (k p) n -> p (e k) n", p=q)

            places = [0]

            def alone(idx):
                if not isinstance(idx, int) or idx > 2:
                    n = places[0] = places[0] + 1
                    pool.tensor_tensor(pace[:, n:n + 1], pace[:, 0:1], pace[:, 0:1], ALU.add)

            def w_raw(idx, p):
                pool.dma_start(w_rows(p, (HID, HID, D)[p]), w_part(idx, p)).then_inc(s_wst[p], 16)

            def w_place(whole, slot, p, width):
                q, at, step = ((P, W_1, G_W), (P, W_3, HID), (HP, W_2, D))[p]
                return whole[0:q, slot, at:at + HC * step].rearrange("p (k n) -> p k n", k=HC)[:, :, 0:width]

            def w_high(idx, p, slot):
                pool.dma_start(w_place(Wh, slot, p, (HID, HID, D)[p]), w_part(idx, p)).then_inc(s_whi[p], 16)

            def w_low(idx, p, slot):
                width = (HID, HID, D)[p]
                if isinstance(idx, int) and idx == 0:
                    pool.wait_ge(s_wsh[p], 16)
                else:
                    pool.wait_ge(s_wst[p], 16 * idx)
                pool.wait_ge(s_whi[p], 16 * (idx + 1))
                pool.tensor_tensor(w_place(Wl, slot, p, width), w_rows(p, width), f32(w_place(Wh, slot, p, width)), ALU.subtract)\
                    .then_inc((s_w13, s_w13, s_w2)[p], 1)
                if p < 2:
                    pool.wait_ge(s_w13, 2 * idx + p + 1)
                else:
                    pool.wait_ge(s_w2, idx + 1)

            for q in range(3):
                pool.wait_ge(s_gu, 8 * q + 4)
                pool.dma_start(xs1_dram.rearrange("(q p r) (a d) -> q p (r a) d", p=P, q=3, d=P)[q],
                               zero[:, :].unsqueeze(1).broadcast_to([P, NT1 // 3 * DC, P])).then_inc(s_zero1, 16)
            pool.wait_ge(s_zero1, 48)
            pool.wait_ge(s_acc, 16 * NJ)
            inv_std(8)
            pool.memset(pace[:, :], 0.0).then_inc(s_zero, 1)
            pool.wait_ge(s_zero, 2)

            def w_shared():
                pool.dma_start(w_place(Wh, 0, 0, G_W)[:, :, HID:G_W], router).then_inc(s_gwhi, 16)
                for p in range(3):
                    w_high(0, p, 0)

            def w_router_low():
                pool.wait_ge(s_gw, 16)
                pool.wait_ge(s_gwhi, 16)
                pool.tensor_tensor(w_place(Wl, 0, 0, G_W)[:, :, HID:G_W], w_rows(0, G_W)[:, :, HID:G_W],
                                   f32(w_place(Wh, 0, 0, G_W))[:, :, HID:G_W], ALU.subtract).then_inc(s_gwlow, 1)

            def w_all(idx, slot, ups=None, downs=None, more=True):
                if ups is not None:
                    pool.wait_ge(s_dup, ups)
                    alone(idx)
                for p in range(2):
                    w_high(idx, p, slot)
                for p in range(2):
                    w_low(idx, p, slot)
                    if more:
                        alone(idx)
                        w_raw(idx + 1, p)
                if downs is not None:
                    pool.wait_ge(s_dd, downs)
                    alone(idx)
                w_high(idx, 2, slot)
                w_low(idx, 2, slot)
                if more:
                    alone(idx)
                    w_raw(idx + 1, 2)

            def clamp(n):
                pool.wait_ge(s_cf, n + 1)
                wait(pool, s_ce, 3 * n)
                pool.tensor_scalar(row[:, 0, :], cd[:, :], 0.0, None, ALU.max).then_inc(s_cl, 1)
                pool.tensor_scalar(row[:, 1, :], cd[:, :], 0.0, None, ALU.min).then_inc(s_cl, 1)
                pool.tensor_scalar(row[:, 2, :], cd[:, :], wlim[:, n % DC:n % DC + 1], None, ALU.min).then_inc(s_cl, 1)

            def finish(n):
                pool.wait_ge(s_cn, n + 1)
                pool.tensor_tensor(cnum[:, :], cnum[:, :], cp[:, 0:512], ALU.add).then_inc(s_cna, 1)
                pool.wait_ge(s_cna, n + 1)
                pool.wait_ge(s_cd, n + 1)
                wait(pool, s_cr, n - 1)
                pool.tensor_tensor(cy[n % 2][:, :], cnum[:, :], ce[n % 2][:, 2, :], ALU.mult).then_inc(s_cy, 1)

            clamp(0)
            w_shared()
            power = 9
            for n in range(NU + 1):
                if n + 1 < NU:
                    clamp(n + 1)
                if n < NU:
                    finish(n)
                if n == 0:
                    w_router_low()
                if 1 <= n <= 3:
                    w_low(0, n - 1, 0)
                if n % 4 == 2 and n + 2 < NU:
                    inv_std(power, n // 4 + 1)
                    power += 1
                if n % 4 == 0 and n >= 4:
                    inv_std(power, n // 4 - 1)
                    power += 1
            pool.wait_ge(s_co, NU)
            for p in range(3):
                w_raw(1, p)
            w_all(1, 1)
            pool.wait_ge(s_slot1, 1)
            for t in range(TT):
                for k in range(2):
                    n = 2 * t + k
                    pool.wait_ge(s_row, n + 1)
                    pool.indirect_dma_start(xs1_dram, bass.IndirectOffsetOnAxis(ap=slw[:, k, t:t + 1], axis=0),
                                            row[:, n % 4, :], None).then_inc(s_rsc[n % 4], 16)
            w_all(2, 0, TT, TT)

            def w_next(idx, slot, more=True):
                last = pool.value_load(tend1_i[0:1, bass.ds(idx - 3, 1)], min_val=1, max_val=NT1)
                w_all(idx, slot, last + TT, last + TT, more)

            with pool.Fori(3, E1 - 2, 2) as idx:
                w_next(idx, 1)
                w_next(idx + 1, 0)
            w_next(E1 - 1, 1)
            w_next(E1, 0, False)
            for i in range(2):
                pool.wait_ge(s_dst[i], 16 * ((TT + NT1 + 1 - i) // 2))
            for t in range(TT):
                if t >= 6:
                    pool.wait_ge(s_x4, t - 5)
                for k in range(2):
                    pool.indirect_dma_start(fin[:, 2 * (t % 6) + k, :], None, y1_dram,
                                            bass.IndirectOffsetOnAxis(ap=slr[:, k, t:t + 1], axis=0))\
                        .then_inc(s_fin[t % 6][k], 16)

        @block.scalar
        def _(act):
            act.dma_start(gates_raw[:, 0:2], g_xattn.rearrange("(a n) -> a n", a=1).broadcast_to([P, 2])).then_inc(s_gl, 16)
            act.dma_start(gates_raw[:, 2:4], g_ffn.rearrange("(a n) -> a n", a=1).broadcast_to([P, 2])).then_inc(s_gl, 16)
            act.dma_start(wrow[:, :], wscale_dp.rearrange("(a n) -> a n", a=1).broadcast_to([P, D])).then_inc(s_wrow, 16)
            act.wait_ge(s_gl, 32)
            act.activation(gates[:, :], gates_raw[:, :], ACT.Tanh).then_inc(s_gate, 1)
            act.wait_ge(s_tabT, 1)
            act.activation(tab[:, :], bank[4][:, 0:T_ROWS], ACT.Copy).then_inc(s_tabc, 1)
            act.wait_ge(s_tabc, 1)
            act.mul(tab[:, T_SUG:T_SDP], tab[:, T_SUG:T_SDP], float(D) ** -0.5).then_inc(s_tabc, 1)
            act.mul(tab[:, T_SDP:T_WUP], tab[:, T_SDP:T_WUP], float(F0) ** -0.5).then_inc(s_tabc, 1)
            act.wait_ge(s_wrow, 16)
            act.wait_ge(s_gate, 1)
            act.mul(wrow[:, :], wrow[:, :], gates[:, 2:3]).then_inc(s_tabc, 1)
            for j in range(E0 * DC):
                act.wait_ge(s_wT, j + 1)
                act.activation(wh[:, j, :], bank[6 + j % 2][:, :], ACT.Copy).then_inc(s_wh, 1)


            def x_high(t, par):
                act.wait_ge(s_xT, t + 1)
                if inside(t - 2, 0, NT0):
                    act.wait_ge(s_up, t - 1)
                act.activation(xh[par][:, :, :].rearrange("p k n -> p (k n)"), bank[0][:, :], ACT.Copy).then_inc(s_xh, 1)

            def step(t, par):
                if inside(t + 1, 0, NT0):
                    x_high(t + 1, 1 - par)
                if inside(t, 0, NT0):
                    act.wait_ge(s_up, t + 1)
                    if inside(t - 2, 0, NT0):
                        act.wait_ge(s_mid, t - 1)
                    act.activation(sg[par][:, :], bank[2 + par][:, :], ACT.Silu).then_inc(s_sg, 1)
                if inside(t - 1, 0, NT0):
                    act.wait_ge(s_mT, t)
                    if inside(t - 3, 0, NT0):
                        act.wait_ge(s_down, t - 2)
                    act.activation(hh[1 - par][:, :, :].rearrange("p k n -> p (k n)"), bank[1][:, :], ACT.Copy).then_inc(s_hh, 1)
                if inside(t - 2, 0, NT0):
                    act.wait_ge(s_down, t - 1)
                    if inside(t - 4, 0, NT0):
                        act.wait_ge(s_yst[par], 16 * (t // 2 - 1) if isinstance(t, int) else ((t - par) * 8 - 16))
                    act.activation(ysb[par][:, :], bank[4 + par][:, :], ACT.Copy).then_inc(s_y, 1)

            x_high(0, 0)
            for t in range(0, 4):
                step(t, t % 2)
            with act.Fori(4, 4 + 2 * ((NT0 - 1 - 4) // 2), 2) as t:
                step(t, 0)
                step(t + 1, 1)
            for t in range(4 + 2 * ((NT0 - 1 - 4) // 2), NT0 + 2):
                step(t, t % 2)

            for n in range(16):
                act.wait_ge(s_w16, n + 1)
                act.activation(wd16[:, :, 32 * n:32 * n + 32],
                               bank[6 + n % 2][:, :].rearrange("p (n c) -> p c n", c=FC), ACT.Copy).then_inc(s_w16c, 1)

            for n in range(NB * DC):
                act.wait_ge(s_bT, n + 1)
                b, c = divmod(n, DC)
                act.mul(xTh[:, b, c, :], bank[n % 4][:, :], tab[:, T_SUG + c:T_SUG + c + 1]).then_inc(s_bTh, 1)

            def prep_t(j, m):
                wait(act, s_pb, 4 * j + 2 * m)
                for i in range(2):
                    act.wait_ge(s_pa, 4 * j + 2 * m + i + 1)
                    act.activation(wt1h[:, :, i * P:(i + 1) * P], bank[6 + i][:, :].rearrange("p (n c) -> p c n", c=DC),
                                   ACT.Copy).then_inc(s_t1h, 1)

            def prep_gu(j, m, slot):
                for i in range(2):
                    act.wait_ge(s_pb, 4 * j + 2 * m + i + 1)
                    wait(act, s_gu, 8 * (j - 1))
                    act.activation(gwh[slot][:, m, 2 * i:2 * i + 2, :].rearrange("p c f -> p (c f)"),
                                   bank[6 + i][:, :], ACT.Copy).then_inc(s_gwh, 1)

            def chunk(j, slot, more):
                for b in range(NB):
                    for f in range(2):
                        k = 8 * j + 2 * b + f
                        act.wait_ge(s_gu, k + 1)
                        wait(act, s_bhl, k - 1)
                        if b == 0 and f == 0:
                            act.wait_ge(s_gsc, j + 1)
                        act.activation(bs[:, f, :], bank[2 * f][:, :], ACT.Silu,
                                       scale=gsc[slot][:, f:f + 1]).then_inc(s_bs, 1)
                        act.wait_ge(s_bh, k + 1)
                        wait(act, s_bd, 4 * (4 * j + b - 1))
                        act.activation(bhh[b % 2][:, f, :], bs[:, f, :], ACT.Copy).then_inc(s_bhh, 1)
                    if b == 0:
                        wait(act, s_bd, 16 * j)
                        for f in range(2):
                            act.wait_ge(s_wdt, 2 * j + f + 1)
                            act.activation(wdh[:, f, :], wdt[:, f, :], ACT.Copy).then_inc(s_wdh, 1)
                    if more and b == 0:
                        prep_t(j + 1, 0)
                    if more and b in (1, 2):
                        prep_gu(j + 1, b - 1, 1 - slot)
                    if more and b == 1:
                        prep_t(j + 1, 1)

            act.activation(Hr[:, :], cst[:, C_H:C_H + P], ACT.Copy).then_inc(s_hr, 1)
            for m in range(2):
                prep_t(0, m)
                prep_gu(0, m, 0)
            chunk(0, 0, True)
            with act.Fori(1, NJ - 2, 2) as j:
                chunk(j, 1, True)
                chunk(j + 1, 0, True)
            chunk(NJ - 1, 1, False)

            def exps(n):
                act.wait_ge(s_cl, 3 * n + 3)
                wait(act, s_cy, n - 1)
                e = ce[n % 2]
                act.activation(e[:, 0, :], row[:, 0, :], ACT.Exp, scale=-1.0).then_inc(s_ce, 1)
                act.activation(e[:, 1, :], row[:, 1, :], ACT.Exp).then_inc(s_ce, 1)
                act.activation(e[:, 2, :], row[:, 2, :], ACT.Exp, bias=wub[:, n % DC:n % DC + 1]).then_inc(s_ce, 1)

            def d_x(t, par):
                act.wait_ge(s_dxT, t + 1)
                if x_buf(t, par) == par:
                    wait(act, s_dup, t - 1)
                act.activation(dxh[x_buf(t, par)][:, :, :].rearrange("p k n -> p (k n)"), bank[0][:, :], ACT.Copy).then_inc(s_dxh, 1)

            def d_gate(t, par):
                act.wait_ge(s_dup, t + 1)
                wait(act, s_dmid, t)
                act.activation(dsg[:, :], bank[2][:, 0:HID], ACT.Silu).then_inc(s_dsg, 1)

            def d_hid(t, par):
                act.wait_ge(s_dmT, t + 1)
                wait(act, s_dd, t - 1)
                act.activation(dhh[par][:, :, :].rearrange("p k n -> p (k n)"), bank[1][0:HP, :], ACT.Copy).then_inc(s_dhh, 1)

            def d_y(t, par):
                act.wait_ge(s_dd, t + 1)
                if not isinstance(t, int) or t >= 2:
                    act.wait_ge(s_dst[par], 16 * (t // 2) if isinstance(t, int) else (t - par) * 8)
                act.activation(dys[par][:, :], bank[4][:, :], ACT.Copy).then_inc(s_dy, 1)

            act.wait_ge(s_acc, 16 * NJ)
            exps(0)
            for n in range(NU + 1):
                t = n - 5
                if t >= 0 and t % 4 != 3:
                    d_x(t + 1, (t + 1) % 2)
                if t >= 1:
                    d_hid(t - 1, (t - 1) % 2)
                if n + 1 < NU:
                    exps(n + 1)
                if t >= 0:
                    d_gate(t, t % 2)
                if t >= 2:
                    d_y(t - 2, t % 2)
                if t >= -1 and t % 4 == 3:
                    d_x(t + 1, (t + 1) % 2)
            d_x(HELD + 1, 1)
            d_hid(HELD - 1, 1)
            d_x(HELD + 2, 0)
            d_y(HELD - 2, 0)
            d_x(HELD + 3, 1)
            act.wait_ge(s_lg, HELD + 2)
            act.activation(prob[:, :, :], lg[:, :, :], ACT.Exp).then_inc(s_ex8, 1)
            for t in range(HELD, TT):
                d_gate(t, t % 2)
                d_y(t - 1, (t - 1) % 2)
                d_hid(t, t % 2)
            d_y(TT - 1, 1)
            d_x(TT, 0)
            d_x(TT + 1, 1)
            d_gate(TT, 0)
            d_x(TT + 2, 0)
            d_gate(TT + 1, 1)
            d_hid(TT, 0)
            with act.Fori(TT + 2, TT + NT1 - 2, 2) as t:
                for i in range(2):
                    d_x(t + i + 1, 1 - i)
                    d_gate(t + i, i)
                    d_hid(t + i - 1, 1 - i)
                    d_y(t + i - 2, i)
            T = TT + NT1 - 1
            d_gate(T, T % 2)
            d_hid(T - 1, (T - 1) % 2)
            d_y(T - 2, T % 2)
            d_hid(T, T % 2)
            d_y(T - 1, (T - 1) % 2)
            d_y(T, T % 2)

        @block.tensor
        def _(pe):
            pe.wait_ge(s_cst, 32)

            def weights(e):
                pe.wait_ge(s_ctx[e], 16)
                for k in range(DC):
                    j = e * DC + k
                    if j >= 2:
                        pe.wait_ge(s_wl, j - 1)
                    for f in range(DC):
                        mm = pe.transpose(bank[6 + j % 2][:, f * P:(f + 1) * P], nat[:, e % 2, f, k * P:(k + 1) * P], ident)
                    mm.then_inc(s_wT, 1)

            pe.wait_ge(s_tab, 80)
            pe.transpose(bank[4][:, 0:T_ROWS], tab_in[:, :], ident[0:T_ROWS, 0:T_ROWS]).then_inc(s_tabT, 1)
            pe.wait_ge(s_rt, 1)
            n = (TT + 1) * E0
            pe.matmul(bank[5][:, 0:n], tri, mask[:, :, :].rearrange("p i e -> p (i e)"), start=True, stop=False)
            for j in range(TT):
                pe.matmul(bank[5][:, (j + 1) * E0:n].rearrange("p (i e) -> p i e", e=E0), ones,
                               mask[:, j:j + 1, :].broadcast_to([P, TT - j, E0]), start=False, stop=False,
                               skip_group_check=True)
            pe.matmul(bank[5][:, 0:n].rearrange("p (i e) -> p i e", e=E0), ones,
                      mask[:, TT:TT + 1, :].broadcast_to([P, TT + 1, E0]), start=False, stop=True).then_inc(s_rank, 1)
            for e in range(E0):
                weights(e)
            pe.wait_ge(s_wl, E0 * DC)
            pe.wait_ge(s_slot, 1)

            def x_turn(t, par):
                pe.wait_ge(s_xs[par], (t // 2 + 1) * 16 if isinstance(t, int) else (t - par) * 8 + 16)
                if inside(t - 1, 0, NT0):
                    pe.wait_ge(s_xl, t)
                for k in range(DC):
                    mm = pe.transpose(bank[0][:, k * P:(k + 1) * P], xs[par][:, k * P:(k + 1) * P], ident)
                mm.then_inc(s_xT, 1)

            def step(t, par, ex=[None, None]):
                if inside(t + 1, 0, NT0):
                    x_turn(t + 1, 1 - par)
                if inside(t, 0, NT0):
                    ex[par] = pe.value_load(tex_i[0:1, bass.ds(t, 1)], min_val=0, max_val=E0 - 1)
                    pe.wait_ge(s_xl, t + 1)
                    if inside(t - 2, 0, NT0):
                        pe.wait_ge(s_mid, t - 1)
                    n = 0
                    for a, w in ((xl, wh), (xh, wl), (xh, wh)):
                        for k in range(DC):
                            mm = pe.matmul(bank[2 + par][:, :], a[par][:, k, :], w[:, bass.ds(ex[par] * DC + k, 1), :],
                                           start=(n == 0), stop=(n == 3 * DC - 1))
                            n += 1
                    mm.then_inc(s_up, 1)
                if inside(t - 1, 0, NT0):
                    pe.wait_ge(s_mid, t)
                    if inside(t - 2, 0, NT0):
                        pe.wait_ge(s_hl, t - 1)
                    for k in range(DC):
                        mm = pe.transpose(bank[1][:, k * P:(k + 1) * P], mid[1 - par][:, k * P:(k + 1) * P], ident)
                    mm.then_inc(s_mT, 1)
                if inside(t - 2, 0, NT0):
                    ey = pe.value_load(tex_i[0:1, bass.ds(t - 2, 1)], min_val=0, max_val=E0 - 1)
                    pe.wait_ge(s_hl, t - 1)
                    if inside(t - 4, 0, NT0):
                        pe.wait_ge(s_y, t - 3)
                    n = 0
                    for a, w in ((hl, wh), (hh, wl), (hh, wh)):
                        for k in range(DC):
                            mm = pe.matmul(bank[4 + par][:, :], a[par][:, k, :], w[:, bass.ds(ey * DC + k, 1), :],
                                           start=(n == 0), stop=(n == 3 * DC - 1))
                            n += 1
                    mm.then_inc(s_down, 1)

            x_turn(0, 0)
            for t in range(0, 4):
                step(t, t % 2)
            with pe.Fori(4, 4 + 2 * ((NT0 - 1 - 4) // 2), 2) as t:
                step(t, 0)
                step(t + 1, 1)
            for t in range(4 + 2 * ((NT0 - 1 - 4) // 2), NT0 + 2):
                step(t, t % 2)

            for n in range(16):
                if n % 2 == 0:
                    pe.wait_ge(s_wdn[n // 2 % 4], 16 * (n // 8 + 1))
                wait(pe, s_w16c, n - 1)
                for i in range(4):
                    mm = pe.matmul(bank[6 + n % 2][:, i * P:(i + 1) * P], wdn_at[n // 2 % 4][:, 4 * (n % 2) + i, :],
                                   cst[:, C_H16:C_H16 + P], start=True, stop=True)
                mm.then_inc(s_w16, 1)

            for b in range(NB):
                pe.wait_ge(s_xnb, 4 * b + 4)
                for c in range(DC):
                    n = b * DC + c
                    wait(pe, s_bTl, n - 3)
                    for i in range(4):
                        mm = pe.transpose(bank[n % 4][:, i * P:(i + 1) * P], xnb[:, i, c * P:(c + 1) * P], ident)
                    mm.then_inc(s_bT, 1)

            def prep_a(j, m):
                pe.wait_ge(s_wn, 16 * (2 * j + m + 1))
                for i in range(2):
                    if m == 0:
                        wait(pe, s_wdt, 2 * j - 1 + i)
                    else:
                        pe.wait_ge(s_gwl, 4 * j + 1 + i)
                    for h in range(4):
                        mm = pe.matmul(bank[6 + i][:, h * P:(h + 1) * P], wn[:, 4 * i + h, :], cst[:, C_H4:C_H4 + P],
                                       start=True, stop=True)
                    mm.then_inc(s_pa, 1)

            def prep_b(j, m):
                pe.wait_ge(s_t1, 4 * j + 2 * m + 2)
                for i in range(2):
                    pe.matmul(bank[6 + i][:, :], Hr[:, :], wt1l[:, 2 * i:2 * i + 2, :].rearrange("p c f -> p (c f)"),
                              start=True, stop=False)
                    pe.matmul(bank[6 + i][:, :], Hr[:, :], wt1h[:, 2 * i:2 * i + 2, :].rearrange("p c f -> p (c f)"),
                              start=False, stop=True).then_inc(s_pb, 1)

            def prep_w(j):
                for f in range(2):
                    pe.wait_ge(s_gwl, 4 * j + 3 + f)
                    pe.matmul(bank[6 + f][:, :], cst[:, C_H:C_H + P],
                              wd16[:, bass.ds(2 * j + f, 1), :].rearrange("p a d -> p (a d)"), start=True, stop=True)\
                        .then_inc(s_pw, 1)

            def gate_up(j, b, slot):
                pe.wait_ge(s_gwl, 4 * j + 4)
                for f in range(2):
                    wait(pe, s_bh, 8 * j + 2 * b + f - 1)
                    for m in range(2):
                        n = 0
                        for w, a in ((gwl, xTh), (gwh, xTl), (gwh, xTh)):
                            for c in range(DC):
                                mm = pe.matmul(bank[2 * f + m][:, :], w[slot][:, m, c, f * P:(f + 1) * P], a[:, b, c, :],
                                               start=(n == 0), stop=(n == 3 * DC - 1))
                                n += 1
                    mm.then_inc(s_gu, 1)

            def down(j, b):
                pe.wait_ge(s_bhl, 8 * j + 2 * b + 2)
                pe.wait_ge(s_wdl, 2 * j + 2)
                for i in range(4):
                    wait(pe, s_acc, 16 * j + 4 * b + i - 1)
                    n = 0
                    for a, w in ((bhl, wdh), (bhh, wdl), (bhh, wdh)):
                        for f in range(2):
                            mm = pe.matmul(bank[4 + i % 2][:, :], a[b % 2][:, f, i * P:(i + 1) * P], w[:, f, :],
                                           start=(n == 0), stop=(n == 5))
                            n += 1
                    mm.then_inc(s_bd, 1)

            def chunk(j, slot, first, more):
                gate_up(j, 0, slot)
                if not first:
                    down(j - 1, 3)
                if more:
                    prep_a(j + 1, 0)
                gate_up(j, 1, slot)
                down(j, 0)
                if more:
                    prep_b(j + 1, 0)
                    prep_a(j + 1, 1)
                gate_up(j, 2, slot)
                down(j, 1)
                if more:
                    prep_b(j + 1, 1)
                gate_up(j, 3, slot)
                down(j, 2)
                if more:
                    prep_w(j + 1)

            pe.wait_ge(s_hr, 1)
            prep_a(0, 0)
            prep_b(0, 0)
            prep_a(0, 1)
            prep_b(0, 1)
            prep_w(0)
            chunk(0, 0, True, True)
            with pe.Fori(1, NJ - 2, 2) as j:
                chunk(j, 1, False, True)
                chunk(j + 1, 0, False, True)
            chunk(NJ - 1, 1, False, False)
            down(NJ - 1, 3)

            def c_keys(n):
                pe.wait_ge(s_cxn, n // DC * 4 + 4)
                wait(pe, s_cf, n)
                for i in range(4):
                    mm = pe.transpose(bank[5][:, i * P:(i + 1) * P], xnc[:, i, n % DC * P:(n % DC + 1) * P], ident)
                mm.then_inc(s_ck, 1)

            def c_values(n):
                pe.wait_ge(s_vn, 16 * (n // DC + 1))
                wait(pe, s_cn, n)
                for i in range(4):
                    mm = pe.transpose(bank[6][:, i * P:(i + 1) * P], vnat[:, i, n % DC * P:(n % DC + 1) * P], ident)
                mm.then_inc(s_cv, 1)

            def c_back(n):
                pe.wait_ge(s_cy, n + 1)
                wait(pe, s_co, n)
                for i in range(4):
                    mm = pe.transpose(bank[7][:, i * P:(i + 1) * P], cy[n % 2][:, i * P:(i + 1) * P], ident)
                mm.then_inc(s_cr, 1)

            def d_x(t, par, shared):
                if shared:
                    pe.wait_ge(s_dxn, t + 1)
                else:
                    pe.wait_ge(s_dxs[par], ((t - TT) // 2 + 1) * 16 if isinstance(t, int) else (t - TT - par) * 8 + 16)
                wait(pe, s_dxl, t)
                for k in range(DC):
                    mm = pe.transpose(bank[0][:, k * P:(k + 1) * P], xsd[par][:, k * P:(k + 1) * P], ident)
                mm.then_inc(s_dxT, 1)

            def d_up(t, par, shared):
                slot = 0
                if not shared:
                    e = pe.value_load(tex1_i[0:1, bass.ds(t - TT, 1)], min_val=0, max_val=E1 - 1)
                    pe.wait_ge(s_w13, e * 2 + 4)
                    slot = (e + 1) % 2
                else:
                    pe.wait_ge(s_w13, 2)
                    pe.wait_ge(s_gwlow, 1)
                pe.wait_ge(s_dxl, t + 1)
                wait(pe, s_dmid, t)
                for o, at, step, width in ((2, W_1, G_W, G_W if shared and t < HELD else HID), (3, W_3, HID, HID)):
                    n = 0
                    for a, w in ((dxl, Wh), (dxh, Wl), (dxh, Wh)):
                        for k in range(DC):
                            mm = pe.matmul(bank[o][:, 0:width], a[x_buf(t, par)][:, k, :],
                                           w[:, bass.ds(slot, 1), at + k * step:at + k * step + width].rearrange("p a n -> p (a n)"),
                                           start=(n == 0), stop=(n == 3 * DC - 1))
                            n += 1
                mm.then_inc(s_dup, 1)

            def d_router(t, par):
                pe.wait_ge(s_dxl, t + 1)
                if t == HELD:
                    pe.wait_ge(s_cf, NU)
                n, i = 0, (t - HELD) * E1
                for a, w in ((dxl, Wh), (dxh, Wl), (dxh, Wh)):
                    for k in range(DC):
                        at = W_1 + k * G_W + HID
                        mm = pe.matmul(bank[5][:, i:i + E1], a[x_buf(t, par)][:, k, :], w[:, 0, at:at + E1],
                                       start=(n == 0), stop=(n == 3 * DC - 1))
                        n += 1
                mm.then_inc(s_lp, 1)

            def d_mid(t, par):
                pe.wait_ge(s_dmid, t + 1)
                wait(pe, s_dhl, t)
                for k in range(HC):
                    mm = pe.transpose(bank[1][0:HP, k * P:(k + 1) * P], dmid[par][:, k * HP:(k + 1) * HP], ident)
                mm.then_inc(s_dmT, 1)

            def d_down(t, par, shared):
                slot = 0
                if not shared:
                    e = pe.value_load(tex1_i[0:1, bass.ds(t - TT, 1)], min_val=0, max_val=E1 - 1)
                    pe.wait_ge(s_w2, e + 2)
                    slot = (e + 1) % 2
                else:
                    pe.wait_ge(s_w2, 1)
                pe.wait_ge(s_dhl, t + 1)
                wait(pe, s_dy, t)
                n = 0
                for a, w in ((dhl, Wh), (dhh, Wl), (dhh, Wh)):
                    for k in range(HC):
                        mm = pe.matmul(bank[4][:, :], a[par][:, k, :],
                                       w[0:HP, bass.ds(slot, 1), W_2 + k * D:W_2 + (k + 1) * D].rearrange("p a n -> p (a n)"),
                                       start=(n == 0), stop=(n == 3 * HC - 1))
                        n += 1
                mm.then_inc(s_dd, 1)

            pe.wait_ge(s_acc, 16 * NJ)
            c_keys(0)
            for n in range(NU + 1):
                if n + 1 < NU:
                    c_keys(n + 1)
                t = n - 5
                if t >= 0 and t % 4 != 3:
                    d_x(t + 1, (t + 1) % 2, True)
                if 1 <= n <= NU:
                    c_back(n - 1)
                if n < NU:
                    c_values(n)
                if t >= 0:
                    if t >= 1:
                        d_mid(t - 1, (t - 1) % 2)
                    d_up(t, t % 2, True)
                    if t >= 2:
                        d_down(t - 2, t % 2, True)
                if t >= -1 and t % 4 == 3:
                    d_x(t + 1, (t + 1) % 2, True)
            d_x(HELD + 1, 1, True)
            d_mid(HELD - 1, 1)
            d_router(HELD, 0)
            d_x(HELD + 2, 0, True)
            d_down(HELD - 2, 0, True)
            d_router(HELD + 1, 1)
            d_x(HELD + 3, 1, True)
            d_router(HELD + 2, 0)
            d_router(HELD + 3, 1)
            d_up(HELD, 0, True)
            d_down(HELD - 1, 1, True)
            pe.wait_ge(s_mask1, 1)
            w = (TT + 1) * E1
            pe.matmul(bank[5][:, 0:w], tri, mask1[:, :, :].rearrange("p i e -> p (i e)"), start=True, stop=False)
            for j in range(TT):
                pe.matmul(bank[5][:, (j + 1) * E1:w].rearrange("p (i e) -> p i e", e=E1), ones,
                          mask1[:, j:j + 1, :].broadcast_to([P, TT - j, E1]), start=False, stop=False, skip_group_check=True)
            pe.matmul(bank[5][:, 0:w].rearrange("p (i e) -> p i e", e=E1), ones,
                      mask1[:, TT:TT + 1, :].broadcast_to([P, TT + 1, E1]), start=False, stop=True).then_inc(s_rank1, 1)
            d_mid(HELD, 0)
            for t in range(HELD + 1, TT):
                d_up(t, t % 2, True)
                d_down(t - 1, (t - 1) % 2, True)
                d_mid(t, t % 2)
            d_down(TT - 1, 1, True)
            pe.wait_ge(s_slot1, 1)
            d_x(TT, 0, False)
            d_x(TT + 1, 1, False)
            d_up(TT, 0, False)
            d_x(TT + 2, 0, False)
            d_up(TT + 1, 1, False)
            d_mid(TT, 0)
            with pe.Fori(TT + 2, TT + NT1 - 2, 2) as t:
                for i in range(2):
                    d_x(t + i + 1, 1 - i, False)
                    d_up(t + i, i, False)
                    d_mid(t + i - 1, 1 - i)
                    d_down(t + i - 2, i, False)
            T = TT + NT1 - 1
            d_up(T, T % 2, False)
            d_mid(T - 1, (T - 1) % 2)
            d_down(T - 2, T % 2, False)
            d_mid(T, T % 2)
            d_down(T - 1, (T - 1) % 2, False)
            d_down(T, T % 2, False)

        @block.vector
        def _(dve):
            rt = [0]

            def chain(ins):
                rt[0] += 1
                ins.then_inc(s_rt, 1)
                dve.wait_ge(s_rt, rt[0])

            dve.memset(mask[:, :, :], 0.0)
            dve.wait_ge(s_cst, 32)
            for e in range(E0 + 1):
                last = dve.tensor_scalar(ge[:, 0:TT, e], tok_sb[:, :], float(e * (VOCAB // E0)) if 0 < e < E0 else (-3.0e9 if e == 0 else 3.0e9),
                                         None, ALU.is_ge)
            last.then_inc(s_gate, 1)
            dve.wait_ge(s_gate, 2)
            chain(dve.tensor_tensor(mask[:, 0:TT, :], ge[:, 0:TT, 0:E0], ge[:, 0:TT, 1:E0 + 1], ALU.subtract))
            for q in range(4):
                dve.wait_ge(s_x[q], 16)
                for i in range(4 * q, 4 * q + 4):
                    last = dve.bn_stats(stats[:, i, :], xres[:, i, :])
                chain(last)
                for i in range(4 * q, 4 * q + 4):
                    last = dve.bn_aggr(mv[:, i, :], stats[:, i, :])
                chain(last)
                dve.tensor_scalar(vare[:, 4 * q:4 * q + 4], mv[:, 4 * q:4 * q + 4, 1], EPS, None, ALU.add).then_inc(s_var, 1)
            dve.wait_ge(s_rank, 1)
            chain(dve.tensor_copy(base[:, :, :].rearrange("p i e -> p (i e)"), bank[5][:, 0:(TT + 1) * E0]))
            chain(dve.tensor_tensor(cmp[:, :, :], base[:, TT, :].unsqueeze(2).broadcast_to([P, E0, TT]),
                                    cst[:, C_THR:C_THR + TT].unsqueeze(1).broadcast_to([P, E0, TT]), ALU.is_gt))
            chain(dve.tensor_reduce(ntile[:, :], cmp[:, :, :], AX.X, ALU.add))
            chain(dve.tensor_tensor_scan(tend[:, :], ones[:, 0:E0], ntile[:, :], 0.0, ALU.mult, ALU.add))
            chain(dve.tensor_scalar(tlast[:, :], tend[:, :], -1.0, 0.0, ALU.add, ALU.max))
            chain(dve.tensor_copy(tlast_i[:, :], tlast[:, :]))
            chain(dve.tensor_tensor(tstart[:, :], tend[:, :], ntile[:, :], ALU.subtract))
            chain(dve.tensor_scalar(tstart[:, :], tstart[:, :], float(P), None, ALU.mult))
            chain(dve.tensor_tensor(base[:, 0:TT, :], base[:, 0:TT, :], tstart[:, :].unsqueeze(1).broadcast_to([P, TT, E0]), ALU.add))
            chain(dve.tensor_tensor(base[:, 0:TT, :], base[:, 0:TT, :], mask[:, 0:TT, :], ALU.mult))
            chain(dve.tensor_reduce(slot_f[:, :], base[:, 0:TT, :], AX.X, ALU.add))
            chain(dve.tensor_copy(slot[:, :], slot_f[:, :]))
            chain(dve.tensor_tensor(tcmp[:, :, :], cst[:, C_IOTA:C_IOTA + 48].unsqueeze(2).broadcast_to([P, 48, E0 - 1]),
                                    tend[:, 0:E0 - 1].unsqueeze(1).broadcast_to([P, 48, E0 - 1]), ALU.is_ge))
            chain(dve.tensor_reduce(tex[:, :], tcmp[:, :, :], AX.X, ALU.add))
            dve.tensor_copy(tex_i[:, :], tex[:, :]).then_inc(s_slot, 1)
            for i in range(TT):
                if i % 4 == 0:
                    dve.wait_ge(s_rstd, i // 4 + 1)
                wait(dve, s_scat[i % 4], 16 * (i // 4))
                dve.tensor_scalar(xn[:, i % 4, :], xres[:, i, :], mv[:, i, 0:1], rstd[:, i:i + 1],
                                  ALU.subtract, ALU.mult).then_inc(s_xn, 1)
                dve.wait_ge(s_wh, i + 1)
                dve.tensor_tensor(wl[:, i, :], bank[6 + i % 2][:, :], f32(wh[:, i, :]), ALU.subtract).then_inc(s_wl, 1)

            def x_low(t, par):
                dve.wait_ge(s_xh, t + 1)
                dve.tensor_tensor(xl[par][:, :, :].rearrange("p k n -> p (k n)"), bank[0][:, :],
                                  f32(xh[par][:, :, :]).rearrange("p k n -> p (k n)"), ALU.subtract).then_inc(s_xl, 1)

            def step(t, par):
                if inside(t + 1, 0, NT0):
                    x_low(t + 1, 1 - par)
                if inside(t, 0, NT0):
                    dve.wait_ge(s_sg, t + 1)
                    if inside(t - 2, 0, NT0):
                        dve.wait_ge(s_mT, t - 1)
                    dve.tensor_tensor(mid[par][:, :], bank[2 + par][:, :], sg[par][:, :], ALU.mult).then_inc(s_mid, 1)
                if inside(t - 1, 0, NT0):
                    dve.wait_ge(s_hh, t)
                    dve.tensor_tensor(hl[1 - par][:, :, :].rearrange("p k n -> p (k n)"), bank[1][:, :],
                                      f32(hh[1 - par][:, :, :]).rearrange("p k n -> p (k n)"), ALU.subtract).then_inc(s_hl, 1)

            x_low(0, 0)
            for t in range(0, 4):
                step(t, t % 2)
            with dve.Fori(4, 4 + 2 * ((NT0 - 1 - 4) // 2), 2) as t:
                step(t, 0)
                step(t + 1, 1)
            for t in range(4 + 2 * ((NT0 - 1 - 4) // 2), NT0 + 2):
                step(t, t % 2)
            for q in range(NB):
                for i in range(4 * q, 4 * q + 4):
                    dve.wait_ge(s_yg[i % 4], 16 * (i // 4 + 1))
                    dve.scalar_tensor_tensor(out=xres[:, i, :], in0=yg[i % 4], scalar=gates[:, 0:1], in1=xres[:, i, :],
                                             op0=ALU.mult, op1=ALU.add).then_inc(s_x1, 1)
                    dve.wait_ge(s_x1, i + 1)
                    last = dve.bn_stats(stats[:, i, :], xres[:, i, :])
                chain(last)
                for i in range(4 * q, 4 * q + 4):
                    last = dve.bn_aggr(mv[:, i, :], stats[:, i, :])
                chain(last)
                dve.tensor_scalar(vare[:, 4 * q:4 * q + 4], mv[:, 4 * q:4 * q + 4, 1], EPS, None, ALU.add).then_inc(s_var, 1)

            for b in range(NB):
                dve.wait_ge(s_rstd, 4 + b + 1)
                wait(dve, s_bT, 4 * b)
                for i in range(4):
                    t = 4 * b + i
                    dve.tensor_scalar(xnb[:, i, :], xres[:, t, :], mv[:, t, 0:1], rstd[:, t:t + 1],
                                      ALU.subtract, ALU.mult).then_inc(s_xnb, 1)
                for c in range(DC):
                    n = b * DC + c
                    dve.wait_ge(s_bTh, n + 1)
                    dve.scalar_tensor_tensor(out=xTl[:, b, c, :], in0=bank[n % 4][:, :], scalar=tab[:, T_SUG + c:T_SUG + c + 1],
                                             in1=f32(xTh[:, b, c, :]), op0=ALU.mult, op1=ALU.subtract).then_inc(s_bTl, 1)

            def prep_a(j, m):
                wait(dve, s_pb, 4 * j + 2 * m)
                if m == 0:
                    wait(dve, s_wdl, 2 * j)
                for i in range(2):
                    dve.wait_ge(s_t1h, 4 * j + 2 * m + i + 1)
                    dve.tensor_tensor(wt1l[:, :, i * P:(i + 1) * P], bank[6 + i][:, :].rearrange("p (n c) -> p c n", c=DC),
                                      f32(wt1h[:, :, i * P:(i + 1) * P]), ALU.subtract).then_inc(s_t1, 1)

            def prep_b(j, m, slot):
                for i in range(2):
                    dve.wait_ge(s_gwh, 4 * j + 2 * m + i + 1)
                    dve.tensor_tensor(gwl[slot][:, m, 2 * i:2 * i + 2, :].rearrange("p c f -> p (c f)"), bank[6 + i][:, :],
                                      f32(gwh[slot][:, m, 2 * i:2 * i + 2, :]).rearrange("p c f -> p (c f)"), ALU.subtract)\
                       .then_inc(s_gwl, 1)

            def prep_w(j, slot):
                dve.tensor_scalar(gsc[slot][:, :], tab[:, bass.ds(T_WGT + 2 * j, 2)], 1.0, None, ALU.mult).then_inc(s_gsc, 1)
                wait(dve, s_wdh, 2 * j)
                wait(dve, s_wdl, 2 * j)
                for f in range(2):
                    dve.wait_ge(s_pw, 2 * j + f + 1)
                    dve.scalar_tensor_tensor(out=wdt[:, f, :], in0=bank[6 + f][:, :], scalar=tab[:, bass.ds(T_SDP + 2 * j + f, 1)],
                                             in1=wrow[:, :], op0=ALU.mult, op1=ALU.mult).then_inc(s_wdt, 1)

            def add_down(j, b, i):
                dve.wait_ge(s_bd, 16 * j + 4 * b + i + 1)
                wait(dve, s_acc, 16 * j + 4 * b + i - 8)
                dve.tensor_tensor(xres[:, 4 * b + i, :], bank[4 + i % 2][:, :], xres[:, 4 * b + i, :], ALU.add)\
                   .then_inc(s_acc, 1)

            def hidden(j, b, before):
                for f in range(2):
                    k = 8 * j + 2 * b + f
                    dve.wait_ge(s_bs, k + 1)
                    dve.scalar_tensor_tensor(out=bs[:, f, :], in0=bank[2 * f + 1][:, :], scalar=tab[:, bass.ds(T_WUP + 2 * j + f, 1)],
                                             in1=bs[:, f, :], op0=ALU.mult, op1=ALU.mult).then_inc(s_bh, 1)
                    if f == 1 and before is not None:
                        add_down(*before, 0)
                    dve.wait_ge(s_bhh, k + 1)
                    dve.tensor_tensor(bhl[b % 2][:, f, :], bs[:, f, :], f32(bhh[b % 2][:, f, :]), ALU.subtract)\
                       .then_inc(s_bhl, 1)
                if before is not None:
                    for i in range(1, 4):
                        add_down(*before, i)

            def low_down(j):
                for f in range(2):
                    dve.wait_ge(s_wdh, 2 * j + f + 1)
                    dve.tensor_tensor(wdl[:, f, :], wdt[:, f, :], f32(wdh[:, f, :]), ALU.subtract).then_inc(s_wdl, 1)

            def chunk(j, slot, first, more):
                hidden(j, 0, None if first else (j - 1, 3))
                low_down(j)
                if more:
                    prep_a(j + 1, 0)
                hidden(j, 1, (j, 0))
                if more:
                    prep_b(j + 1, 0, 1 - slot)
                    prep_a(j + 1, 1)
                hidden(j, 2, (j, 1))
                if more:
                    prep_b(j + 1, 1, 1 - slot)
                hidden(j, 3, (j, 2))
                if more:
                    prep_w(j + 1, 1 - slot)

            dve.wait_ge(s_tabc, 4)
            prep_a(0, 0)
            prep_b(0, 0, 0)
            prep_a(0, 1)
            prep_b(0, 1, 0)
            prep_w(0, 0)
            chunk(0, 0, True, True)
            with dve.Fori(1, NJ - 2, 2) as j:
                chunk(j, 1, False, True)
                chunk(j + 1, 0, False, True)
            chunk(NJ - 1, 1, False, False)
            for i in range(4):
                add_down(NJ - 1, 3, i)

            def norm_stats(b, done):
                for i in range(4 * b, 4 * b + 4):
                    last = dve.bn_stats(stats[:, i, :], xres[:, i, :])
                chain(last)
                for i in range(4 * b, 4 * b + 4):
                    last = dve.bn_aggr(mv[:, i, :], stats[:, i, :])
                chain(last)
                dve.tensor_scalar(vare[:, 4 * b:4 * b + 4], mv[:, 4 * b:4 * b + 4, 1], EPS, None, ALU.add).then_inc(s_var, 1)
                dve.wait_ge(s_rstd, done)

            def norm(out_ap, t, scale):
                return dve.tensor_scalar(out_ap, xres[:, t, :], mv[:, t, 0:1], scale, ALU.subtract, ALU.mult)

            def c_norm(b):
                norm_stats(b, 9 + (0, 1, 3, 5)[b])
                wait(dve, s_ck, 4 * b)
                for i in range(4):
                    norm(xnc[:, i, :], 4 * b + i, rstd[:, 4 * b + i:4 * b + i + 1]).then_inc(s_cxn, 1)

            def front(n):
                decay = tab[:, T_DEC + n % DC:T_DEC + n % DC + 1]
                dve.wait_ge(s_ck, n + 1)
                chain(dve.tensor_tensor_scan(co[:, 1:513], decay.broadcast_to([P, 512]), bank[5][:, :], LOWEST, ALU.add, ALU.max))
                wait(dve, s_cl, 3 * n)
                dve.scalar_tensor_tensor(out=cd[:, :], in0=bank[5][:, :], scalar=decay, in1=co[:, 0:512],
                                         op0=ALU.subtract, op1=ALU.subtract).then_inc(s_cf, 1)

            def back(n):
                e = ce[n % 2]
                dve.wait_ge(s_ce, 3 * n + 3)
                dve.wait_ge(s_cv, n + 1)
                chain(dve.tensor_tensor(cev[:, :], bank[6][:, :], e[:, 1, :], ALU.mult))
                wait(dve, s_cna, n)
                dve.tensor_tensor_scan(cp[:, 1:513], e[:, 0, :], cev[:, :], 0.0, ALU.mult, ALU.add)
                chain(dve.tensor_tensor_scan(cq[:, 1:513], e[:, 0, :], e[:, 1, :], 0.0, ALU.mult, ALU.add))
                wait(dve, s_cy, n)
                dve.tensor_tensor(cnum[:, :], bank[6][:, :], e[:, 2, :], ALU.mult).then_inc(s_cn, 1)
                chain(dve.tensor_tensor(e[:, 2, :], e[:, 2, :], cq[:, 0:512], ALU.add))
                dve.reciprocal(e[:, 2, :], e[:, 2, :]).then_inc(s_cd, 1)

            def add_out(n):
                b, c = divmod(n, DC)
                dve.wait_ge(s_cr, n + 1)
                x_part = xres[:, 4 * b:4 * b + 4, c * P:(c + 1) * P]
                dve.scalar_tensor_tensor(out=x_part, in0=bank[7][:, :].rearrange("p (i c) -> p i c", i=4), scalar=gates[:, 1:2],
                                         in1=x_part, op0=ALU.mult, op1=ALU.add).then_inc(s_co, 1)

            def d_norm(b):
                dve.wait_ge(s_co, 4 * b + 4)
                norm_stats(b, 9 + (2, 4, 6, 7)[b])

            def d_xn(t, par):
                wait(dve, s_dxT, t - 1)
                norm(xsd[par][:, :], t, rstd[:, t:t + 1]).then_inc(s_dxn, 1)

            def d_x(t, par):
                dve.wait_ge(s_dxh, t + 1)
                dve.tensor_tensor(dxl[x_buf(t, par)][:, :, :].rearrange("p k n -> p (k n)"), bank[0][:, :],
                                  f32(dxh[x_buf(t, par)][:, :, :]).rearrange("p k n -> p (k n)"), ALU.subtract).then_inc(s_dxl, 1)

            def d_mul(t, par, shared):
                dve.wait_ge(s_dsg, t + 1)
                wait(dve, s_dmT, t - 1)
                if shared and t < HELD:
                    dve.tensor_copy(lg[:, t, :], bank[2][:, HID:G_W]).then_inc(s_lg, 1)
                dve.tensor_tensor(dmid[par][:, :], bank[3][:, 0:HID], dsg[:, :], ALU.mult).then_inc(s_dmid, 1)

            def d_hid(t, par):
                dve.wait_ge(s_dhh, t + 1)
                dve.tensor_tensor(dhl[par][:, :, :].rearrange("p k n -> p (k n)"), bank[1][0:HP, :],
                                  f32(dhh[par][:, :, :]).rearrange("p k n -> p (k n)"), ALU.subtract).then_inc(s_dhl, 1)

            dve.wait_ge(s_acc, 16 * NJ)
            dve.memset(co[:, 0:1], LOWEST)
            dve.memset(cp[:, 0:1], 0.0)
            dve.memset(cq[:, 0:1], 0.0)
            dve.memset(mask1[:, :, :], 0.0)
            chain(dve.tensor_tensor(wub[:, :], tab[:, T_DEC:T_BON], tab[:, T_BON:T_ROWS], ALU.add))
            chain(dve.tensor_scalar(wlim[:, :], wub[:, :], -1.0, BIG, ALU.mult, ALU.add))
            c_norm(0)
            front(0)
            for n in range(NU + 1):
                t = n - 5
                if t >= 0 and t % 4 != 3:
                    d_xn(t + 1, (t + 1) % 2)
                if n + 1 < NU:
                    front(n + 1)
                if t >= 0 and t % 4 != 3:
                    d_x(t + 1, (t + 1) % 2)
                if t >= 1:
                    d_hid(t - 1, (t - 1) % 2)
                if 1 <= n <= NU:
                    add_out(n - 1)
                if n < NU:
                    back(n)
                if t >= 0:
                    d_mul(t, t % 2, True)
                if n % 4 == 2 and n + 2 < NU:
                    c_norm(n // 4 + 1)
                if n % 4 == 0 and 4 <= n <= NU:
                    d_norm(n // 4 - 1)
                    d_xn(t + 1, (t + 1) % 2)
                    d_x(t + 1, (t + 1) % 2)
            d_xn(HELD + 1, 1)
            d_x(HELD + 1, 1)
            d_hid(HELD - 1, 1)
            for t in (HELD + 2, HELD + 3):
                d_xn(t, t % 2)
                d_x(t, t % 2)

            def per_token(ap):
                return ap.unsqueeze(2).broadcast_to([P, TT, E1])

            dve.wait_ge(s_lp, TT - HELD)
            dve.tensor_copy(lg[:, HELD:TT, :].rearrange("p i e -> p (i e)"), bank[5][:, 0:(TT - HELD) * E1]).then_inc(s_lg, 1)
            dve.wait_ge(s_lg, HELD + 1)
            dve.wait_ge(s_b8, 16)
            chain(dve.tensor_reduce(red[:, :], lg[:, :, :], AX.X, ALU.max))
            dve.tensor_tensor(lg[:, :, :], lg[:, :, :], per_token(red[:, :]), ALU.subtract).then_inc(s_lg, 1)
            dve.wait_ge(s_ex8, 1)
            chain(dve.tensor_reduce(red[:, :], prob[:, :, :], AX.X, ALU.add))
            chain(dve.reciprocal(red[:, :], red[:, :]))
            chain(dve.tensor_tensor(prob[:, :, :], prob[:, :, :], per_token(red[:, :]), ALU.mult))
            chain(dve.tensor_tensor(pb[:, :, :], prob[:, :, :], bias8[:, :].unsqueeze(1).broadcast_to([P, TT, E1]), ALU.add))
            for t in range(TT):
                last = dve.max(best[:, t, :], pb[:, t, :])
            chain(last)
            for t in range(TT):
                last = dve.max_index(bix[:, t, :], best[:, t, :], pb[:, t, :])
            chain(last)
            chain(dve.tensor_copy(bixf[:, :, :], bix[:, :, :]))
            count = cst[:, C_IOTA:C_IOTA + E1].unsqueeze(1).broadcast_to([P, TT, E1])
            for k in range(2):
                last = dve.tensor_tensor(sel[k][:, :, :], per_token(bixf[:, :, k]), count, ALU.is_equal)
            chain(last)
            dve.tensor_tensor(mask1[:, 0:TT, :], sel[0][:, :, :], sel[1][:, :, :], ALU.add).then_inc(s_mask1, 1)
            d_mul(HELD, 0, True)
            for k in range(2):
                chain(dve.tensor_tensor(tmp8[:, :, :], sel[k][:, :, :], prob[:, :, :], ALU.mult))
                chain(dve.tensor_reduce(rsc[:, k, :], tmp8[:, :, :], AX.X, ALU.add))
                chain(dve.tensor_tensor(rsc[:, k, :], rsc[:, k, :], rstd[:, :], ALU.mult))
            dve.wait_ge(s_rank1, 1)
            chain(dve.tensor_copy(base1[:, :, :].rearrange("p i e -> p (i e)"), bank[5][:, 0:(TT + 1) * E1]))
            chain(dve.tensor_tensor(cmp1[:, :, :], base1[:, TT, :].unsqueeze(2).broadcast_to([P, E1, TT]),
                                    cst[:, C_THR:C_THR + TT].unsqueeze(1).broadcast_to([P, E1, TT]), ALU.is_gt))
            chain(dve.tensor_reduce(nt1[:, :], cmp1[:, :, :], AX.X, ALU.add))
            chain(dve.tensor_scalar(nt1[:, :], nt1[:, :], 1.0, None, ALU.max))
            chain(dve.tensor_tensor_scan(tend1[:, :], ones[:, 0:E1], nt1[:, :], 0.0, ALU.mult, ALU.add))
            chain(dve.tensor_tensor(tst1[:, :], tend1[:, :], nt1[:, :], ALU.subtract))
            chain(dve.tensor_scalar(tst1[:, :], tst1[:, :], float(P), None, ALU.mult))
            chain(dve.tensor_tensor(base1[:, 0:TT, :], base1[:, 0:TT, :], tst1[:, :].unsqueeze(1).broadcast_to([P, TT, E1]), ALU.add))
            for k in range(2):
                chain(dve.tensor_tensor(tmp8[:, :, :], base1[:, 0:TT, :], sel[k][:, :, :], ALU.mult))
                chain(dve.tensor_reduce(slf[:, k, :], tmp8[:, :, :], AX.X, ALU.add))
            chain(dve.tensor_copy(slw[:, :, :], slf[:, :, :]))
            chain(dve.tensor_scalar(slf[:, :, :], slf[:, :, :], float(TOK), None, ALU.add))
            chain(dve.tensor_copy(slr[:, :, :], slf[:, :, :]))
            chain(dve.tensor_copy(tend1_i[:, :], tend1[:, :]))
            chain(dve.tensor_tensor(tcmp1[:, :, :], cst[:, C_IOTA:C_IOTA + 48].unsqueeze(2).broadcast_to([P, 48, E1 - 1]),
                                    tend1[:, 0:E1 - 1].unsqueeze(1).broadcast_to([P, 48, E1 - 1]), ALU.is_ge))
            chain(dve.tensor_reduce(tex1[:, :], tcmp1[:, :, :], AX.X, ALU.add))
            dve.tensor_copy(tex1_i[:, :], tex1[:, :]).then_inc(s_slot1, 1)
            for q in range(4):
                d_hid(HELD + q, q % 2)
                if q < 3:
                    d_mul(HELD + q + 1, (q + 1) % 2, True)
                for t in range(4 * q, 4 * q + 4):
                    for k in range(2):
                        n = 2 * t + k
                        wait(dve, s_rsc[n % 4], 16 * (n // 4))
                        norm(row[:, n % 4, :], t, rsc[:, k, t:t + 1]).then_inc(s_row, 1)
            d_x(TT, 0)
            d_x(TT + 1, 1)
            d_mul(TT, 0, False)
            d_x(TT + 2, 0)
            d_mul(TT + 1, 1, False)
            d_hid(TT, 0)

            def pair(t):
                for i in range(2):
                    d_x(t + i + 1, 1 - i)
                    d_mul(t + i, i, False)
                    d_hid(t + i - 1, 1 - i)

            xres_flat = xres[:, :, :].rearrange("p t d -> p (t d)")
            dve.sem_inc(s_sha, 2)
            with dve.Fori(TT + 2, TT + 1 + 2 * TT, 2) as t:
                pair(t)
                here = xres_flat[:, bass.ds((t - TT - 2) * (D // 2), D)]
                dve.wait_ge(s_shl, (t - TT) * 8)
                dve.scalar_tensor_tensor(out=here, in0=row[:, 0, :], scalar=gates[:, 3:4], in1=here,
                                         op0=ALU.mult, op1=ALU.add).then_inc(s_sha, 2)
            for t in range(TT + 2 + 2 * TT, TT + NT1 - 2, 2):
                pair(t)
            T = TT + NT1 - 1
            d_mul(T, T % 2, False)
            d_hid(T - 1, (T - 1) % 2)
            d_hid(T, T % 2)
            dve.wait_ge(s_sha, 2 * TT + 2)
            for t in range(TT):
                for k in range(2):
                    dve.wait_ge(s_fin[t % 6][k], 16 * (t // 6 + 1))
                    last = dve.scalar_tensor_tensor(out=xres[:, t, :], in0=fin[:, 2 * (t % 6) + k, :], scalar=gates[:, 3:4],
                                                    in1=xres[:, t, :], op0=ALU.mult, op1=ALU.add)
                    if k < 1:
                        chain(last)
                last.then_inc(s_x4, 1)


def shape_constants():
    import numpy as np
    def had(n):
        h = np.ones((1, 1), np.float32)
        while h.shape[0] < n:
            h = np.block([[h, h], [h, -h]])
        return h
    c = np.zeros((P, C_W), np.float32)
    c[:, C_ID:C_ID + P] = np.eye(P)
    c[:, C_TRI:C_TRI + P] = np.triu(np.ones((P, P)), 1)
    c[:, C_ONES:C_ONES + P] = 1.0
    c[:, C_H:C_H + P] = had(P)
    c[:, C_H4:C_H4 + P] = np.kron(np.eye(32), had(4))
    c[:, C_H16:C_H16 + P] = np.kron(np.eye(8), had(16))
    c[:, C_THR:C_THR + 16] = P * np.arange(16)
    c[:, C_IOTA:C_IOTA + 48] = np.arange(48)
    c[:, C_HALF:C_HALF + 4] = -0.5
    return c


_INS = ['x', 'itok_BxS_13_99985', 'ctx_2048', 'g_xattn', 'g_ffn',
        'L0_ffn_SU_ug', 'L0_ffn_SU_dp', 'L0_ffn_Wscale_ug', 'L0_ffn_Wscale_dp', 'L0_ffn_W_up', 'L0_ffn_W_gate', 'L0_ffn_W_down',
        'L1_xattn_w', 'L1_xattn_u', 'L1_ffn_gate_w', 'L1_ffn_w1', 'L1_ffn_w2', 'L1_ffn_w3',
        'L1_ffn_sw1', 'L1_ffn_sw2', 'L1_ffn_sw3', 'L1_ffn_expert_bias']


def kernel(**inputs):
    import numpy as _np
    import concourse.bacc as _bacc
    from concourse import mybir as _mybir
    from concourse.bass_utils import run_bass_kernel_spmd as _run

    nc = _bacc.Bacc("TRN2", target_bir_lowering=False, num_devices=1)
    arrays, args = {}, []
    for name in _INS:
        a = _np.ascontiguousarray(inputs[name])
        arrays[f"in_{name}"] = a
        args.append(nc.dram_tensor(f"in_{name}", a.shape, _mybir.dt.from_np(a.dtype), kind="ExternalInput").ap())
    arrays["shape_constants"] = shape_constants()
    args.append(nc.dram_tensor("shape_constants", (P, C_W), F32, kind="ExternalInput").ap())
    args.append(nc.dram_tensor("out_0", (4, 512, D), F32, kind="ExternalOutput").ap())
    program(nc, *args)
    r = _run(nc, [arrays], core_ids=[0])
    return r.results[0]["out_0"]
```

```python
import concourse.bass as bass
from concourse import mybir
from contextlib import ExitStack

ALU = mybir.AluOpType
ACT = mybir.ActivationFunctionType
AX = mybir.AxisListType
F32 = mybir.dt.float32
F32R = mybir.dt.float32r
I32 = mybir.dt.int32

P = 128
D = 512
DC = D // P
TOK = 2048
TT = TOK // P
EPS = 1e-5

E0 = 4
VOCAB = 25000
NT0 = TT + E0 - 1

F0 = 2048
FC = F0 // P
FB = 256
NJ = F0 // FB
NB = 4
T_SUG, T_SDP, T_WUP, T_WGT, T_DEC, T_BON, T_ROWS = 0, 4, 20, 36, 52, 56, 60

NU = NB * DC
BIG = 34.0
LOWEST = -1.0e38

E1 = 8
HID = 448
HC = 4
HP = HID // HC
HELD = TT - 4
NT1 = 2 * TT + E1 - 1
G_W = HID + E1
W_1, W_3, W_2, W_W = 0, HC * G_W, HC * (G_W + HID), HC * (G_W + HID + D)

C_ID, C_TRI, C_ONES, C_H, C_H4, C_H16, C_THR, C_IOTA = 0, 128, 256, 384, 512, 640, 768, 784
C_HALF = C_IOTA + 48
C_W = C_HALF + 4




def program(nc, x, tok, ctx, g_xattn, g_ffn, su_ug, su_dp, wscale_ug, wscale_dp, w_up, w_gate, w_down,
            wkv_w, wkv_u, gate_w, w1, w2, w3, sw1, sw2, sw3, expert_bias, consts, out):
    es = ExitStack()
    with es:
        def sb(name, shape, dt=F32, stack=es):
            return stack.enter_context(nc.sbuf_tensor(name, shape, dt))

        def sem(name):
            return es.enter_context(nc.semaphore(name))

        bank = [es.enter_context(nc.psum_tensor(f"bank{i}", [P, 512], F32)) for i in range(8)]
        xs_dram = nc.dram_tensor("xs_sorted", ((NT0 + E0) * P, D), F32).ap()
        xs1_dram = nc.dram_tensor("xs1_sorted", (NT1 * P, D), F32).ap()
        y1_dram = nc.dram_tensor("y1_all", ((TT + NT1) * P, D), F32).ap()
        y_dram = nc.dram_tensor("y_sorted", (NT0 * P, D), F32).ap()

        cst = sb("cst", [P, C_W])
        gates = sb("gates", [P, 4])
        zero = sb("zero", [P, P])
        slot = sb("slot", [P, TT], I32)
        gates_raw = sb("gates_raw", [P, 4])
        tab_in = sb("tab_in", [T_ROWS, P])
        tab = sb("tab", [P, T_ROWS])
        wrow = sb("wrow", [P, D])
        stats = sb("stats", [P, TT, 6])
        mv = sb("mv", [P, TT, 2])
        vare = sb("vare", [P, TT])
        rstd = sb("rstd", [P, TT])
        xres = sb("xres", [P, TT, D])
        sd = ExitStack()
        pace = sb("pace", [P, 32], F32, sd)
        wlim = sb("wlim", [P, DC], F32, sd)
        wub = sb("wub", [P, DC], F32, sd)
        row = sb("row", [P, 4, D], F32, sd)
        s1 = ExitStack()
        xnc = sb("xnc", [P, 4, D], F32, s1)
        vnat = sb("vnat", [P, 4, D], F32, s1)
        co = sb("co", [P, 513], F32, s1)
        cd = sb("cd", [P, 512], F32, s1)
        ce = [sb(f"ce{i}", [P, 3, 512], F32, s1) for i in range(2)]
        cev = sb("cev", [P, 512], F32, s1)
        cp = sb("cp", [P, 513], F32, s1)
        cq = sb("cq", [P, 513], F32, s1)
        cy = [sb(f"cy{i}", [P, 512], F32, s1) for i in range(2)]
        cnum = sb("cnum", [P, 512], F32, s1)
        s1.close()
        s1 = ExitStack()
        fin = sb("fin", [P, 12, D], F32, s1)
        s1.close()
        W = sb("W", [P, 2, 2, W_W], F32R, sd)
        Wh, Wl = W[:, :, 0, :], W[:, :, 1, :]
        xsd = [sb(f"xsd{i}", [P, D], F32, sd) for i in range(2)]
        dxh = [sb(f"dxh{i}", [P, DC, P], F32R, sd) for i in range(4)]
        dxl = [sb(f"dxl{i}", [P, DC, P], F32R, sd) for i in range(4)]
        dsg = sb("dsg", [P, HID], F32, sd)
        dmid = [sb(f"dmid{i}", [P, HID], F32, sd) for i in range(2)]
        dhh = [sb(f"dhh{i}", [HP, HC, P], F32R, sd) for i in range(2)]
        dhl = [sb(f"dhl{i}", [HP, HC, P], F32R, sd) for i in range(2)]
        dys = [sb(f"dys{i}", [P, D], F32, sd) for i in range(2)]
        wst = [sb(f"wst{i}", [P, 2048], F32, sd) for i in range(3)]
        lg = sb("lg", [P, TT, E1], F32, sd)
        prob = sb("prob", [P, TT, E1], F32, sd)
        pb = sb("pb", [P, TT, E1], F32, sd)
        bias8 = sb("bias8", [P, E1], F32, sd)
        best = sb("best", [P, TT, 8], F32, sd)
        bix = sb("bix", [P, TT, 8], mybir.dt.uint32, sd)
        bixf = sb("bixf", [P, TT, 8], F32, sd)
        red = sb("red", [P, TT], F32, sd)
        sel = [sb(f"sel{i}", [P, TT, E1], F32, sd) for i in range(2)]
        tmp8 = sb("tmp8", [P, TT, E1], F32, sd)
        mask1 = sb("mask1", [P, TT + 1, E1], F32, sd)
        base1 = sb("base1", [P, TT + 1, E1], F32, sd)
        cmp1 = sb("cmp1", [P, E1, TT], F32, sd)
        nt1 = sb("nt1", [P, E1], F32, sd)
        tend1 = sb("tend1", [P, E1], F32, sd)
        tst1 = sb("tst1", [P, E1], F32, sd)
        tcmp1 = sb("tcmp1", [P, 48, E1 - 1], F32, sd)
        tex1 = sb("tex1", [P, 48], F32, sd)
        tex1_i = sb("tex1_i", [P, 48], I32, sd)
        tend1_i = sb("tend1_i", [P, E1], I32, sd)
        slf = sb("slf", [P, 2, TT], F32, sd)
        slw = sb("slw", [P, 2, TT], I32, sd)
        slr = sb("slr", [P, 2, TT], I32, sd)
        rsc = sb("rsc", [P, 2, TT], F32, sd)
        sd.close()

        wd16 = sb("wd16", [P, FC, D])

        sa = ExitStack()
        wh = sb("wh", [P, E0 * DC, D], F32R, sa)
        wl = sb("wl", [P, E0 * DC, D], F32R, sa)
        nat = sb("nat", [P, 2, DC, D], F32, sa)
        wdn = sb("wdn", [P, 2, 8, P], F32, sa)
        xn = sb("xn", [P, 4, D], F32, sa)
        tok_sb = sb("tok_sb", [P, TT], I32, sa)
        ge = sb("ge", [P, TT + 1, E0 + 1], F32, sa)
        mask = sb("mask", [P, TT + 1, E0], F32, sa)
        base = sb("base", [P, TT + 1, E0], F32, sa)
        cmp = sb("cmp", [P, E0, TT], F32, sa)
        ntile = sb("ntile", [P, E0], F32, sa)
        tend = sb("tend", [P, E0], F32, sa)
        tstart = sb("tstart", [P, E0], F32, sa)
        tlast = sb("tlast", [P, E0], F32, sa)
        tspare = sb("tspare", [P, E0], F32, sa)
        tlast_i = sb("tlast_i", [P, E0], I32, sa)
        tcmp = sb("tcmp", [P, 48, E0 - 1], F32, sa)
        tex = sb("tex", [P, 48], F32, sa)
        tex_i = sb("tex_i", [P, 48], I32, sa)
        slot_f = sb("slot_f", [P, TT], F32, sa)
        xs = [sb(f"xs{i}", [P, D], F32, sa) for i in range(2)]
        xh = [sb(f"xh{i}", [P, DC, P], F32R, sa) for i in range(2)]
        xl = [sb(f"xl{i}", [P, DC, P], F32R, sa) for i in range(2)]
        sg = [sb(f"sg{i}", [P, D], F32, sa) for i in range(2)]
        mid = [sb(f"mid{i}", [P, D], F32, sa) for i in range(2)]
        hh = [sb(f"hh{i}", [P, DC, P], F32R, sa) for i in range(2)]
        hl = [sb(f"hl{i}", [P, DC, P], F32R, sa) for i in range(2)]
        ysb = [sb(f"ysb{i}", [P, D], F32, sa) for i in range(2)]
        sa.close()

        sbk = ExitStack()
        wn = sb("wn", [P, 8, P], F32, sbk)
        wt1h = sb("wt1h", [P, DC, FB], F32R, sbk)
        gwh = [sb("gwh0", [P, 2, DC, FB], F32R, sbk), None]
        gwl = [sb("gwl0", [P, 2, DC, FB], F32R, sbk), None]
        sx = ExitStack()
        yg = [sb(f"yg{i}", [P, D], F32, sx) for i in range(4)]
        xnb = sb("xnb", [P, 4, D], F32, sx)
        sx.close()
        gwh[1] = sb("gwh1", [P, 2, DC, FB], F32R, sbk)
        gwl[1] = sb("gwl1", [P, 2, DC, FB], F32R, sbk)
        gsc = [sb(f"gsc{i}", [P, 2], F32, sbk) for i in range(2)]
        sx = ExitStack()
        wt1l = sb("wt1l", [P, DC, FB], F32R, sx)
        sx.close()
        wdt = sb("wdt", [P, 2, D], F32, sbk)
        Hr = sb("Hr", [P, P], F32R, sbk)
        wdh = sb("wdh", [P, 2, D], F32R, sbk)
        wdl = sb("wdl", [P, 2, D], F32R, sbk)
        xTh = sb("xTh", [P, NB, DC, 512], F32R, sbk)
        xTl = sb("xTl", [P, NB, DC, 512], F32R, sbk)
        bhh = [sb(f"bhh{i}", [P, 2, 512], F32R, sbk) for i in range(2)]
        bhl = [sb(f"bhl{i}", [P, 2, 512], F32R, sbk) for i in range(2)]
        bs = sb("bs", [P, 2, 512], F32, sbk)
        sbk.close()

        ident = cst[:, C_ID:C_ID + P]
        tri = cst[:, C_TRI:C_TRI + P]
        ones = cst[:, C_ONES:C_ONES + P]

        s_cst = sem("s_cst")
        s_gl = sem("s_gl")
        s_x = [sem(f"s_xin{i}") for i in range(4)]
        s_ctx = [sem(f"s_ctx{i}") for i in range(E0)]
        s_zero = sem("s_zero")
        s_zeroed = sem("s_zeroed")
        s_zlast = sem("s_zlast")
        s_gate = sem("s_gate")
        s_rt = sem("s_rt")
        s_rank = sem("s_rank")
        s_slot = sem("s_slot")
        s_var = sem("s_var")
        s_rstd = sem("s_rstd")
        s_xn = sem("s_xn")
        s_scat = [sem(f"s_scat{i}") for i in range(4)]
        s_wT = sem("s_wT")
        s_wh = sem("s_wh")
        s_wl = sem("s_wl")
        s_xs = [sem(f"s_xs{i}") for i in range(2)]
        s_xT = sem("s_xT")
        s_xh = sem("s_xh")
        s_xl = sem("s_xl")
        s_up = sem("s_up")
        s_sg = sem("s_sg")
        s_mid = sem("s_mid")
        s_mT = sem("s_mT")
        s_hh = sem("s_hh")
        s_hl = sem("s_hl")
        s_down = sem("s_down")
        s_y = sem("s_y")
        s_yst = [sem(f"s_yst{i}") for i in range(2)]
        s_yg = [sem(f"s_yg{i}") for i in range(4)]
        s_x1 = sem("s_x1")
        s_out = sem("s_out")
        s_tab = sem("s_tab")
        s_tabT = sem("s_tabT")
        s_tabc = sem("s_tabc")
        s_wrow = sem("s_wrow")
        s_wdn = [sem(f"s_wdn{i}") for i in range(4)]
        s_w16 = sem("s_w16")
        s_w16c = sem("s_w16c")
        s_xnb = sem("s_xnb")
        s_bT = sem("s_bT")
        s_bTh = sem("s_bTh")
        s_bTl = sem("s_bTl")
        s_wn = sem("s_wn")
        s_pa = sem("s_pa")
        s_pb = sem("s_pb")
        s_pw = sem("s_pw")
        s_t1h = sem("s_t1h")
        s_t1 = sem("s_t1")
        s_hr = sem("s_hr")
        s_gwh = sem("s_gwh")
        s_gwl = sem("s_gwl")
        s_gsc = sem("s_gsc")
        s_wdt = sem("s_wdt")
        s_wdh = sem("s_wdh")
        s_wdl = sem("s_wdl")
        s_gu = sem("s_gu")
        s_bs = sem("s_bs")
        s_bh = sem("s_bh")
        s_bhh = sem("s_bhh")
        s_bhl = sem("s_bhl")
        s_bd = sem("s_bd")
        s_acc = sem("s_acc")
        s_vn = sem("s_vn")
        s_cxn = sem("s_cxn")
        s_ck = sem("s_ck")
        s_cv = sem("s_cv")
        s_cf = sem("s_cf")
        s_cl = sem("s_cl")
        s_ce = sem("s_ce")
        s_cn = sem("s_cn")
        s_cna = sem("s_cna")
        s_cd = sem("s_cd")
        s_cy = sem("s_cy")
        s_co = sem("s_co")
        s_cr = sem("s_cr")
        s_wst = [sem(f"s_wst{i}") for i in range(3)]
        s_whi = [sem(f"s_whi{i}") for i in range(3)]
        s_w13 = sem("s_w13")
        s_w2 = sem("s_w2")
        s_dxn = sem("s_dxn")
        s_dxs = [sem(f"s_dxs{i}") for i in range(2)]
        s_dxT = sem("s_dxT")
        s_dxh = sem("s_dxh")
        s_dxl = sem("s_dxl")
        s_dup = sem("s_dup")
        s_dsg = sem("s_dsg")
        s_dmid = sem("s_dmid")
        s_dmT = sem("s_dmT")
        s_dhh = sem("s_dhh")
        s_dhl = sem("s_dhl")
        s_dd = sem("s_dd")
        s_dy = sem("s_dy")
        s_dst = [sem(f"s_dst{i}") for i in range(2)]
        s_b8 = sem("s_b8")
        s_lp = sem("s_lp")
        s_lg = sem("s_lg")
        s_gw = sem("s_gw")
        s_gwhi = sem("s_gwhigh")
        s_wsh = [sem(f"s_wsh{i}") for i in range(3)]
        s_gwlow = sem("s_gwlow")
        s_ex8 = sem("s_ex8")
        s_mask1 = sem("s_mask1")
        s_rank1 = sem("s_rank1")
        s_slot1 = sem("s_slot1")
        s_row = sem("s_row")
        s_rsc = [sem(f"s_rsc{i}") for i in range(4)]
        s_zero1 = sem("s_zero1")
        s_shl = sem("s_shl")
        s_sha = sem("s_sha")
        s_fin = [[sem(f"s_fin{i}_{k}") for k in range(2)] for i in range(6)]
        s_x4 = sem("s_x4")

        x_v = x.rearrange("b (i p) d -> p (b i) d", p=P)
        out_v = out.rearrange("b (i p) d -> p (b i) d", p=P)
        tok_v = tok.rearrange("b (i p) -> p (b i)", p=P)
        ctx_v = ctx.rearrange("e (f p) d -> p e f d", p=P)
        wdn_at = [wdn[:, n, :, :] for n in range(2)] + [
            nat[:, 1, 2 * n:2 * n + 2, :].rearrange("p a (h c) -> p (a h) c", c=P) for n in range(2)]
        wd_v = w_down.rearrange("(h a) (c p) -> (a c) h p", a=8, p=P)
        wug_v = [w.rearrange("(h a) (c p) -> (a c) h p", a=32, p=P) for w in (w_gate, w_up)]

        def wait(eng, s, v):
            if not isinstance(v, int) or v > 0:
                eng.wait_ge(s, v)

        def f32(ap):
            return ap.bitcast(F32)

        def inside(t, lo, hi):
            return not isinstance(t, int) or lo <= t < hi

        shared_part = (sw1.rearrange("(k p) n -> p k n", p=P), sw3.rearrange("(k p) n -> p k n", p=P),
                       sw2.rearrange("(k p) n -> p k n", p=HP))
        router = gate_w.rearrange("(k p) n -> p k n", p=P)

        def w_rows(p, width):
            q, step = ((P, G_W), (P, HID), (HP, D))[p]
            return wst[p][0:q, 0:HC * step].rearrange("p (k n) -> p k n", k=HC)[:, :, 0:width]

        def c_keys_bank(n):
            return 6 if n < 2 else 5

        def c_values_bank(n):
            return 7 if n < 1 else 6

        def x_buf(t, par):
            return par + 2 if isinstance(t, int) and HELD + 2 <= t < TT else par

        block = es.enter_context(nc.Block())

        @block.sync
        def _(sp):
            sp.dma_start(cst[:, :], consts).then_inc(s_cst, 16)
            sp.dma_start(tok_sb[:, :], tok_v, allow_slow_non_contiguous=True).then_inc(s_cst, 16)
            sp.dma_start(tab_in[T_SUG:T_SDP, :], su_ug.rearrange("(c p) -> c p", p=P)).then_inc(s_tab, 16)
            sp.dma_start(tab_in[T_SDP:T_WUP, :], su_dp.rearrange("(c p) -> c p", p=P)).then_inc(s_tab, 16)
            sp.dma_start(tab_in[T_DEC:T_BON, :], wkv_w.rearrange("(c p) -> c p", p=P)).then_inc(s_tab, 16)
            sp.dma_start(tab_in[T_BON:T_ROWS, :], wkv_u.rearrange("(c p) -> c p", p=P)).then_inc(s_tab, 16)
            sp.dma_start(tab_in[T_WUP:T_DEC, :], wscale_ug.rearrange("(c p) -> c p", p=P)).then_inc(s_tab, 16)
            for e in range(2):
                sp.dma_start(nat[:, e, :, :], ctx_v[:, e, :, :]).then_inc(s_ctx[e], 16)
            for q in range(4):
                sp.dma_start(xres[:, 4 * q:4 * q + 4, :], x_v[:, 4 * q:4 * q + 4, :]).then_inc(s_x[q], 16)
            for e in range(2, E0):
                sp.wait_ge(s_wT, (e - 1) * DC)
                sp.dma_start(nat[:, e % 2, :, :], ctx_v[:, e, :, :]).then_inc(s_ctx[e], 16)
            for q in range(4):
                sp.wait_ge(s_scat[q], 16 * TT // 4)
            sp.wait_ge(s_wT, E0 * DC)

            def load(t, par):
                sp.dma_start(xs[par][:, :], xs_dram[bass.ds(t * P, P), :]).then_inc(s_xs[par], 16)

            load(0, 0)
            load(1, 1)
            for n in range(4):
                sp.dma_start(wdn_at[n], wd_v[:, 8 * n:8 * n + 8, :]).then_inc(s_wdn[n], 16)

            def step(t, par):
                if inside(t + 2, 0, NT0):
                    sp.wait_ge(s_xT, t + 1)
                    load(t + 2, par)
                if inside(t - 2, 0, NT0):
                    sp.wait_ge(s_y, t - 1)
                    sp.dma_start(y_dram[bass.ds((t - 2) * P, P), :], ysb[par][:, :]).then_inc(s_yst[par], 16)

            step(0, 0)
            step(1, 1)
            with sp.Fori(2, 2 + 2 * ((NT0 - 4) // 2), 2) as t:
                step(t, 0)
                step(t + 1, 1)
            for t in range(2 + 2 * ((NT0 - 4) // 2), NT0 + 2):
                step(t, t % 2)

            def load_wn(j, m):
                wait(sp, s_pa, 4 * j + 2 * m)
                sp.dma_start(wn[:, :, :], wug_v[m][:, bass.ds(j * 8, 8), :]).then_inc(s_wn, 16)

            sp.wait_ge(s_down, NT0)
            load_wn(0, 0)
            load_wn(0, 1)
            for n in range(4, 8):
                sp.wait_ge(s_w16, 2 * (n - 3))
                sp.dma_start(wdn_at[n % 4], wd_v[:, 8 * n:8 * n + 8, :]).then_inc(s_wdn[n % 4], 16)
            load_wn(1, 0)
            load_wn(1, 1)
            with sp.Fori(2, NJ) as j:
                load_wn(j, 0)
                load_wn(j, 1)

            sp.wait_ge(s_acc, 16 * (NJ - 1) + 4)
            sp.dma_start(vnat[:, :, :], ctx_v[:, 0, :, :]).then_inc(s_vn, 16)
            sp.wait_ge(s_acc, 16 * NJ)
            sp.dma_start(w_rows(0, G_W)[:, :, HID:G_W], router).then_inc(s_gw, 16)
            for p in range(3):
                sp.dma_start(w_rows(p, (HID, HID, D)[p]), shared_part[p]).then_inc(s_wsh[p], 16)
            sp.dma_start(bias8[:, :], expert_bias.rearrange("(a n) -> a n", a=1).broadcast_to([P, E1])).then_inc(s_b8, 16)

            def load(t, par):
                sp.dma_start(xsd[par][:, :], xs1_dram[bass.ds((t - TT) * P, P), :]).then_inc(s_dxs[par], 16)

            def store(t, par):
                sp.wait_ge(s_dy, t + 1)
                sp.dma_start(y1_dram[bass.ds(t * P, P), :], dys[par][:, :]).then_inc(s_dst[par], 16)

            for n in range(TT + 7):
                if n % 4 == 3 and n + 1 < NU:
                    sp.wait_ge(s_cv, n + 1)
                    sp.dma_start(vnat[:, :, :], ctx_v[:, n // 4 + 1, :, :]).then_inc(s_vn, 16)
                if n >= 7:
                    store(n - 7, (n - 7) % 2)
            for i in range(4):
                sp.wait_ge(s_rsc[i], 16 * 2 * TT // 4)
            load(TT, 0)
            load(TT + 1, 1)
            for t in range(2):
                sp.wait_ge(s_dxT, TT + t + 1)
                load(TT + 2 + t, t)
            for i in range(2):
                sp.wait_ge(s_dst[i], 16 * TT // 2)

            def pair(t):
                for i in range(2):
                    sp.wait_ge(s_dxT, t + i + 1)
                    load(t + i + 2, i)
                    store(t + i - 2, i)

            with sp.Fori(TT + 2, TT + 1 + 2 * TT, 2) as t:
                sp.wait_ge(s_sha, t - TT)
                sp.dma_start(row[:, 0, :], y1_dram[bass.ds((t - TT - 2) * (P // 2), P), :]).then_inc(s_shl, 16)
                pair(t)
            for t in range(TT + 2 + 2 * TT, TT + NT1 - 4, 2):
                pair(t)
            sp.wait_ge(s_dxT, TT + NT1 - 2)
            load(TT + NT1 - 1, 0)
            for t in range(TT + NT1 - 5, TT + NT1):
                store(t, t % 2)

            for t in range(0, TT, 2):
                sp.wait_ge(s_x4, t + 2)
                sp.dma_start(out_v[:, t:t + 2, :], xres[:, t:t + 2, :]).then_inc(s_out, 16)
            sp.wait_ge(s_out, 16 * TT // 2)

        @block.gpsimd
        def _(pool):
            pool.wait_ge(s_cst, 32)
            pool.memset(zero[:, :], 0.0).then_inc(s_zero, 1)
            pool.wait_ge(s_zero, 1)
            pool.dma_start(xs_dram[TOK:NT0 * P, :].rearrange("(p r) (a d) -> p (r a) d", p=P, d=P),
                           zero[:, :].unsqueeze(1).broadcast_to([P, (NT0 - TT) * DC, P])).then_inc(s_zeroed, 16)

            def inv_std(n, q=None):
                q = n % 4 if q is None else q
                pool.wait_ge(s_var, n + 1)
                pool.tensor_tensor(rstd[:, 4 * q:4 * q + 4], vare[:, 4 * q:4 * q + 4],
                                   cst[:, C_HALF:C_HALF + 4], ALU.pow).then_inc(s_rstd, 1)

            pool.wait_ge(s_zeroed, 16)
            pool.wait_ge(s_slot, 1)
            for e in range(E0):
                last = pool.value_load(tlast_i[0:1, e:e + 1], min_val=0, max_val=NT0 + E0 - 1)
                pool.dma_start(xs_dram[bass.ds(last * P, P), :].rearrange("p (a d) -> p a d", d=P),
                               zero[:, :].unsqueeze(1).broadcast_to([P, DC, P])).then_inc(s_zlast, 16)
                if e < 2:
                    inv_std(e)
            pool.wait_ge(s_zlast, 16 * E0)
            for i in range(TT):
                if i in (2, 3):
                    inv_std(i)
                pool.wait_ge(s_xn, i + 1)
                pool.indirect_dma_start(xs_dram, bass.IndirectOffsetOnAxis(ap=slot[:, i:i + 1], axis=0),
                                        xn[:, i % 4, :], None).then_inc(s_scat[i % 4], 16)
            pool.wait_ge(s_yst[0], 16 * ((NT0 + 1) // 2))
            pool.wait_ge(s_yst[1], 16 * (NT0 // 2))
            for q in range(NB):
                for i in range(4 * q, 4 * q + 4):
                    if q >= 1 and i == 4 * q + 3:
                        inv_std(4 + q - 1)
                    if i >= 4:
                        pool.wait_ge(s_x1, i - 3)
                    pool.indirect_dma_start(yg[i % 4][:, :], None, y_dram,
                                            bass.IndirectOffsetOnAxis(ap=slot[:, i:i + 1], axis=0))\
                        .then_inc(s_yg[i % 4], 16)
            inv_std(4 + NB - 1)

            def w_part(idx, p):
                if isinstance(idx, int) and idx == 0:
                    return shared_part[p]
                w, q = ((w1, P), (w3, P), (w2, HP))[p]
                return w[bass.ds(idx - 1, 1), :, :].rearrange("e (k p) n -> p (e k) n", p=q)

            places = [0]

            def alone(idx):
                if not isinstance(idx, int) or idx > 2:
                    n = places[0] = places[0] + 1
                    pool.tensor_tensor(pace[:, n:n + 1], pace[:, 0:1], pace[:, 0:1], ALU.add)

            def w_raw(idx, p):
                pool.dma_start(w_rows(p, (HID, HID, D)[p]), w_part(idx, p)).then_inc(s_wst[p], 16)

            def w_place(whole, slot, p, width):
                q, at, step = ((P, W_1, G_W), (P, W_3, HID), (HP, W_2, D))[p]
                return whole[0:q, slot, at:at + HC * step].rearrange("p (k n) -> p k n", k=HC)[:, :, 0:width]

            def w_high(idx, p, slot):
                pool.dma_start(w_place(Wh, slot, p, (HID, HID, D)[p]), w_part(idx, p)).then_inc(s_whi[p], 16)

            def w_low(idx, p, slot):
                width = (HID, HID, D)[p]
                if isinstance(idx, int) and idx == 0:
                    pool.wait_ge(s_wsh[p], 16)
                else:
                    pool.wait_ge(s_wst[p], 16 * idx)
                pool.wait_ge(s_whi[p], 16 * (idx + 1))
                pool.tensor_tensor(w_place(Wl, slot, p, width), w_rows(p, width), f32(w_place(Wh, slot, p, width)), ALU.subtract)\
                    .then_inc((s_w13, s_w13, s_w2)[p], 1)
                if p < 2:
                    pool.wait_ge(s_w13, 2 * idx + p + 1)
                else:
                    pool.wait_ge(s_w2, idx + 1)

            for q in range(3):
                pool.wait_ge(s_gu, 8 * q + 4)
                pool.dma_start(xs1_dram.rearrange("(q p r) (a d) -> q p (r a) d", p=P, q=3, d=P)[q],
                               zero[:, :].unsqueeze(1).broadcast_to([P, NT1 // 3 * DC, P])).then_inc(s_zero1, 16)
            pool.wait_ge(s_zero1, 48)
            inv_std(8)
            pool.memset(pace[:, :], 0.0).then_inc(s_zero, 1)
            pool.wait_ge(s_zero, 2)

            def w_shared():
                pool.dma_start(w_place(Wh, 1, 0, G_W)[:, :, HID:G_W], router).then_inc(s_gwhi, 16)
                for p in range(3):
                    w_high(0, p, 1)

            def w_router_low():
                pool.wait_ge(s_gw, 16)
                pool.wait_ge(s_gwhi, 16)
                pool.tensor_tensor(w_place(Wl, 1, 0, G_W)[:, :, HID:G_W], w_rows(0, G_W)[:, :, HID:G_W],
                                   f32(w_place(Wh, 1, 0, G_W))[:, :, HID:G_W], ALU.subtract).then_inc(s_gwlow, 1)

            def w_all(idx, slot, ups=None, downs=None, more=True):
                if ups is not None:
                    pool.wait_ge(s_dup, ups)
                    alone(idx)
                for p in range(2):
                    w_high(idx, p, slot)
                for p in range(2):
                    w_low(idx, p, slot)
                    if more:
                        alone(idx)
                        w_raw(idx + 1, p)
                if downs is not None:
                    pool.wait_ge(s_dd, downs)
                    alone(idx)
                w_high(idx, 2, slot)
                w_low(idx, 2, slot)
                if more:
                    alone(idx)
                    w_raw(idx + 1, 2)

            def clamp(n):
                pool.wait_ge(s_cf, n + 1)
                wait(pool, s_ce, 3 * n)
                pool.tensor_scalar(row[:, 0, :], cd[:, :], 0.0, None, ALU.max).then_inc(s_cl, 1)
                pool.tensor_scalar(row[:, 1, :], cd[:, :], 0.0, None, ALU.min).then_inc(s_cl, 1)
                pool.tensor_scalar(row[:, 2, :], cd[:, :], wlim[:, n % DC:n % DC + 1], None, ALU.min).then_inc(s_cl, 1)

            def finish(n):
                pool.wait_ge(s_cn, n + 1)
                pool.tensor_tensor(cnum[:, :], cnum[:, :], cp[:, 0:512], ALU.add).then_inc(s_cna, 1)
                pool.wait_ge(s_cna, n + 1)
                pool.wait_ge(s_cd, n + 1)
                wait(pool, s_cr, n - 1)
                pool.tensor_tensor(cy[n % 2][:, :], cnum[:, :], ce[n % 2][:, 2, :], ALU.mult).then_inc(s_cy, 1)

            clamp(0)
            power = 9
            for n in range(NU + 1):
                if n + 1 < NU:
                    clamp(n + 1)
                if n == 0:
                    pool.wait_ge(s_acc, 16 * NJ)
                    w_shared()
                if n % 4 == 2 and n + 2 < NU:
                    inv_std(power, n // 4 + 1)
                    power += 1
                if n < NU:
                    finish(n)
                if n == 0:
                    w_router_low()
                if 1 <= n <= 3:
                    w_low(0, n - 1, 1)
                if n % 4 == 0 and n >= 4:
                    inv_std(power, n // 4 - 1)
                    power += 1
            pool.wait_ge(s_co, NU)
            for p in range(3):
                w_raw(1, p)
            w_all(1, 0)
            pool.wait_ge(s_slot1, 1)
            for t in range(TT):
                for k in range(2):
                    n = 2 * t + k
                    pool.wait_ge(s_row, n + 1)
                    pool.indirect_dma_start(xs1_dram, bass.IndirectOffsetOnAxis(ap=slw[:, k, t:t + 1], axis=0),
                                            row[:, n % 4, :], None).then_inc(s_rsc[n % 4], 16)
            w_all(2, 1, TT, TT)

            def w_next(idx, slot, more=True):
                last = pool.value_load(tend1_i[0:1, bass.ds(idx - 3, 1)], min_val=1, max_val=NT1)
                w_all(idx, slot, last + TT, last + TT, more)

            with pool.Fori(3, E1 - 2, 2) as idx:
                w_next(idx, 0)
                w_next(idx + 1, 1)
            w_next(E1 - 1, 0)
            w_next(E1, 1, False)
            for i in range(2):
                pool.wait_ge(s_dst[i], 16 * ((TT + NT1 + 1 - i) // 2))
            for t in range(TT):
                if t >= 6:
                    pool.wait_ge(s_x4, t - 5)
                for k in range(2):
                    pool.indirect_dma_start(fin[:, 2 * (t % 6) + k, :], None, y1_dram,
                                            bass.IndirectOffsetOnAxis(ap=slr[:, k, t:t + 1], axis=0))\
                        .then_inc(s_fin[t % 6][k], 16)

        @block.scalar
        def _(act):
            act.dma_start(gates_raw[:, 0:2], g_xattn.rearrange("(a n) -> a n", a=1).broadcast_to([P, 2])).then_inc(s_gl, 16)
            act.dma_start(gates_raw[:, 2:4], g_ffn.rearrange("(a n) -> a n", a=1).broadcast_to([P, 2])).then_inc(s_gl, 16)
            act.dma_start(wrow[:, :], wscale_dp.rearrange("(a n) -> a n", a=1).broadcast_to([P, D])).then_inc(s_wrow, 16)
            act.wait_ge(s_gl, 32)
            act.activation(gates[:, :], gates_raw[:, :], ACT.Tanh).then_inc(s_gate, 1)
            act.wait_ge(s_tabT, 1)
            act.activation(tab[:, :], bank[4][:, 0:T_ROWS], ACT.Copy).then_inc(s_tabc, 1)
            act.wait_ge(s_tabc, 1)
            act.mul(tab[:, T_SUG:T_SDP], tab[:, T_SUG:T_SDP], float(D) ** -0.5).then_inc(s_tabc, 1)
            act.mul(tab[:, T_SDP:T_WUP], tab[:, T_SDP:T_WUP], float(F0) ** -0.5).then_inc(s_tabc, 1)
            act.wait_ge(s_wrow, 16)
            act.wait_ge(s_gate, 1)
            act.mul(wrow[:, :], wrow[:, :], gates[:, 2:3]).then_inc(s_tabc, 1)
            for j in range(E0 * DC):
                act.wait_ge(s_wT, j + 1)
                act.activation(wh[:, j, :], bank[6 + j % 2][:, :], ACT.Copy).then_inc(s_wh, 1)


            def x_high(t, par):
                act.wait_ge(s_xT, t + 1)
                if inside(t - 2, 0, NT0):
                    act.wait_ge(s_up, t - 1)
                act.activation(xh[par][:, :, :].rearrange("p k n -> p (k n)"), bank[0][:, :], ACT.Copy).then_inc(s_xh, 1)

            def step(t, par):
                if inside(t + 1, 0, NT0):
                    x_high(t + 1, 1 - par)
                if inside(t, 0, NT0):
                    act.wait_ge(s_up, t + 1)
                    if inside(t - 2, 0, NT0):
                        act.wait_ge(s_mid, t - 1)
                    act.activation(sg[par][:, :], bank[2 + par][:, :], ACT.Silu).then_inc(s_sg, 1)
                if inside(t - 1, 0, NT0):
                    act.wait_ge(s_mT, t)
                    if inside(t - 3, 0, NT0):
                        act.wait_ge(s_down, t - 2)
                    act.activation(hh[1 - par][:, :, :].rearrange("p k n -> p (k n)"), bank[1][:, :], ACT.Copy).then_inc(s_hh, 1)
                if inside(t - 2, 0, NT0):
                    act.wait_ge(s_down, t - 1)
                    if inside(t - 4, 0, NT0):
                        act.wait_ge(s_yst[par], 16 * (t // 2 - 1) if isinstance(t, int) else ((t - par) * 8 - 16))
                    act.activation(ysb[par][:, :], bank[4 + par][:, :], ACT.Copy).then_inc(s_y, 1)

            x_high(0, 0)
            for t in range(0, 4):
                step(t, t % 2)
            with act.Fori(4, 4 + 2 * ((NT0 - 1 - 4) // 2), 2) as t:
                step(t, 0)
                step(t + 1, 1)
            for t in range(4 + 2 * ((NT0 - 1 - 4) // 2), NT0 + 2):
                step(t, t % 2)

            def turn(b):
                for n in range(DC * b, DC * b + DC):
                    act.wait_ge(s_bT, n + 1)
                    c = n % DC
                    act.mul(xTh[:, b, c, :], bank[6 + n % 2][:, :], tab[:, T_SUG + c:T_SUG + c + 1]).then_inc(s_bTh, 1)

            def prep_t(j, m):
                wait(act, s_pb, 4 * j + 2 * m)
                for i in range(2):
                    act.wait_ge(s_pa, 4 * j + 2 * m + i + 1)
                    act.activation(wt1h[:, :, i * P:(i + 1) * P], bank[6 + i][:, :].rearrange("p (n c) -> p c n", c=DC),
                                   ACT.Copy).then_inc(s_t1h, 1)

            def prep_gu(j, m, slot):
                for i in range(2):
                    act.wait_ge(s_pb, 4 * j + 2 * m + i + 1)
                    wait(act, s_gu, 8 * (j - 1))
                    act.activation(gwh[slot][:, m, 2 * i:2 * i + 2, :].rearrange("p c f -> p (c f)"),
                                   bank[6 + i][:, :], ACT.Copy).then_inc(s_gwh, 1)

            def exps(n):
                act.wait_ge(s_cl, 3 * n + 3)
                wait(act, s_cy, n - 1)
                e = ce[n % 2]
                act.activation(e[:, 0, :], row[:, 0, :], ACT.Exp, scale=-1.0).then_inc(s_ce, 1)
                act.activation(e[:, 1, :], row[:, 1, :], ACT.Exp).then_inc(s_ce, 1)
                act.activation(e[:, 2, :], row[:, 2, :], ACT.Exp, bias=wub[:, n % DC:n % DC + 1]).then_inc(s_ce, 1)

            def chunk(j, slot, more, turns=False):
                for b in range(NB):
                    for f in range(2):
                        k = 8 * j + 2 * b + f
                        act.wait_ge(s_gu, k + 1)
                        wait(act, s_bhl, k - 1)
                        if b == 0 and f == 0:
                            act.wait_ge(s_gsc, j + 1)
                        act.activation(bs[:, f, :], bank[2 * f][:, :], ACT.Silu,
                                       scale=gsc[slot][:, f:f + 1]).then_inc(s_bs, 1)
                        act.wait_ge(s_bh, k + 1)
                        wait(act, s_bd, 4 * (4 * j + b - 1))
                        act.activation(bhh[b % 2][:, f, :], bs[:, f, :], ACT.Copy).then_inc(s_bhh, 1)
                    if b == 0:
                        wait(act, s_bd, 16 * j)
                        for f in range(2):
                            act.wait_ge(s_wdt, 2 * j + f + 1)
                            act.activation(wdh[:, f, :], wdt[:, f, :], ACT.Copy).then_inc(s_wdh, 1)
                    if turns:
                        if b < NB - 1:
                            turn(b + 1)
                        if b >= 2:
                            prep_gu(j + 1, b - 2, 1 - slot)
                        if b in (1, 2):
                            prep_t(j + 1, b - 1)
                    elif not more:
                        if b == 3:
                            exps(0)
                    else:
                        if b == 0:
                            prep_t(j + 1, 0)
                        if b in (1, 2):
                            prep_gu(j + 1, b - 1, 1 - slot)
                        if b == 1:
                            prep_t(j + 1, 1)

            act.wait_ge(s_down, NT0)
            act.activation(Hr[:, :], cst[:, C_H:C_H + P], ACT.Copy).then_inc(s_hr, 1)
            for m in range(2):
                prep_t(0, m)
                prep_gu(0, m, 0)
                for n in range(8 * m, 8 * m + 8):
                    act.wait_ge(s_w16, n + 1)
                    act.activation(wd16[:, :, 32 * n:32 * n + 32],
                                   bank[6 + n % 2][:, :].rearrange("p (n c) -> p c n", c=FC), ACT.Copy).then_inc(s_w16c, 1)
            turn(0)
            chunk(0, 0, True, turns=True)
            with act.Fori(1, NJ - 2, 2) as j:
                chunk(j, 1, True)
                chunk(j + 1, 0, True)
            chunk(NJ - 1, 1, False)

            def d_x(t, par):
                act.wait_ge(s_dxT, t + 1)
                if x_buf(t, par) == par:
                    wait(act, s_dup, t - 1)
                act.activation(dxh[x_buf(t, par)][:, :, :].rearrange("p k n -> p (k n)"), bank[0][:, :], ACT.Copy).then_inc(s_dxh, 1)

            def d_gate(t, par):
                act.wait_ge(s_dup, t + 1)
                wait(act, s_dmid, t)
                act.activation(dsg[:, :], bank[2][:, 0:HID], ACT.Silu).then_inc(s_dsg, 1)

            def d_hid(t, par):
                act.wait_ge(s_dmT, t + 1)
                wait(act, s_dd, t - 1)
                act.activation(dhh[par][:, :, :].rearrange("p k n -> p (k n)"), bank[1][0:HP, :], ACT.Copy).then_inc(s_dhh, 1)

            def d_y(t, par):
                act.wait_ge(s_dd, t + 1)
                if not isinstance(t, int) or t >= 2:
                    act.wait_ge(s_dst[par], 16 * (t // 2) if isinstance(t, int) else (t - par) * 8)
                act.activation(dys[par][:, :], bank[4][:, :], ACT.Copy).then_inc(s_dy, 1)

            act.wait_ge(s_acc, 16 * NJ)
            for n in range(NU + 1):
                t = n - 5
                if t >= 0 and t % 4 == 0:
                    d_x(t, t % 2)
                if t >= 1:
                    d_hid(t - 1, (t - 1) % 2)
                if t >= 0 and t % 4 != 3:
                    d_x(t + 1, (t + 1) % 2)
                if n + 1 < NU:
                    exps(n + 1)
                if t >= 0:
                    d_gate(t, t % 2)
                if t >= 2:
                    d_y(t - 2, t % 2)
            d_x(HELD, 0)
            d_hid(HELD - 1, 1)
            d_x(HELD + 1, 1)
            d_x(HELD + 2, 0)
            d_y(HELD - 2, 0)
            d_x(HELD + 3, 1)
            act.wait_ge(s_lg, HELD + 2)
            act.activation(prob[:, :, :], lg[:, :, :], ACT.Exp).then_inc(s_ex8, 1)
            for t in range(HELD, TT):
                d_gate(t, t % 2)
                d_y(t - 1, (t - 1) % 2)
                d_hid(t, t % 2)
            d_y(TT - 1, 1)
            d_x(TT, 0)
            d_x(TT + 1, 1)
            d_gate(TT, 0)
            d_x(TT + 2, 0)
            d_gate(TT + 1, 1)
            d_hid(TT, 0)
            with act.Fori(TT + 2, TT + NT1 - 2, 2) as t:
                for i in range(2):
                    d_x(t + i + 1, 1 - i)
                    d_gate(t + i, i)
                    d_hid(t + i - 1, 1 - i)
                    d_y(t + i - 2, i)
            T = TT + NT1 - 1
            d_gate(T, T % 2)
            d_hid(T - 1, (T - 1) % 2)
            d_y(T - 2, T % 2)
            d_hid(T, T % 2)
            d_y(T - 1, (T - 1) % 2)
            d_y(T, T % 2)

        @block.tensor
        def _(pe):
            pe.wait_ge(s_cst, 32)

            def weights(e):
                pe.wait_ge(s_ctx[e], 16)
                for k in range(DC):
                    j = e * DC + k
                    if j >= 2:
                        pe.wait_ge(s_wl, j - 1)
                    for f in range(DC):
                        mm = pe.transpose(bank[6 + j % 2][:, f * P:(f + 1) * P], nat[:, e % 2, f, k * P:(k + 1) * P], ident)
                    mm.then_inc(s_wT, 1)

            pe.wait_ge(s_tab, 80)
            pe.transpose(bank[4][:, 0:T_ROWS], tab_in[:, :], ident[0:T_ROWS, 0:T_ROWS]).then_inc(s_tabT, 1)
            pe.wait_ge(s_rt, 1)
            n = (TT + 1) * E0
            pe.matmul(bank[5][:, 0:n], tri, mask[:, :, :].rearrange("p i e -> p (i e)"), start=True, stop=False)
            for j in range(TT):
                pe.matmul(bank[5][:, (j + 1) * E0:n].rearrange("p (i e) -> p i e", e=E0), ones,
                               mask[:, j:j + 1, :].broadcast_to([P, TT - j, E0]), start=False, stop=False,
                               skip_group_check=True)
            pe.matmul(bank[5][:, 0:n].rearrange("p (i e) -> p i e", e=E0), ones,
                      mask[:, TT:TT + 1, :].broadcast_to([P, TT + 1, E0]), start=False, stop=True).then_inc(s_rank, 1)
            for e in range(E0):
                weights(e)
            pe.wait_ge(s_wl, E0 * DC)
            pe.wait_ge(s_slot, 1)

            def x_turn(t, par):
                pe.wait_ge(s_xs[par], (t // 2 + 1) * 16 if isinstance(t, int) else (t - par) * 8 + 16)
                if inside(t - 1, 0, NT0):
                    pe.wait_ge(s_xl, t)
                for k in range(DC):
                    mm = pe.transpose(bank[0][:, k * P:(k + 1) * P], xs[par][:, k * P:(k + 1) * P], ident)
                mm.then_inc(s_xT, 1)

            def step(t, par, ex=[None, None]):
                if inside(t + 1, 0, NT0):
                    x_turn(t + 1, 1 - par)
                if inside(t, 0, NT0):
                    ex[par] = pe.value_load(tex_i[0:1, bass.ds(t, 1)], min_val=0, max_val=E0 - 1)
                    pe.wait_ge(s_xl, t + 1)
                    if inside(t - 2, 0, NT0):
                        pe.wait_ge(s_mid, t - 1)
                    n = 0
                    for a, w in ((xl, wh), (xh, wl), (xh, wh)):
                        for k in range(DC):
                            mm = pe.matmul(bank[2 + par][:, :], a[par][:, k, :], w[:, bass.ds(ex[par] * DC + k, 1), :],
                                           start=(n == 0), stop=(n == 3 * DC - 1))
                            n += 1
                    mm.then_inc(s_up, 1)
                if inside(t - 1, 0, NT0):
                    pe.wait_ge(s_mid, t)
                    if inside(t - 2, 0, NT0):
                        pe.wait_ge(s_hl, t - 1)
                    for k in range(DC):
                        mm = pe.transpose(bank[1][:, k * P:(k + 1) * P], mid[1 - par][:, k * P:(k + 1) * P], ident)
                    mm.then_inc(s_mT, 1)
                if inside(t - 2, 0, NT0):
                    ey = pe.value_load(tex_i[0:1, bass.ds(t - 2, 1)], min_val=0, max_val=E0 - 1)
                    pe.wait_ge(s_hl, t - 1)
                    if inside(t - 4, 0, NT0):
                        pe.wait_ge(s_y, t - 3)
                    n = 0
                    for a, w in ((hl, wh), (hh, wl), (hh, wh)):
                        for k in range(DC):
                            mm = pe.matmul(bank[4 + par][:, :], a[par][:, k, :], w[:, bass.ds(ey * DC + k, 1), :],
                                           start=(n == 0), stop=(n == 3 * DC - 1))
                            n += 1
                    mm.then_inc(s_down, 1)

            x_turn(0, 0)
            for t in range(0, 4):
                step(t, t % 2)
            with pe.Fori(4, 4 + 2 * ((NT0 - 1 - 4) // 2), 2) as t:
                step(t, 0)
                step(t + 1, 1)
            for t in range(4 + 2 * ((NT0 - 1 - 4) // 2), NT0 + 2):
                step(t, t % 2)

            def turn(b):
                pe.wait_ge(s_xnb, 4 * b + 4)
                for n in range(DC * b, DC * b + DC):
                    wait(pe, s_bTl, n - 1)
                    for i in range(4):
                        mm = pe.transpose(bank[6 + n % 2][:, i * P:(i + 1) * P], xnb[:, i, n % DC * P:(n % DC + 1) * P], ident)
                    mm.then_inc(s_bT, 1)

            def c_keys(n):
                pe.wait_ge(s_cxn, n // DC * 4 + 4)
                wait(pe, s_cf, n)
                for i in range(4):
                    mm = pe.transpose(bank[c_keys_bank(n)][:, i * P:(i + 1) * P], xnc[:, i, n % DC * P:(n % DC + 1) * P], ident)
                mm.then_inc(s_ck, 1)

            def c_values(n):
                pe.wait_ge(s_vn, 16 * (n // DC + 1))
                wait(pe, s_cn, n)
                if n == 1:
                    pe.wait_ge(s_cf, 2)
                for i in range(4):
                    mm = pe.transpose(bank[c_values_bank(n)][:, i * P:(i + 1) * P], vnat[:, i, n % DC * P:(n % DC + 1) * P], ident)
                mm.then_inc(s_cv, 1)

            def prep_a(j, m):
                pe.wait_ge(s_wn, 16 * (2 * j + m + 1))
                for i in range(2):
                    if m == 0:
                        wait(pe, s_wdt, 2 * j - 1 + i)
                    else:
                        pe.wait_ge(s_gwl, 4 * j + 1 + i)
                    for h in range(4):
                        mm = pe.matmul(bank[6 + i][:, h * P:(h + 1) * P], wn[:, 4 * i + h, :], cst[:, C_H4:C_H4 + P],
                                       start=True, stop=True)
                    mm.then_inc(s_pa, 1)

            def prep_b(j, m):
                pe.wait_ge(s_t1, 4 * j + 2 * m + 2)
                for i in range(2):
                    pe.matmul(bank[6 + i][:, :], Hr[:, :], wt1l[:, 2 * i:2 * i + 2, :].rearrange("p c f -> p (c f)"),
                              start=True, stop=False)
                    pe.matmul(bank[6 + i][:, :], Hr[:, :], wt1h[:, 2 * i:2 * i + 2, :].rearrange("p c f -> p (c f)"),
                              start=False, stop=True).then_inc(s_pb, 1)

            def prep_w(j):
                for f in range(2):
                    pe.wait_ge(s_gwl, 4 * j + 3 + f)
                    pe.matmul(bank[6 + f][:, :], cst[:, C_H:C_H + P],
                              wd16[:, bass.ds(2 * j + f, 1), :].rearrange("p a d -> p (a d)"), start=True, stop=True)\
                        .then_inc(s_pw, 1)

            def gate_up(j, b, slot):
                pe.wait_ge(s_gwl, 4 * j + 4)
                if isinstance(j, int) and j == 0:
                    pe.wait_ge(s_bTl, DC * b + DC)
                for f in range(2):
                    wait(pe, s_bh, 8 * j + 2 * b + f - 1)
                    for m in range(2):
                        n = 0
                        for w, a in ((gwl, xTh), (gwh, xTl), (gwh, xTh)):
                            for c in range(DC):
                                mm = pe.matmul(bank[2 * f + m][:, :], w[slot][:, m, c, f * P:(f + 1) * P], a[:, b, c, :],
                                               start=(n == 0), stop=(n == 3 * DC - 1))
                                n += 1
                    mm.then_inc(s_gu, 1)

            def down(j, b):
                pe.wait_ge(s_bhl, 8 * j + 2 * b + 2)
                pe.wait_ge(s_wdl, 2 * j + 2)
                for i in range(4):
                    wait(pe, s_acc, 16 * j + 4 * b + i - 1)
                    n = 0
                    for a, w in ((bhl, wdh), (bhh, wdl), (bhh, wdh)):
                        for f in range(2):
                            mm = pe.matmul(bank[4 + i % 2][:, :], a[b % 2][:, f, i * P:(i + 1) * P], w[:, f, :],
                                           start=(n == 0), stop=(n == 5))
                            n += 1
                    mm.then_inc(s_bd, 1)

            def chunk(j, slot, first, more):
                gate_up(j, 0, slot)
                if not first:
                    down(j - 1, 3)
                if more:
                    prep_a(j + 1, 0)
                gate_up(j, 1, slot)
                down(j, 0)
                if more:
                    prep_b(j + 1, 0)
                    prep_a(j + 1, 1)
                gate_up(j, 2, slot)
                down(j, 1)
                if more:
                    prep_b(j + 1, 1)
                gate_up(j, 3, slot)
                down(j, 2)
                if more:
                    prep_w(j + 1)

            pe.wait_ge(s_hr, 1)
            for m in range(2):
                wait(pe, s_w16c, 8 * m)
                prep_a(0, m)
                prep_b(0, m)
                pe.wait_ge(s_gwl, 2 * m + 2)
                for n in range(8 * m, 8 * m + 8):
                    if n % 2 == 0:
                        pe.wait_ge(s_wdn[n // 2 % 4], 16 * (n // 8 + 1))
                    wait(pe, s_w16c, n - 1)
                    for i in range(4):
                        mm = pe.matmul(bank[6 + n % 2][:, i * P:(i + 1) * P], wdn_at[n // 2 % 4][:, 4 * (n % 2) + i, :],
                                       cst[:, C_H16:C_H16 + P], start=True, stop=True)
                    mm.then_inc(s_w16, 1)
            pe.wait_ge(s_w16c, 16)
            turn(0)
            pe.wait_ge(s_bTl, DC)
            prep_w(0)
            gate_up(0, 0, 0)
            pe.wait_ge(s_wdt, 2)
            turn(1)
            gate_up(0, 1, 0)
            down(0, 0)
            turn(2)
            pe.wait_ge(s_bTl, 3 * DC)
            prep_a(1, 0)
            gate_up(0, 2, 0)
            down(0, 1)
            pe.wait_ge(s_t1, 6)
            turn(3)
            pe.wait_ge(s_bTl, 4 * DC)
            prep_b(1, 0)
            prep_a(1, 1)
            gate_up(0, 3, 0)
            prep_b(1, 1)
            down(0, 2)
            prep_w(1)
            with pe.Fori(1, NJ - 2, 2) as j:
                chunk(j, 1, False, True)
                chunk(j + 1, 0, False, True)
            j = NJ - 1
            gate_up(j, 0, 1)
            down(j - 1, 3)
            gate_up(j, 1, 1)
            down(j, 0)
            gate_up(j, 2, 1)
            c_keys(0)
            c_values(0)
            down(j, 1)
            gate_up(j, 3, 1)
            c_keys(1)
            down(j, 2)
            down(j, 3)

            def c_back(n):
                pe.wait_ge(s_cy, n + 1)
                wait(pe, s_co, n)
                for i in range(4):
                    mm = pe.transpose(bank[7][:, i * P:(i + 1) * P], cy[n % 2][:, i * P:(i + 1) * P], ident)
                mm.then_inc(s_cr, 1)

            def d_x(t, par, shared):
                if shared:
                    pe.wait_ge(s_dxn, t + 1)
                else:
                    pe.wait_ge(s_dxs[par], ((t - TT) // 2 + 1) * 16 if isinstance(t, int) else (t - TT - par) * 8 + 16)
                wait(pe, s_dxl, t)
                for k in range(DC):
                    mm = pe.transpose(bank[0][:, k * P:(k + 1) * P], xsd[par][:, k * P:(k + 1) * P], ident)
                mm.then_inc(s_dxT, 1)

            def d_up(t, par, shared):
                slot = 1
                if not shared:
                    e = pe.value_load(tex1_i[0:1, bass.ds(t - TT, 1)], min_val=0, max_val=E1 - 1)
                    pe.wait_ge(s_w13, e * 2 + 4)
                    slot = e % 2
                else:
                    pe.wait_ge(s_w13, 2)
                    pe.wait_ge(s_gwlow, 1)
                pe.wait_ge(s_dxl, t + 1)
                wait(pe, s_dmid, t)
                for o, at, step, width in ((2, W_1, G_W, G_W if shared and t < HELD else HID), (3, W_3, HID, HID)):
                    n = 0
                    for a, w in ((dxl, Wh), (dxh, Wl), (dxh, Wh)):
                        for k in range(DC):
                            mm = pe.matmul(bank[o][:, 0:width], a[x_buf(t, par)][:, k, :],
                                           w[:, bass.ds(slot, 1), at + k * step:at + k * step + width].rearrange("p a n -> p (a n)"),
                                           start=(n == 0), stop=(n == 3 * DC - 1))
                            n += 1
                mm.then_inc(s_dup, 1)

            def d_router(t, par):
                pe.wait_ge(s_dxl, t + 1)
                if t == HELD:
                    pe.wait_ge(s_cf, NU)
                n, i = 0, (t - HELD) * E1
                for a, w in ((dxl, Wh), (dxh, Wl), (dxh, Wh)):
                    for k in range(DC):
                        at = W_1 + k * G_W + HID
                        mm = pe.matmul(bank[5][:, i:i + E1], a[x_buf(t, par)][:, k, :], w[:, 1, at:at + E1],
                                       start=(n == 0), stop=(n == 3 * DC - 1))
                        n += 1
                mm.then_inc(s_lp, 1)

            def d_mid(t, par):
                pe.wait_ge(s_dmid, t + 1)
                wait(pe, s_dhl, t)
                for k in range(HC):
                    mm = pe.transpose(bank[1][0:HP, k * P:(k + 1) * P], dmid[par][:, k * HP:(k + 1) * HP], ident)
                mm.then_inc(s_dmT, 1)

            def d_down(t, par, shared):
                slot = 1
                if not shared:
                    e = pe.value_load(tex1_i[0:1, bass.ds(t - TT, 1)], min_val=0, max_val=E1 - 1)
                    pe.wait_ge(s_w2, e + 2)
                    slot = e % 2
                else:
                    pe.wait_ge(s_w2, 1)
                pe.wait_ge(s_dhl, t + 1)
                wait(pe, s_dy, t)
                n = 0
                for a, w in ((dhl, Wh), (dhh, Wl), (dhh, Wh)):
                    for k in range(HC):
                        mm = pe.matmul(bank[4][:, :], a[par][:, k, :],
                                       w[0:HP, bass.ds(slot, 1), W_2 + k * D:W_2 + (k + 1) * D].rearrange("p a n -> p (a n)"),
                                       start=(n == 0), stop=(n == 3 * HC - 1))
                        n += 1
                mm.then_inc(s_dd, 1)

            pe.wait_ge(s_acc, 16 * NJ)
            for n in range(NU + 1):
                if 1 <= n and n + 1 < NU:
                    c_keys(n + 1)
                t = n - 5
                if t >= 0 and t % 4 == 0:
                    d_x(t, t % 2, True)
                if 1 <= n <= NU:
                    c_back(n - 1)
                if 1 <= n < NU:
                    c_values(n)
                if t >= 1:
                    d_mid(t - 1, (t - 1) % 2)
                if t >= 0 and t % 4 != 3:
                    d_x(t + 1, (t + 1) % 2, True)
                if t >= 0:
                    d_up(t, t % 2, True)
                if t >= 2:
                    d_down(t - 2, t % 2, True)
            d_x(HELD, 0, True)
            d_mid(HELD - 1, 1)
            d_x(HELD + 1, 1, True)
            d_router(HELD, 0)
            d_x(HELD + 2, 0, True)
            d_down(HELD - 2, 0, True)
            d_router(HELD + 1, 1)
            d_x(HELD + 3, 1, True)
            d_router(HELD + 2, 0)
            d_router(HELD + 3, 1)
            d_up(HELD, 0, True)
            d_down(HELD - 1, 1, True)
            pe.wait_ge(s_mask1, 1)
            w = (TT + 1) * E1
            pe.matmul(bank[5][:, 0:w], tri, mask1[:, :, :].rearrange("p i e -> p (i e)"), start=True, stop=False)
            for j in range(TT):
                pe.matmul(bank[5][:, (j + 1) * E1:w].rearrange("p (i e) -> p i e", e=E1), ones,
                          mask1[:, j:j + 1, :].broadcast_to([P, TT - j, E1]), start=False, stop=False, skip_group_check=True)
            pe.matmul(bank[5][:, 0:w].rearrange("p (i e) -> p i e", e=E1), ones,
                      mask1[:, TT:TT + 1, :].broadcast_to([P, TT + 1, E1]), start=False, stop=True).then_inc(s_rank1, 1)
            d_mid(HELD, 0)
            for t in range(HELD + 1, TT):
                d_up(t, t % 2, True)
                d_down(t - 1, (t - 1) % 2, True)
                d_mid(t, t % 2)
            d_down(TT - 1, 1, True)
            pe.wait_ge(s_slot1, 1)
            d_x(TT, 0, False)
            d_x(TT + 1, 1, False)
            d_up(TT, 0, False)
            d_x(TT + 2, 0, False)
            d_up(TT + 1, 1, False)
            d_mid(TT, 0)
            with pe.Fori(TT + 2, TT + NT1 - 2, 2) as t:
                for i in range(2):
                    d_x(t + i + 1, 1 - i, False)
                    d_up(t + i, i, False)
                    d_mid(t + i - 1, 1 - i)
                    d_down(t + i - 2, i, False)
            T = TT + NT1 - 1
            d_up(T, T % 2, False)
            d_mid(T - 1, (T - 1) % 2)
            d_down(T - 2, T % 2, False)
            d_mid(T, T % 2)
            d_down(T - 1, (T - 1) % 2, False)
            d_down(T, T % 2, False)

        @block.vector
        def _(dve):
            rt = [0]

            def chain(ins):
                rt[0] += 1
                ins.then_inc(s_rt, 1)
                dve.wait_ge(s_rt, rt[0])

            dve.memset(mask[:, :, :], 0.0)
            dve.wait_ge(s_cst, 32)
            for e in range(E0 + 1):
                last = dve.tensor_scalar(ge[:, 0:TT, e], tok_sb[:, :], float(e * (VOCAB // E0)) if 0 < e < E0 else (-3.0e9 if e == 0 else 3.0e9),
                                         None, ALU.is_ge)
            last.then_inc(s_gate, 1)
            dve.wait_ge(s_gate, 2)
            chain(dve.tensor_tensor(mask[:, 0:TT, :], ge[:, 0:TT, 0:E0], ge[:, 0:TT, 1:E0 + 1], ALU.subtract))
            dve.wait_ge(s_rank, 1)
            chain(dve.tensor_copy(base[:, :, :].rearrange("p i e -> p (i e)"), bank[5][:, 0:(TT + 1) * E0]))
            chain(dve.tensor_tensor(cmp[:, :, :], base[:, TT, :].unsqueeze(2).broadcast_to([P, E0, TT]),
                                    cst[:, C_THR:C_THR + TT].unsqueeze(1).broadcast_to([P, E0, TT]), ALU.is_gt))
            chain(dve.tensor_reduce(ntile[:, :], cmp[:, :, :], AX.X, ALU.add))
            chain(dve.tensor_tensor_scan(tend[:, :], ones[:, 0:E0], ntile[:, :], 0.0, ALU.mult, ALU.add))
            chain(dve.tensor_scalar(tlast[:, :], tend[:, :], -1.0, None, ALU.add))
            chain(dve.scalar_tensor_tensor(out=tspare[:, :], in0=cst[:, C_IOTA:C_IOTA + E0], scalar=float(NT0), in1=tlast[:, :],
                                           op0=ALU.add, op1=ALU.subtract))
            chain(dve.scalar_tensor_tensor(out=tspare[:, :], in0=ntile[:, :], scalar=0.0, in1=tspare[:, :],
                                           op0=ALU.is_equal, op1=ALU.mult))
            chain(dve.tensor_tensor(tlast[:, :], tlast[:, :], tspare[:, :], ALU.add))
            chain(dve.tensor_copy(tlast_i[:, :], tlast[:, :]))
            chain(dve.tensor_tensor(tstart[:, :], tend[:, :], ntile[:, :], ALU.subtract))
            chain(dve.tensor_scalar(tstart[:, :], tstart[:, :], float(P), None, ALU.mult))
            chain(dve.tensor_tensor(base[:, 0:TT, :], base[:, 0:TT, :], tstart[:, :].unsqueeze(1).broadcast_to([P, TT, E0]), ALU.add))
            chain(dve.tensor_tensor(base[:, 0:TT, :], base[:, 0:TT, :], mask[:, 0:TT, :], ALU.mult))
            chain(dve.tensor_reduce(slot_f[:, :], base[:, 0:TT, :], AX.X, ALU.add))
            chain(dve.tensor_copy(slot[:, :], slot_f[:, :]))
            chain(dve.tensor_tensor(tcmp[:, :, :], cst[:, C_IOTA:C_IOTA + 48].unsqueeze(2).broadcast_to([P, 48, E0 - 1]),
                                    tend[:, 0:E0 - 1].unsqueeze(1).broadcast_to([P, 48, E0 - 1]), ALU.is_ge))
            chain(dve.tensor_reduce(tex[:, :], tcmp[:, :, :], AX.X, ALU.add))
            dve.tensor_copy(tex_i[:, :], tex[:, :]).then_inc(s_slot, 1)

            def statistics(q):
                dve.wait_ge(s_x[q], 16)
                for i in range(4 * q, 4 * q + 4):
                    last = dve.bn_stats(stats[:, i, :], xres[:, i, :])
                chain(last)
                for i in range(4 * q, 4 * q + 4):
                    last = dve.bn_aggr(mv[:, i, :], stats[:, i, :])
                chain(last)
                dve.tensor_scalar(vare[:, 4 * q:4 * q + 4], mv[:, 4 * q:4 * q + 4, 1], EPS, None, ALU.add).then_inc(s_var, 1)

            statistics(0)
            statistics(1)
            for i in range(TT):
                if i % 4 == 0:
                    dve.wait_ge(s_rstd, i // 4 + 1)
                wait(dve, s_scat[i % 4], 16 * (i // 4))
                dve.tensor_scalar(xn[:, i % 4, :], xres[:, i, :], mv[:, i, 0:1], rstd[:, i:i + 1],
                                  ALU.subtract, ALU.mult).then_inc(s_xn, 1)
                dve.wait_ge(s_wh, i + 1)
                dve.tensor_tensor(wl[:, i, :], bank[6 + i % 2][:, :], f32(wh[:, i, :]), ALU.subtract).then_inc(s_wl, 1)
                if i in (2, 3):
                    statistics(i)

            def x_low(t, par):
                dve.wait_ge(s_xh, t + 1)
                dve.tensor_tensor(xl[par][:, :, :].rearrange("p k n -> p (k n)"), bank[0][:, :],
                                  f32(xh[par][:, :, :]).rearrange("p k n -> p (k n)"), ALU.subtract).then_inc(s_xl, 1)

            def step(t, par):
                if inside(t + 1, 0, NT0):
                    x_low(t + 1, 1 - par)
                if inside(t, 0, NT0):
                    dve.wait_ge(s_sg, t + 1)
                    if inside(t - 2, 0, NT0):
                        dve.wait_ge(s_mT, t - 1)
                    dve.tensor_tensor(mid[par][:, :], bank[2 + par][:, :], sg[par][:, :], ALU.mult).then_inc(s_mid, 1)
                if inside(t - 1, 0, NT0):
                    dve.wait_ge(s_hh, t)
                    dve.tensor_tensor(hl[1 - par][:, :, :].rearrange("p k n -> p (k n)"), bank[1][:, :],
                                      f32(hh[1 - par][:, :, :]).rearrange("p k n -> p (k n)"), ALU.subtract).then_inc(s_hl, 1)

            x_low(0, 0)
            for t in range(0, 4):
                step(t, t % 2)
            with dve.Fori(4, 4 + 2 * ((NT0 - 1 - 4) // 2), 2) as t:
                step(t, 0)
                step(t + 1, 1)
            for t in range(4 + 2 * ((NT0 - 1 - 4) // 2), NT0 + 2):
                step(t, t % 2)
            def residual(q):
                for i in range(4 * q, 4 * q + 4):
                    dve.wait_ge(s_yg[i % 4], 16 * (i // 4 + 1))
                    dve.scalar_tensor_tensor(out=xres[:, i, :], in0=yg[i % 4][:, :], scalar=gates[:, 0:1], in1=xres[:, i, :],
                                             op0=ALU.mult, op1=ALU.add).then_inc(s_x1, 1)
                    dve.wait_ge(s_x1, i + 1)
                    last = dve.bn_stats(stats[:, i, :], xres[:, i, :])
                chain(last)
                for i in range(4 * q, 4 * q + 4):
                    last = dve.bn_aggr(mv[:, i, :], stats[:, i, :])
                chain(last)
                dve.tensor_scalar(vare[:, 4 * q:4 * q + 4], mv[:, 4 * q:4 * q + 4, 1], EPS, None, ALU.add).then_inc(s_var, 1)

            def normal(q):
                dve.wait_ge(s_rstd, 4 + q + 1)
                wait(dve, s_bT, 4 * q)
                for i in range(4):
                    t = 4 * q + i
                    dve.tensor_scalar(xnb[:, i, :], xres[:, t, :], mv[:, t, 0:1], rstd[:, t:t + 1],
                                      ALU.subtract, ALU.mult).then_inc(s_xnb, 1)

            def turn(b):
                for n in range(DC * b, DC * b + DC):
                    c = n % DC
                    dve.wait_ge(s_bTh, n + 1)
                    dve.scalar_tensor_tensor(out=xTl[:, b, c, :], in0=bank[6 + n % 2][:, :], scalar=tab[:, T_SUG + c:T_SUG + c + 1],
                                             in1=f32(xTh[:, b, c, :]), op0=ALU.mult, op1=ALU.subtract).then_inc(s_bTl, 1)

            def prep_a(j, m):
                wait(dve, s_pb, 4 * j + 2 * m)
                if m == 0:
                    wait(dve, s_wdl, 2 * j)
                for i in range(2):
                    dve.wait_ge(s_t1h, 4 * j + 2 * m + i + 1)
                    dve.tensor_tensor(wt1l[:, :, i * P:(i + 1) * P], bank[6 + i][:, :].rearrange("p (n c) -> p c n", c=DC),
                                      f32(wt1h[:, :, i * P:(i + 1) * P]), ALU.subtract).then_inc(s_t1, 1)

            def prep_b(j, m, slot):
                for i in range(2):
                    dve.wait_ge(s_gwh, 4 * j + 2 * m + i + 1)
                    dve.tensor_tensor(gwl[slot][:, m, 2 * i:2 * i + 2, :].rearrange("p c f -> p (c f)"), bank[6 + i][:, :],
                                      f32(gwh[slot][:, m, 2 * i:2 * i + 2, :]).rearrange("p c f -> p (c f)"), ALU.subtract)\
                       .then_inc(s_gwl, 1)

            def prep_w(j, slot):
                dve.tensor_scalar(gsc[slot][:, :], tab[:, bass.ds(T_WGT + 2 * j, 2)], 1.0, None, ALU.mult).then_inc(s_gsc, 1)
                wait(dve, s_wdh, 2 * j)
                wait(dve, s_wdl, 2 * j)
                for f in range(2):
                    dve.wait_ge(s_pw, 2 * j + f + 1)
                    dve.scalar_tensor_tensor(out=wdt[:, f, :], in0=bank[6 + f][:, :], scalar=tab[:, bass.ds(T_SDP + 2 * j + f, 1)],
                                             in1=wrow[:, :], op0=ALU.mult, op1=ALU.mult).then_inc(s_wdt, 1)

            def add_down(j, b, i):
                dve.wait_ge(s_bd, 16 * j + 4 * b + i + 1)
                wait(dve, s_acc, 16 * j + 4 * b + i - 8)
                dve.tensor_tensor(xres[:, 4 * b + i, :], bank[4 + i % 2][:, :], xres[:, 4 * b + i, :], ALU.add)\
                   .then_inc(s_acc, 1)

            def hidden(j, b, before):
                for f in range(2):
                    k = 8 * j + 2 * b + f
                    dve.wait_ge(s_bs, k + 1)
                    dve.scalar_tensor_tensor(out=bs[:, f, :], in0=bank[2 * f + 1][:, :], scalar=tab[:, bass.ds(T_WUP + 2 * j + f, 1)],
                                             in1=bs[:, f, :], op0=ALU.mult, op1=ALU.mult).then_inc(s_bh, 1)
                    if f == 1 and before is not None:
                        add_down(*before, 0)
                    dve.wait_ge(s_bhh, k + 1)
                    dve.tensor_tensor(bhl[b % 2][:, f, :], bs[:, f, :], f32(bhh[b % 2][:, f, :]), ALU.subtract)\
                       .then_inc(s_bhl, 1)
                if before is not None:
                    for i in range(1, 4):
                        add_down(*before, i)

            def low_down(j):
                for f in range(2):
                    dve.wait_ge(s_wdh, 2 * j + f + 1)
                    dve.tensor_tensor(wdl[:, f, :], wdt[:, f, :], f32(wdh[:, f, :]), ALU.subtract).then_inc(s_wdl, 1)

            def chunk(j, slot, first, more):
                hidden(j, 0, None if first else (j - 1, 3))
                low_down(j)
                if more:
                    prep_a(j + 1, 0)
                hidden(j, 1, (j, 0))
                if more:
                    prep_b(j + 1, 0, 1 - slot)
                    prep_a(j + 1, 1)
                hidden(j, 2, (j, 1))
                if more:
                    prep_b(j + 1, 1, 1 - slot)
                hidden(j, 3, (j, 2))
                if more:
                    prep_w(j + 1, 1 - slot)

            def norm_stats(b):
                for i in range(4 * b, 4 * b + 4):
                    last = dve.bn_stats(stats[:, i, :], xres[:, i, :])
                chain(last)
                for i in range(4 * b, 4 * b + 4):
                    last = dve.bn_aggr(mv[:, i, :], stats[:, i, :])
                chain(last)
                dve.tensor_scalar(vare[:, 4 * b:4 * b + 4], mv[:, 4 * b:4 * b + 4, 1], EPS, None, ALU.add).then_inc(s_var, 1)

            def norm(out_ap, t, scale):
                return dve.tensor_scalar(out_ap, xres[:, t, :], mv[:, t, 0:1], scale, ALU.subtract, ALU.mult)

            def c_norm(b):
                dve.wait_ge(s_rstd, 9 + (0, 1, 3, 5)[b])
                wait(dve, s_ck, 4 * b)
                for i in range(4):
                    norm(xnc[:, i, :], 4 * b + i, rstd[:, 4 * b + i:4 * b + i + 1]).then_inc(s_cxn, 1)

            def front(n):
                decay = tab[:, T_DEC + n % DC:T_DEC + n % DC + 1]
                dve.wait_ge(s_ck, n + 1)
                chain(dve.tensor_tensor_scan(co[:, 1:513], decay.broadcast_to([P, 512]), bank[c_keys_bank(n)][:, :], LOWEST, ALU.add, ALU.max))
                wait(dve, s_cl, 3 * n)
                dve.scalar_tensor_tensor(out=cd[:, :], in0=bank[c_keys_bank(n)][:, :], scalar=decay, in1=co[:, 0:512],
                                         op0=ALU.subtract, op1=ALU.subtract).then_inc(s_cf, 1)

            def back(n):
                e = ce[n % 2]
                dve.wait_ge(s_ce, 3 * n + 3)
                dve.wait_ge(s_cv, n + 1)
                chain(dve.tensor_tensor(cev[:, :], bank[c_values_bank(n)][:, :], e[:, 1, :], ALU.mult))
                wait(dve, s_cna, n)
                dve.tensor_tensor_scan(cp[:, 1:513], e[:, 0, :], cev[:, :], 0.0, ALU.mult, ALU.add)
                chain(dve.tensor_tensor_scan(cq[:, 1:513], e[:, 0, :], e[:, 1, :], 0.0, ALU.mult, ALU.add))
                wait(dve, s_cy, n)
                dve.tensor_tensor(cnum[:, :], bank[c_values_bank(n)][:, :], e[:, 2, :], ALU.mult).then_inc(s_cn, 1)
                chain(dve.tensor_tensor(e[:, 2, :], e[:, 2, :], cq[:, 0:512], ALU.add))
                dve.reciprocal(e[:, 2, :], e[:, 2, :]).then_inc(s_cd, 1)

            dve.wait_ge(s_tabc, 4)
            prep_a(0, 0)
            prep_b(0, 0, 0)
            residual(0)
            prep_a(0, 1)
            prep_b(0, 1, 0)
            normal(0)
            residual(1)
            turn(0)
            prep_w(0, 0)
            normal(1)
            hidden(0, 0, None)
            low_down(0)
            turn(1)
            residual(2)
            normal(2)
            hidden(0, 1, (0, 0))
            turn(2)
            prep_a(1, 0)
            residual(3)
            normal(3)
            hidden(0, 2, (0, 1))
            turn(3)
            prep_b(1, 0, 1)
            prep_a(1, 1)
            hidden(0, 3, (0, 2))
            prep_b(1, 1, 1)
            prep_w(1, 1)
            with dve.Fori(1, NJ - 2, 2) as j:
                chunk(j, 1, False, True)
                chunk(j + 1, 0, False, True)
            j = NJ - 1
            hidden(j, 0, (j - 1, 3))
            low_down(j)
            hidden(j, 1, (j, 0))
            dve.memset(co[:, 0:1], LOWEST)
            dve.memset(cp[:, 0:1], 0.0)
            dve.memset(cq[:, 0:1], 0.0)
            chain(dve.tensor_tensor(wub[:, :], tab[:, T_DEC:T_BON], tab[:, T_BON:T_ROWS], ALU.add))
            chain(dve.tensor_scalar(wlim[:, :], wub[:, :], -1.0, BIG, ALU.mult, ALU.add))
            norm_stats(0)
            c_norm(0)
            hidden(j, 2, (j, 1))
            front(0)
            norm_stats(1)
            hidden(j, 3, (j, 2))
            front(1)
            for i in range(4):
                add_down(j, 3, i)
            back(0)

            def add_out(n):
                b, c = divmod(n, DC)
                dve.wait_ge(s_cr, n + 1)
                x_part = xres[:, 4 * b:4 * b + 4, c * P:(c + 1) * P]
                dve.scalar_tensor_tensor(out=x_part, in0=bank[7][:, :].rearrange("p (i c) -> p i c", i=4), scalar=gates[:, 1:2],
                                         in1=x_part, op0=ALU.mult, op1=ALU.add).then_inc(s_co, 1)

            def d_xn(t, par):
                if t % 4 == 0:
                    dve.wait_ge(s_rstd, 9 + (2, 4, 6, 7)[t // 4])
                wait(dve, s_dxT, t - 1)
                norm(xsd[par][:, :], t, rstd[:, t:t + 1]).then_inc(s_dxn, 1)

            def d_x(t, par):
                dve.wait_ge(s_dxh, t + 1)
                dve.tensor_tensor(dxl[x_buf(t, par)][:, :, :].rearrange("p k n -> p (k n)"), bank[0][:, :],
                                  f32(dxh[x_buf(t, par)][:, :, :]).rearrange("p k n -> p (k n)"), ALU.subtract).then_inc(s_dxl, 1)

            def d_mul(t, par, shared):
                dve.wait_ge(s_dsg, t + 1)
                wait(dve, s_dmT, t - 1)
                if shared and t < HELD:
                    dve.tensor_copy(lg[:, t, :], bank[2][:, HID:G_W]).then_inc(s_lg, 1)
                dve.tensor_tensor(dmid[par][:, :], bank[3][:, 0:HID], dsg[:, :], ALU.mult).then_inc(s_dmid, 1)

            def d_hid(t, par):
                dve.wait_ge(s_dhh, t + 1)
                dve.tensor_tensor(dhl[par][:, :, :].rearrange("p k n -> p (k n)"), bank[1][0:HP, :],
                                  f32(dhh[par][:, :, :]).rearrange("p k n -> p (k n)"), ALU.subtract).then_inc(s_dhl, 1)

            dve.wait_ge(s_acc, 16 * NJ)
            dve.memset(mask1[:, :, :], 0.0)
            for n in range(NU + 1):
                t = n - 5
                if t >= 0:
                    if t % 4 == 0:
                        d_xn(t, t % 2)
                    elif t % 4 != 3:
                        d_xn(t + 1, (t + 1) % 2)
                if 1 <= n and n + 1 < NU:
                    front(n + 1)
                if n % 4 == 2 and 2 < n < NU - 2:
                    norm_stats(n // 4 + 1)
                if t >= 0 and t % 4 == 0:
                    d_x(t, t % 2)
                    d_xn(t + 1, (t + 1) % 2)
                if 1 <= n <= NU:
                    add_out(n - 1)
                if 1 <= n < NU:
                    back(n)
                if n % 4 == 2 and n + 2 < NU:
                    c_norm(n // 4 + 1)
                if t >= 1:
                    d_hid(t - 1, (t - 1) % 2)
                if t >= 0 and t % 4 != 3:
                    d_x(t + 1, (t + 1) % 2)
                if n % 4 == 0 and n >= 4:
                    dve.wait_ge(s_co, n)
                    norm_stats(n // 4 - 1)
                if t >= 0:
                    d_mul(t, t % 2, True)
            d_xn(HELD, 0)
            d_x(HELD, 0)
            d_xn(HELD + 1, 1)
            d_hid(HELD - 1, 1)
            d_x(HELD + 1, 1)
            for t in (HELD + 2, HELD + 3):
                d_xn(t, t % 2)
                d_x(t, t % 2)

            def per_token(ap):
                return ap.unsqueeze(2).broadcast_to([P, TT, E1])

            dve.wait_ge(s_lp, TT - HELD)
            dve.tensor_copy(lg[:, HELD:TT, :].rearrange("p i e -> p (i e)"), bank[5][:, 0:(TT - HELD) * E1]).then_inc(s_lg, 1)
            dve.wait_ge(s_lg, HELD + 1)
            dve.wait_ge(s_b8, 16)
            chain(dve.tensor_reduce(red[:, :], lg[:, :, :], AX.X, ALU.max))
            dve.tensor_tensor(lg[:, :, :], lg[:, :, :], per_token(red[:, :]), ALU.subtract).then_inc(s_lg, 1)
            dve.wait_ge(s_ex8, 1)
            chain(dve.tensor_reduce(red[:, :], prob[:, :, :], AX.X, ALU.add))
            chain(dve.reciprocal(red[:, :], red[:, :]))
            chain(dve.tensor_tensor(prob[:, :, :], prob[:, :, :], per_token(red[:, :]), ALU.mult))
            chain(dve.tensor_tensor(pb[:, :, :], prob[:, :, :], bias8[:, :].unsqueeze(1).broadcast_to([P, TT, E1]), ALU.add))
            for t in range(TT):
                last = dve.max(best[:, t, :], pb[:, t, :])
            chain(last)
            for t in range(TT):
                last = dve.max_index(bix[:, t, :], best[:, t, :], pb[:, t, :])
            chain(last)
            chain(dve.tensor_copy(bixf[:, :, :], bix[:, :, :]))
            count = cst[:, C_IOTA:C_IOTA + E1].unsqueeze(1).broadcast_to([P, TT, E1])
            for k in range(2):
                last = dve.tensor_tensor(sel[k][:, :, :], per_token(bixf[:, :, k]), count, ALU.is_equal)
            chain(last)
            dve.tensor_tensor(mask1[:, 0:TT, :], sel[0][:, :, :], sel[1][:, :, :], ALU.add).then_inc(s_mask1, 1)
            d_mul(HELD, 0, True)
            for k in range(2):
                chain(dve.tensor_tensor(tmp8[:, :, :], sel[k][:, :, :], prob[:, :, :], ALU.mult))
                chain(dve.tensor_reduce(rsc[:, k, :], tmp8[:, :, :], AX.X, ALU.add))
                chain(dve.tensor_tensor(rsc[:, k, :], rsc[:, k, :], rstd[:, :], ALU.mult))
            dve.wait_ge(s_rank1, 1)
            chain(dve.tensor_copy(base1[:, :, :].rearrange("p i e -> p (i e)"), bank[5][:, 0:(TT + 1) * E1]))
            chain(dve.tensor_tensor(cmp1[:, :, :], base1[:, TT, :].unsqueeze(2).broadcast_to([P, E1, TT]),
                                    cst[:, C_THR:C_THR + TT].unsqueeze(1).broadcast_to([P, E1, TT]), ALU.is_gt))
            chain(dve.tensor_reduce(nt1[:, :], cmp1[:, :, :], AX.X, ALU.add))
            chain(dve.tensor_scalar(nt1[:, :], nt1[:, :], 1.0, None, ALU.max))
            chain(dve.tensor_tensor_scan(tend1[:, :], ones[:, 0:E1], nt1[:, :], 0.0, ALU.mult, ALU.add))
            chain(dve.tensor_tensor(tst1[:, :], tend1[:, :], nt1[:, :], ALU.subtract))
            chain(dve.tensor_scalar(tst1[:, :], tst1[:, :], float(P), None, ALU.mult))
            chain(dve.tensor_tensor(base1[:, 0:TT, :], base1[:, 0:TT, :], tst1[:, :].unsqueeze(1).broadcast_to([P, TT, E1]), ALU.add))
            for k in range(2):
                chain(dve.tensor_tensor(tmp8[:, :, :], base1[:, 0:TT, :], sel[k][:, :, :], ALU.mult))
                chain(dve.tensor_reduce(slf[:, k, :], tmp8[:, :, :], AX.X, ALU.add))
            chain(dve.tensor_copy(slw[:, :, :], slf[:, :, :]))
            chain(dve.tensor_scalar(slf[:, :, :], slf[:, :, :], float(TOK), None, ALU.add))
            chain(dve.tensor_copy(slr[:, :, :], slf[:, :, :]))
            chain(dve.tensor_copy(tend1_i[:, :], tend1[:, :]))
            chain(dve.tensor_tensor(tcmp1[:, :, :], cst[:, C_IOTA:C_IOTA + 48].unsqueeze(2).broadcast_to([P, 48, E1 - 1]),
                                    tend1[:, 0:E1 - 1].unsqueeze(1).broadcast_to([P, 48, E1 - 1]), ALU.is_ge))
            chain(dve.tensor_reduce(tex1[:, :], tcmp1[:, :, :], AX.X, ALU.add))
            dve.tensor_copy(tex1_i[:, :], tex1[:, :]).then_inc(s_slot1, 1)
            for q in range(4):
                d_hid(HELD + q, q % 2)
                if q < 3:
                    d_mul(HELD + q + 1, (q + 1) % 2, True)
                for t in range(4 * q, 4 * q + 4):
                    for k in range(2):
                        n = 2 * t + k
                        wait(dve, s_rsc[n % 4], 16 * (n // 4))
                        norm(row[:, n % 4, :], t, rsc[:, k, t:t + 1]).then_inc(s_row, 1)
            d_x(TT, 0)
            d_x(TT + 1, 1)
            d_mul(TT, 0, False)
            d_x(TT + 2, 0)
            d_mul(TT + 1, 1, False)
            d_hid(TT, 0)

            def pair(t):
                for i in range(2):
                    d_x(t + i + 1, 1 - i)
                    d_mul(t + i, i, False)
                    d_hid(t + i - 1, 1 - i)

            xres_flat = xres[:, :, :].rearrange("p t d -> p (t d)")
            dve.sem_inc(s_sha, 2)
            with dve.Fori(TT + 2, TT + 1 + 2 * TT, 2) as t:
                pair(t)
                here = xres_flat[:, bass.ds((t - TT - 2) * (D // 2), D)]
                dve.wait_ge(s_shl, (t - TT) * 8)
                dve.scalar_tensor_tensor(out=here, in0=row[:, 0, :], scalar=gates[:, 3:4], in1=here,
                                         op0=ALU.mult, op1=ALU.add).then_inc(s_sha, 2)
            for t in range(TT + 2 + 2 * TT, TT + NT1 - 2, 2):
                pair(t)
            T = TT + NT1 - 1
            d_mul(T, T % 2, False)
            d_hid(T - 1, (T - 1) % 2)
            d_hid(T, T % 2)
            dve.wait_ge(s_sha, 2 * TT + 2)
            for t in range(TT):
                for k in range(2):
                    dve.wait_ge(s_fin[t % 6][k], 16 * (t // 6 + 1))
                    last = dve.scalar_tensor_tensor(out=xres[:, t, :], in0=fin[:, 2 * (t % 6) + k, :], scalar=gates[:, 3:4],
                                                    in1=xres[:, t, :], op0=ALU.mult, op1=ALU.add)
                    if k < 1:
                        chain(last)
                last.then_inc(s_x4, 1)


def shape_constants():
    import numpy as np
    def had(n):
        h = np.ones((1, 1), np.float32)
        while h.shape[0] < n:
            h = np.block([[h, h], [h, -h]])
        return h
    c = np.zeros((P, C_W), np.float32)
    c[:, C_ID:C_ID + P] = np.eye(P)
    c[:, C_TRI:C_TRI + P] = np.triu(np.ones((P, P)), 1)
    c[:, C_ONES:C_ONES + P] = 1.0
    c[:, C_H:C_H + P] = had(P)
    c[:, C_H4:C_H4 + P] = np.kron(np.eye(32), had(4))
    c[:, C_H16:C_H16 + P] = np.kron(np.eye(8), had(16))
    c[:, C_THR:C_THR + 16] = P * np.arange(16)
    c[:, C_IOTA:C_IOTA + 48] = np.arange(48)
    c[:, C_HALF:C_HALF + 4] = -0.5
    return c


_INS = ['x', 'itok_BxS_13_99985', 'ctx_2048', 'g_xattn', 'g_ffn',
        'L0_ffn_SU_ug', 'L0_ffn_SU_dp', 'L0_ffn_Wscale_ug', 'L0_ffn_Wscale_dp', 'L0_ffn_W_up', 'L0_ffn_W_gate', 'L0_ffn_W_down',
        'L1_xattn_w', 'L1_xattn_u', 'L1_ffn_gate_w', 'L1_ffn_w1', 'L1_ffn_w2', 'L1_ffn_w3',
        'L1_ffn_sw1', 'L1_ffn_sw2', 'L1_ffn_sw3', 'L1_ffn_expert_bias']


def kernel(**inputs):
    import numpy as _np
    import concourse.bacc as _bacc
    from concourse import mybir as _mybir
    from concourse.bass_utils import run_bass_kernel_spmd as _run

    nc = _bacc.Bacc("TRN2", target_bir_lowering=False, num_devices=1)
    arrays, args = {}, []
    for name in _INS:
        a = _np.ascontiguousarray(inputs[name])
        arrays[f"in_{name}"] = a
        args.append(nc.dram_tensor(f"in_{name}", a.shape, _mybir.dt.from_np(a.dtype), kind="ExternalInput").ap())
    arrays["shape_constants"] = shape_constants()
    args.append(nc.dram_tensor("shape_constants", (P, C_W), F32, kind="ExternalInput").ap())
    args.append(nc.dram_tensor("out_0", (4, 512, D), F32, kind="ExternalOutput").ap())
    program(nc, *args)
    r = _run(nc, [arrays], core_ids=[0])
    return r.results[0]["out_0"]
```
